# Optimizing a Trainium2 kernel written in Bass

```python
import numpy as np
import jax
import jax.numpy as jnp

def _softmax(x, axis=-1):
    return jax.nn.softmax(x, axis=axis)

def _gelu(x):
    return jax.nn.gelu(x, approximate=True)

def _silu(x):
    return jax.nn.silu(x)

def _sigmoid(x):
    return jax.nn.sigmoid(x)

def _layernorm(x, axis=-1, eps=1e-05):
    m = jnp.mean(x, axis=axis, keepdims=True)
    v = jnp.var(x, axis=axis, keepdims=True)
    return (x - m) / jnp.sqrt(v + eps)

def _scatter_add(tgt, idx, src, axis=0):
    return tgt.at[idx].add(src)

def _segment_sum(src, seg, n):
    return jax.ops.segment_sum(src, seg, n)
kernel_name = 'mk_adj_resnorm_d4_adj_r2_6cb2a6'

def setup_inputs(seed: int=0):
    np.random.seed(seed)
    _w = jnp.asarray

    def _rec_inputs():
        import jax
        import jax.numpy as jnp
        _gk = jax.random.key(seed)
        x = -0.0002928 + 1 * jax.random.normal(jax.random.fold_in(_gk, 1), (8, 1024, 64), jnp.float32)
        _a = jax.random.bernoulli(jax.random.fold_in(_gk, 2), 0.0078125, (1024, 1024))
        _a = jnp.logical_or(_a, jnp.swapaxes(_a, -1, -2))
        _a = jnp.logical_or(_a, jnp.eye(1024, dtype=bool))
        _af = _a.astype(jnp.float32)
        _af = _af / jnp.maximum(_af.sum(-1, keepdims=True), 1.0)
        adj = _af
        return (x, adj)
    x, adj = _rec_inputs()

    def _L0_gnn_setup():
        import jax, jax.numpy as jnp
        import numpy as np
        key = jax.random.key(seed)
        ks = jax.random.split(key, 5)
        B, N, IN, OUT, K, D = (32, 1024, 64, 64, 3, 16)
        x = jax.random.normal(ks[0], (B, N, IN), dtype=jnp.float32)
        A = jax.random.uniform(ks[1], (N, N), dtype=jnp.float32)
        A = A / jnp.sum(A, axis=-1, keepdims=True)
        embedding = jax.random.normal(ks[2], (N, D), dtype=jnp.float32) * 0.3
        weight = jax.random.normal(ks[3], (D, K, IN, OUT), dtype=jnp.float32) * 0.1
        bias = jax.random.normal(ks[4], (D, OUT), dtype=jnp.float32) * 0.1
        return {'x': x, 'A': A, 'embedding': embedding, 'weight': weight, 'bias': bias}
    _L0_gnn_all = _L0_gnn_setup()
    _L0_gnn_in = {k: v for k, v in _L0_gnn_all.items() if k in ('embedding', 'weight', 'bias')}
    del _L0_gnn_all

    def _L1_gnn_setup():
        import jax, jax.numpy as jnp
        import numpy as np
        NEG_INF = -1e+16

        def gat_layer(x, graph, W, b):
            h = x @ W
            s = jnp.einsum('bnd,bmd->bnm', h, h) * graph
            s = jnp.where(s == 0.0, NEG_INF, s)
            a = jax.nn.softmax(s, axis=2)
            return jnp.einsum('bnm,bmd->bnd', a, h) + b
        key = jax.random.key(seed)
        k1, k2, k3, k4, k5, k6 = jax.random.split(key, 6)
        B, N, C_IN, HID, HEADS, C_OUT = (16, 512, 64, 128, 8, 64)
        flow_x = jax.random.normal(k1, (B, N, C_IN), dtype=jnp.float32)
        graph = jax.random.randint(k2, (N, N), 0, 2).astype(jnp.float32)
        Wh = jax.random.normal(k3, (HEADS, C_IN, HID), dtype=jnp.float32)
        bh = jax.random.normal(k4, (HEADS, HID), dtype=jnp.float32)
        W_out = jax.random.normal(k5, (HID * HEADS, C_OUT), dtype=jnp.float32)
        b_out = jax.random.normal(k6, (C_OUT,), dtype=jnp.float32)
        return {'flow_x': flow_x, 'graph': graph, 'Wh': Wh, 'bh': bh, 'W_out': W_out, 'b_out': b_out}
    _L1_gnn_all = _L1_gnn_setup()
    _L1_gnn_in = {k: v for k, v in _L1_gnn_all.items() if k in ('Wh', 'bh', 'W_out', 'b_out')}
    del _L1_gnn_all

    def _L2_gnn_setup():
        import jax, jax.numpy as jnp
        import numpy as np
        NEG = -1000000000.0
        key = jax.random.key(seed)
        ks = jax.random.split(key, 14)
        B, N, E, NF, NH = (8, 1024, 64, 64, 64)
        x = jax.random.normal(ks[0], (B, N, NF), dtype=jnp.float32)
        base = jax.nn.one_hot(jax.random.randint(ks[1], (N,), 0, E), E, dtype=jnp.float32)
        extra = (jax.random.uniform(ks[2], (N, E)) < 0.03).astype(jnp.float32)
        H = jnp.clip(base + extra, 0.0, 1.0)
        adj = (jax.random.uniform(ks[3], (N, N)) < 0.01).astype(jnp.float32)
        adj = jnp.clip(adj + jnp.eye(N, dtype=jnp.float32), 0.0, 1.0)
        s_in = 1.0 / np.sqrt(NF)
        s_h = 1.0 / np.sqrt(NH)
        W = jax.random.normal(ks[4], (NF, NH), dtype=jnp.float32) * s_in
        W_ind = jax.random.normal(ks[5], (NF, NH), dtype=jnp.float32) * s_in
        a_node = jax.random.normal(ks[6], (NH,), dtype=jnp.float32) * s_h
        a_gn = jax.random.normal(ks[7], (NH,), dtype=jnp.float32) * s_h
        a_ge = jax.random.normal(ks[8], (NH,), dtype=jnp.float32) * s_h
        fcW = jax.random.normal(ks[9], (NH, 2 * NH), dtype=jnp.float32) * s_h
        fcb = jnp.zeros((2 * NH,), dtype=jnp.float32)
        av = jax.random.normal(ks[10], (2 * NH,), dtype=jnp.float32) / np.sqrt(2 * NH)
        return {'x': x, 'H': H, 'adj': adj, 'nhid': NH, 'W': W, 'W_ind': W_ind, 'a_node': a_node, 'a_gn': a_gn, 'a_ge': a_ge, 'fcW': fcW, 'fcb': fcb, 'av': av}
    _L2_gnn_all = _L2_gnn_setup()
    _L2_gnn_in = {k: v for k, v in _L2_gnn_all.items() if k in ('H', 'W', 'W_ind', 'a_node', 'a_gn', 'a_ge', 'fcW', 'fcb', 'av')}
    del _L2_gnn_all

    def _L3_gnn_setup():
        import jax, jax.numpy as jnp
        import numpy as np
        B, N, F_DIM, OUT_DIM = (1, 8192, 64, 64)
        INV_SQRT2 = 1.0 / np.sqrt(2.0)
        key = jax.random.key(seed)
        k = jax.random.split(key, 6)
        x = jax.random.normal(k[0], (B, N, F_DIM), dtype=jnp.float32)
        adj = jax.random.uniform(k[1], (N, N), dtype=jnp.float32) * (1.0 / N)
        w_nl = jax.random.normal(k[2], (F_DIM, 2), dtype=jnp.float32) * 0.5
        b_nl = jax.random.normal(k[3], (F_DIM,), dtype=jnp.float32) * 0.1
        w_out = jax.random.normal(k[4], (OUT_DIM, F_DIM), dtype=jnp.float32) * (1.0 / np.sqrt(F_DIM))
        b_out = jax.random.normal(k[5], (OUT_DIM,), dtype=jnp.float32) * 0.1
        return {'x': x, 'adj': adj, 'w_nl': w_nl, 'b_nl': b_nl, 'w_out': w_out, 'b_out': b_out}
    _L3_gnn_all = _L3_gnn_setup()
    _L3_gnn_in = {k: v for k, v in _L3_gnn_all.items() if k in ('w_nl', 'b_nl', 'w_out', 'b_out')}
    del _L3_gnn_all
    return {'x': x, 'adj': adj, 'L0_gnn_embedding': _L0_gnn_in['embedding'], 'L0_gnn_weight': _L0_gnn_in['weight'], 'L0_gnn_bias': _L0_gnn_in['bias'], 'L1_gnn_Wh': _L1_gnn_in['Wh'], 'L1_gnn_bh': _L1_gnn_in['bh'], 'L1_gnn_W_out': _L1_gnn_in['W_out'], 'L1_gnn_b_out': _L1_gnn_in['b_out'], 'L2_gnn_H': _L2_gnn_in['H'], 'L2_gnn_W': _L2_gnn_in['W'], 'L2_gnn_W_ind': _L2_gnn_in['W_ind'], 'L2_gnn_a_node': _L2_gnn_in['a_node'], 'L2_gnn_a_gn': _L2_gnn_in['a_gn'], 'L2_gnn_a_ge': _L2_gnn_in['a_ge'], 'L2_gnn_fcW': _L2_gnn_in['fcW'], 'L2_gnn_fcb': _L2_gnn_in['fcb'], 'L2_gnn_av': _L2_gnn_in['av'], 'L3_gnn_w_nl': _L3_gnn_in['w_nl'], 'L3_gnn_b_nl': _L3_gnn_in['b_nl'], 'L3_gnn_w_out': _L3_gnn_in['w_out'], 'L3_gnn_b_out': _L3_gnn_in['b_out']}

def reference(x, adj, L0_gnn_embedding, L0_gnn_weight, L0_gnn_bias, L1_gnn_Wh, L1_gnn_bh, L1_gnn_W_out, L1_gnn_b_out, L2_gnn_H, L2_gnn_W, L2_gnn_W_ind, L2_gnn_a_node, L2_gnn_a_gn, L2_gnn_a_ge, L2_gnn_fcW, L2_gnn_fcb, L2_gnn_av, L3_gnn_w_nl, L3_gnn_b_nl, L3_gnn_w_out, L3_gnn_b_out):
    import jax
    import jax.numpy as jnp

    def _L0_gnn_ref(x, A, embedding, weight, bias):
        import jax, jax.numpy as jnp
        import numpy as np
        K = weight.shape[1]
        N = A.shape[-2]
        w = jnp.einsum('nd,dkio->nkio', embedding, weight)
        b = jnp.einsum('nd,do->no', embedding, bias)
        As = [jnp.eye(N, dtype=x.dtype)]
        if K > 1:
            As.append(A)
        for _ in range(2, K):
            As.append(2.0 * (A @ As[-1]) - As[-2])
        A_stack = jnp.stack(As, 0)
        x_g = jnp.einsum('knm,bmc->bnkc', A_stack, x)
        out = jnp.einsum('bnki,nkio->bno', x_g, w)
        return out + b

    def _L1_gnn_ref(flow_x, graph, Wh, bh, W_out, b_out):
        import jax, jax.numpy as jnp
        import numpy as np
        NEG_INF = -1e+16

        def gat_layer(x, graph, W, b):
            h = x @ W
            s = jnp.einsum('bnd,bmd->bnm', h, h) * graph
            s = jnp.where(s == 0.0, NEG_INF, s)
            a = jax.nn.softmax(s, axis=2)
            return jnp.einsum('bnm,bmd->bnd', a, h) + b
        heads = jax.vmap(lambda W, b: gat_layer(flow_x, graph, W, b))(Wh, bh)
        H, B, N, D = heads.shape
        cat = jnp.moveaxis(heads, 0, 2).reshape(B, N, H * D)
        x = jax.nn.leaky_relu(cat, negative_slope=0.01)
        out = gat_layer(x, graph, W_out, b_out)
        return jax.nn.leaky_relu(out, negative_slope=0.01)

    def _L2_gnn_ref(x, H, adj, nhid, W, W_ind, a_node, a_gn, a_ge, fcW, fcb, av):
        import jax, jax.numpy as jnp
        import numpy as np
        NEG = -1000000000.0
        h = x @ W
        maskEN = H.T
        s = jax.nn.leaky_relu(h @ a_node, 0.2)
        logits = jnp.where(maskEN[None, :, :] > 0, s[:, None, :], NEG)
        alpha = jax.nn.softmax(logits, axis=-1)
        agg = jnp.einsum('ben,bnf->bef', alpha, h)
        beta = jax.nn.sigmoid((h @ a_gn)[:, None, :] + (agg @ a_ge)[:, :, None])
        all_he = beta[..., None] * h[:, None, :, :] + (1.0 - beta[..., None]) * agg[:, :, None, :]
        deg = jnp.maximum(adj.sum(-1), 1.0)[:, None]
        industry = jnp.einsum('nm,bmf->bnf', adj / deg, x @ W_ind)
        all_he = jax.nn.elu(all_he)
        he = jax.nn.elu(agg)

        def attn_scores(f):
            return jnp.tanh(f @ fcW + fcb) @ av
        se = attn_scores(he)
        logits2 = jnp.where(H[None, :, :] > 0, se[:, None, :], NEG)
        coefs1 = jax.nn.softmax(logits2, axis=-1)
        g = jnp.einsum('bne,benf->bnf', coefs1, all_he)
        pair = jnp.stack([industry, g], axis=2)
        coefs2 = jax.nn.softmax(attn_scores(pair), axis=-1)
        out = jnp.einsum('bnk,bnkf->bnf', coefs2, pair)
        return out

    def _L3_gnn_ref(x, adj, w_nl, b_nl, w_out, b_out):
        import jax, jax.numpy as jnp
        import numpy as np
        B, N, F_DIM, OUT_DIM = (1, 8192, 64, 64)
        INV_SQRT2 = 1.0 / np.sqrt(2.0)
        agg = jnp.einsum('ij,bjf->bif', adj, x)
        c = jnp.asarray(INV_SQRT2, dtype=agg.dtype)
        wave = jnp.stack([agg * c, agg * c], axis=-1)
        agg_nl = jnp.einsum('bnfk,fk->bnf', wave, w_nl) + b_nl
        out = jnp.einsum('bnf,of->bno', agg_nl, w_out) + b_out
        return out
    x = _layernorm(x + _L0_gnn_ref(x, adj, L0_gnn_embedding, L0_gnn_weight, L0_gnn_bias), axis=-1)
    x = _layernorm(x + _L1_gnn_ref(x, adj, L1_gnn_Wh, L1_gnn_bh, L1_gnn_W_out, L1_gnn_b_out), axis=-1)
    x = _layernorm(x + _L2_gnn_ref(x, L2_gnn_H, adj, 64, L2_gnn_W, L2_gnn_W_ind, L2_gnn_a_node, L2_gnn_a_gn, L2_gnn_a_ge, L2_gnn_fcW, L2_gnn_fcb, L2_gnn_av), axis=-1)
    x = _layernorm(x + _L3_gnn_ref(x, adj, L3_gnn_w_nl, L3_gnn_b_nl, L3_gnn_w_out, L3_gnn_b_out), axis=-1)
    return x

_drawn_inputs = setup_inputs


def setup_inputs(seed=0):
    import zlib

    import numpy as np

    out = dict(_drawn_inputs(seed))
    spreads = {'L2_gnn_fcb': (0.0, 0.8)}
    factors = {'L1_gnn_b_out': 7.161, 'L2_gnn_H': 2.851, 'L2_gnn_a_ge': 4.049}
    for name, (base, spread) in spreads.items():
        noise = np.random.default_rng([zlib.crc32(name.encode()), seed]).standard_normal(out[name].shape)
        drawn = base * np.exp(spread * noise) if base else spread * noise
        out[name] = jnp.asarray(drawn.astype(out[name].dtype))
    for name, factor in factors.items():
        out[name] = (out[name] * factor).astype(out[name].dtype)
    return out
```

```python
from contextlib import ExitStack

import concourse.bass as bass
from concourse import mybir

ALU = mybir.AluOpType
ACT = mybir.ActivationFunctionType
AX = mybir.AxisListType
F32 = mybir.dt.float32
F32R = mybir.dt.float32r

P = 128
HALF = 512
EPS = 1e-5


class Pipeline:
    pass


def adjacency_stack_kernel(nc, x, adj, L0_embedding, L0_weight, L0_bias, L1_Wh, L1_bh, L1_W_out,
                           L1_b_out, L2_H, L2_W, L2_W_ind, L2_a_node, L2_a_gn, L2_a_ge, L2_fcW,
                           L2_fcb, L2_av, L3_w_nl, L3_b_nl, L3_w_out, L3_b_out, out):
    B, N, C = x.shape
    NT = N // P
    TOK = B * NT
    D = L0_embedding.shape[1]
    HEADS, _, HID = L1_Wh.shape
    E = L2_H.shape[1]
    assert N == 1024 and C == 64 and HID == P and E == 64 and B % 2 == 0

    keep = ExitStack()
    with keep:
        def sem(name):
            return keep.enter_context(nc.semaphore(name))

        def sb(name, shape, dtype=F32, scope=keep):
            return scope.enter_context(nc.sbuf_tensor(name, shape, dtype))

        def ps(name, shape, scope, dtype=F32):
            return scope.enter_context(nc.psum_tensor(name, shape, dtype))

        A = sb("A", [P, NT, N])
        J = B // 2
        X = sb("X", [P, J, NT, 2, C])
        Xrows = X[:].rearrange("p j t h c -> p (j t h) c")
        ident = sb("ident", [P, P])

        def row(b, t):
            return b // 2 * (2 * NT) + 2 * t + b % 2

        def transpose_adj(pe, AT, banks, at_banked, at_copied):
            for k in range(2 * NT):
                mt, half = k // 2, k % 2
                if k >= 2:
                    pe.wait_ge(at_copied, k - 1)
                for q in range(4):
                    last = nc.tensor.transpose(banks[k % 2][:, q * P:(q + 1) * P],
                                               A[:, half * 4 + q, mt * P:(mt + 1) * P], ident[:])
                last.then_inc(at_banked, 1)

        def copy_adj(engine, copy, AT, banks, at_banked, at_copied):
            for k in range(2 * NT):
                mt, half = k // 2, k % 2
                engine.wait_ge(at_banked, k + 1)
                copy(AT[:, mt, half * HALF:(half + 1) * HALF], banks[k % 2][:]).then_inc(at_copied, 1)

        def residual_norm(vec, act_sem, vec_sem, done, R, T, stats, base=0):
            Xf = Xrows
            mean, var, sd, rstd = (stats[:, k, :] for k in range(4))
            count = [base]

            def step(instruction):
                instruction.then_inc(done, 1)
                count[0] += 1
                vec.wait_ge(done, count[0])

            def wide(s):
                return s.unsqueeze(2).to_broadcast([P, TOK, C])

            step(nc.vector.tensor_tensor(R, R, Xf, ALU.add))
            step(nc.vector.tensor_reduce(mean, R, AX.X, ALU.add))
            step(nc.vector.tensor_scalar(mean, mean, 1.0 / C, None, ALU.mult))
            step(nc.vector.tensor_tensor(R, R, wide(mean), ALU.subtract))
            step(nc.vector.tensor_tensor(T, R, R, ALU.mult))
            step(nc.vector.tensor_reduce(var, T, AX.X, ALU.add))
            nc.vector.tensor_scalar(var, var, 1.0 / C, EPS, ALU.mult, ALU.add).then_inc(vec_sem, 1)
            vec.wait_ge(act_sem, 1)
            step(nc.vector.reciprocal(rstd, sd))
            step(nc.vector.tensor_tensor(Xf, R, wide(rstd), ALU.mult))
            return count[0]

        def norm_root(act, act_sem, vec_sem, stats):
            act.wait_ge(vec_sem, 1)
            nc.scalar.activation(stats[:, 2, :], stats[:, 1, :], ACT.Sqrt).then_inc(act_sem, 1)

        with ExitStack() as scope:
            AT = sb("AT0", [P, NT, N], F32, scope)
            XG = sb("XG", [P, TOK, 3 * C], F32, scope)
            tile_in = sb("tile_in", [P, 2, 4 * C], F32, scope)
            emb = sb("emb", [P, NT, D], F32, scope)
            embT = sb("embT", [D, N], F32, scope)
            biasw = sb("biasw", [D, C], F32, scope)
            Eb = sb("Eb", [P, NT, C], F32, scope)
            wa = sb("wa", [P, D * C], F32, scope)
            wb = sb("wb", [P, D * C], F32, scope)
            wa_hi = sb("wa_hi", [P, D * C], F32R, scope)
            wa_lo = sb("wa_lo", [P, D * C], F32R, scope)
            wb_hi = sb("wb_hi", [P, D * C], F32R, scope)
            wb_lo = sb("wb_lo", [C, D * C], F32R, scope)
            gT = sb("gT", [P, 2, 2 * P], F32R, scope)
            gTl = sb("gTl", [P, 2, P], F32R, scope)
            zE = sb("zE", [P, D * C], F32, scope)
            R = sb("R0", [P, TOK, C], F32, scope)
            stats = sb("stats0", [P, 4, TOK], F32, scope)
            banks = [ps(f"l0_bank{k}", [P, HALF], scope) for k in range(2)]
            zps = [ps(f"l0_z{k}", [P, D * C], scope) for k in range(2)]

            loaded_adj, loaded_x, loaded_w = sem("l0_loaded_adj"), sem("l0_loaded_x"), sem("l0_loaded_w")
            ident_made = sem("ident_made")
            at_banked, at_copied = sem("l0_at_banked"), sem("l0_at_copied")
            x_placed, split_w = sem("l0_x_placed"), sem("l0_split_w")
            t_summed, t_copied = sem("l0_t_summed"), sem("l0_t_copied")
            emb_banked, emb_copied = sem("l0_emb_banked"), sem("l0_emb_copied")
            staged = sem("l0_staged")
            g_banked, g_hi, g_lo = sem("l0_g_banked"), sem("l0_g_hi"), sem("l0_g_lo")
            z_summed, z_weighted, z_reduced = sem("l0_z_summed"), sem("l0_z_weighted"), sem("l0_z_reduced")
            norm_v, norm_a, norm_steps = sem("l0_norm_v"), sem("l0_norm_a"), sem("l0_norm_steps")

            block = scope.enter_context(nc.Block())

            @block.sync
            def _(sp):
                for q in range(4):
                    sp.dma_start(A[:, 2 * q:2 * q + 2, :],
                                 adj.rearrange("(t p) m -> p t m", p=P)[:, 2 * q:2 * q + 2, :]).then_inc(loaded_adj, 16)
                for b in range(B):
                    sp.dma_start(X[:, b // 2, :, b % 2, :], x[b].rearrange("(t p) c -> p t c", p=P)).then_inc(loaded_x, 16)

            @block.gpsimd
            def _(pool):
                nc.gpsimd.memset(ident[:], 0.0).then_inc(ident_made, 1)
                pool.wait_ge(ident_made, 1)
                nc.gpsimd.affine_select(out=ident[:], in_=ident[:], compare_op=ALU.not_equal, fill=1.0, base=0,
                                        pattern=[[-1, P]], channel_multiplier=1).then_inc(ident_made, 1)
                pool.wait_ge(t_copied, 2 * NT)
                with pool.Fori(0, TOK // 2) as i:
                    for u in range(2):
                        tile = bass.ds(2 * i + u, 1)
                        pool.wait_ge(g_banked, 2 * i + 1)
                        nc.gpsimd.tensor_copy(tile_in[:, u, 0:3 * C].unsqueeze(1), XG[:, tile, :])
                        nc.gpsimd.tensor_copy(tile_in[:, u, 3 * C:4 * C].unsqueeze(1),
                                              XG[:, tile, 2 * C:3 * C]).then_inc(staged, 1)

            @block.scalar
            def _(act):
                wk = L0_weight.rearrange("d k i o -> k i d o")
                for k in range(2):
                    act.dma_start(wa[k * C:(k + 1) * C, :].rearrange("p (d o) -> p d o", o=C), wk[k]).then_inc(loaded_w, 16)
                for k in range(2):
                    act.dma_start(wb[k * C:(k + 1) * C, :].rearrange("p (d o) -> p d o", o=C), wk[2]).then_inc(loaded_w, 16)
                act.dma_start(emb[:], L0_embedding.rearrange("(t p) d -> p t d", p=P)).then_inc(loaded_w, 16)
                act.dma_start(biasw[:], L0_bias).then_inc(loaded_w, 16)
                copy_adj(act, nc.scalar.copy, AT, banks, at_banked, at_copied)
                with act.Fori(0, TOK // 2) as i:
                    for u in range(2):
                        act.wait_ge(g_banked, 2 * i + u + 2)
                        act.wait_ge(z_summed, 2 * i + u + 1)
                        nc.scalar.copy(gT[:, u, :], banks[u][:, 0:2 * P]).then_inc(g_hi, 1)
                norm_root(act, norm_a, norm_v, stats)

            @block.vector
            def _(vec):
                vec.wait_ge(loaded_x, 16 * B)
                nc.vector.tensor_copy(XG[:, :, 0:C], Xrows).then_inc(x_placed, 1)
                vec.wait_ge(loaded_w, 16 * 6)
                nc.vector.tensor_copy(wa_hi[:], wa[:]).then_inc(split_w, 1)
                nc.vector.tensor_copy(wb_hi[:], wb[:]).then_inc(split_w, 1)
                vec.wait_ge(split_w, 2)
                nc.vector.tensor_tensor(wa_lo[:], wa[:], wa_hi[:], ALU.subtract).then_inc(split_w, 1)
                nc.vector.tensor_tensor(wb_lo[:], wb[0:C, :], wb_hi[0:C, :], ALU.subtract).then_inc(split_w, 1)
                XGj = XG[:].rearrange("p (j t h) c -> p j t h c", j=J, h=2)
                for t in range(NT):
                    vec.wait_ge(t_summed, t + 1)
                    nc.vector.tensor_copy(XGj[:, :, t, :, C:2 * C],
                                          banks[t % 2][:].rearrange("p (j h c) -> p j h c", h=2, c=C)).then_inc(t_copied, 1)
                for t in range(NT):
                    vec.wait_ge(t_summed, NT + t + 1)
                    for h in range(2):
                        last = nc.vector.scalar_tensor_tensor(
                            out=XGj[:, :, t, h, 2 * C:3 * C],
                            in0=banks[t % 2][:].rearrange("p (j h c) -> p j h c", h=2, c=C)[:, :, h, :],
                            scalar=2.0, in1=XGj[:, :, t, h, 0:C], op0=ALU.mult, op1=ALU.subtract)
                    last.then_inc(t_copied, 1)
                vec.wait_ge(emb_banked, 1)
                nc.vector.tensor_copy(embT[:], zps[0][0:D, :]).then_inc(emb_copied, 1)
                vec.wait_ge(emb_banked, 2)
                nc.vector.tensor_copy(Eb[:].rearrange("p t c -> p (t c)"), zps[1][:, 0:HALF]).then_inc(emb_copied, 1)
                nc.vector.memset(stats[:, 0, :], 0.0).then_inc(g_lo, 1)
                nc.vector.memset(stats[:, 1, :], 0.0).then_inc(z_weighted, 1)
                with vec.Fori(0, TOK // 2) as i:
                    for u in range(2):
                        vec.wait_ge(g_hi, 2 * i + u + 1)
                        nc.vector.tensor_tensor(gTl[:, u, :], banks[u][:, 0:P], gT[:, u, 0:P], ALU.subtract)
                        nc.vector.tensor_tensor(gT[C:P, u, P:2 * P], banks[u][C:P, P:2 * P],
                                                gT[C:P, u, P:2 * P], ALU.subtract).then_inc(g_lo, 1)
                        vec.wait_ge(z_summed, 2 * i + u + 3)
                        tile = 2 * i + u
                        coef = emb[:, bass.ds(tile // 2 % NT, 1), :].rearrange("p a d -> p (a d)")
                        nc.vector.tensor_tensor(zE[:].rearrange("p (d o) -> p d o", o=C),
                                                zps[u][:].rearrange("p (d o) -> p d o", o=C),
                                                coef.unsqueeze(2).to_broadcast([P, D, C]),
                                                ALU.mult).then_inc(z_weighted, 1)
                        vec.wait_ge(z_weighted, 2 * i + u + 2)
                        nc.vector.tensor_reduce(R[:, bass.ds(tile, 1), :].rearrange("p a c -> p (a c)"),
                                                zE[:].rearrange("p (d o) -> p o d", o=C), AX.X, ALU.add).then_inc(z_reduced, 1)
                vec.wait_ge(z_reduced, TOK)
                Rj = R[:].rearrange("p (j t h) c -> p j t h c", j=J, h=2)
                for j in range(J):
                    last = nc.vector.tensor_tensor(Rj[:, j], Rj[:, j], Eb[:].unsqueeze(2).to_broadcast([P, NT, 2, C]), ALU.add)
                last.then_inc(norm_steps, 1)
                vec.wait_ge(norm_steps, 1)
                residual_norm(vec, norm_a, norm_v, norm_steps, R[:], XG[:, :, 0:C], stats, 1)

            @block.tensor
            def _(pe):
                pe.wait_ge(ident_made, 2)
                pe.wait_ge(loaded_adj, 16 * 4)
                transpose_adj(pe, AT, banks, at_banked, at_copied)
                XGj = XG[:].rearrange("p (j t h) c -> p j t h c", j=J, h=2)
                pe.wait_ge(x_placed, 1)
                pe.wait_ge(at_copied, 2 * NT)
                for k in range(2):
                    if k == 1:
                        pe.wait_ge(t_copied, NT)
                    for t in range(NT):
                        if k * NT + t >= 2:
                            pe.wait_ge(t_copied, k * NT + t - 1)
                        for mt in range(NT):
                            last = nc.tensor.matmul(banks[t % 2][:].rearrange("p (j h c) -> p j h c", h=2, c=C),
                                                    AT[:, mt, t * P:(t + 1) * P],
                                                    XGj[:, :, mt, :, k * C:(k + 1) * C],
                                                    start=(mt == 0), stop=(mt == NT - 1))
                        last.then_inc(t_summed, 1)
                for t in range(NT):
                    last = nc.tensor.transpose(zps[0][0:D, t * P:(t + 1) * P], emb[:, t, :], ident[:])
                last.then_inc(emb_banked, 1)
                pe.wait_ge(emb_copied, 1)
                for t in range(NT):
                    last = nc.tensor.matmul(zps[1][:, t * C:(t + 1) * C], embT[:, t * P:(t + 1) * P], biasw[:],
                                            start=True, stop=True)
                last.then_inc(emb_banked, 1)
                pe.wait_ge(emb_copied, 2)
                pe.wait_ge(t_copied, 2 * NT)
                pe.wait_ge(split_w, 4)

                nc.tensor.transpose(zps[0][0:D, 0:P], emb[:, 0, :], ident[:]).then_inc(z_summed, 2)
                nc.tensor.transpose(banks[0][0:D, 0:P], emb[:, 0, :], ident[:]).then_inc(g_banked, 1)
                with pe.Fori(0, TOK // 2) as i:
                    for u in range(2):
                        tile = 2 * i + u
                        pe.wait_ge(staged, tile + 1)
                        pe.wait_ge(g_lo, 2 * i + 1)
                        for q in range(2):
                            last = nc.tensor.transpose(banks[u][:, q * P:(q + 1) * P],
                                                       tile_in[:, u, q * P:(q + 1) * P], ident[:])
                        last.then_inc(g_banked, 1)
                        pe.wait_ge(g_lo, 2 * i + u + 2)
                        pe.wait_ge(z_weighted, 2 * i + 1)
                        for half in range(2):
                            cols = slice(half * HALF, (half + 1) * HALF)
                            terms = ((gT[:, u, 0:P], wa_hi[:, cols]), (gT[:, u, 0:P], wa_lo[:, cols]),
                                     (gTl[:, u, :], wa_hi[:, cols]), (gT[:, u, P:2 * P], wb_hi[:, cols]),
                                     (gT[0:C, u, P:2 * P], wb_lo[:, cols]))
                            for k, (stay, move) in enumerate(terms):
                                last = nc.tensor.matmul(zps[u][:, cols], stay, move, start=(k == 0),
                                                        stop=(k == len(terms) - 1))
                        last.then_inc(z_summed, 1)

        MASKED = -1.0e16
        OFF = 8
        ZCUT = N // 2
        STEPS = 2 * NT

        def attention(scope, tag):
            s = {}
            for name in ("scored", "weighted", "zeroed", "zeroed_v", "shifted", "exped", "turned", "copied", "mixed",
                         "normed", "filled"):
                s[name] = sem(f"{tag}_{name}")
            work = sb(f"{tag}_work", [P, 4, N], F32, scope)
            masks = sb(f"{tag}_masks", [P, 2, N], F32, scope)
            weighted_start = sb(f"{tag}_weighted_start", [P, 1], F32, scope)
            filled = sb(f"{tag}_filled", [P, 1], F32, scope)
            copied_start = sb(f"{tag}_copied_start", [P, 1], F32, scope)
            probsT = sb(f"{tag}_probsT", [P, 2, NT, P], F32, scope)
            nmax = sb(f"{tag}_nmax", [P, 4], F32, scope)
            rowsum = sb(f"{tag}_rowsum", [P, 4], F32, scope)
            rinv = sb(f"{tag}_rinv", [P, 4], F32, scope)
            outs = sb(f"{tag}_outs", [P, 2, NT, C], F32, scope)
            Y2 = sb(f"{tag}_Y2", [P, 2, N], F32R, scope)
            Yl = sb(f"{tag}_Yl", [C, 2, N], F32R, scope)
            SX = sb(f"{tag}_SX", [P, B, N], F32R, scope)
            score_ps = [ps(f"{tag}_score_ps{k}", [P, N], scope) for k in range(2)]
            turn_ps = [ps(f"{tag}_turn_ps{k}", [P, HALF], scope) for k in range(2)]
            mix_ps = ps(f"{tag}_mix_ps", [P, HALF], scope)
            misc_ps = ps(f"{tag}_misc_ps", [P, HALF], scope)
            inv = sem(f"{tag}_inv")

            def init_pool(pool):
                nc.gpsimd.memset(weighted_start[:], 0.0).then_inc(s["weighted"], OFF)
                nc.gpsimd.memset(work[:], 0.0).then_inc(s["scored"], OFF)
                nc.gpsimd.memset(masks[:], 0.0).then_inc(s["zeroed"], OFF)
                nc.gpsimd.memset(nmax[:], 0.0).then_inc(s["shifted"], OFF - 1)
                nc.gpsimd.memset(rowsum[:], 1.0).then_inc(s["exped"], OFF - 2)
                nc.gpsimd.memset(probsT[:], 0.0).then_inc(s["turned"], 2 * (OFF - 3))
                nc.gpsimd.memset(copied_start[:], 0.0).then_inc(s["copied"], 2 * (OFF - 3))
                nc.gpsimd.memset(outs[:], 0.0).then_inc(s["mixed"], OFF - 4)
                nc.gpsimd.memset(filled[:], 0.0).then_inc(s["filled"], 1)

            def init_vec(vec):
                nc.vector.memset(mix_ps[:], 0.0).then_inc(s["normed"], OFF - 5)
                nc.vector.memset(rinv[:], 0.0).then_inc(s["zeroed_v"], OFF)

            def pe_scores(pe, g, t, u, x_cols):
                pe.wait_ge(s["weighted"], OFF + g - 1)
                rows = slice(t % NT * P, (t % NT + 1) * P)
                for half in range(2):
                    o = score_ps[t % 2][:, half * HALF:(half + 1) * HALF].unsqueeze(1)
                    nc.tensor.matmul(o, Y2[:, u, rows], SX[:, x_cols, half * HALF:(half + 1) * HALF], start=True, stop=False)
                    last = nc.tensor.matmul(o, Yl[:, u, rows], SX[0:C, x_cols, half * HALF:(half + 1) * HALF],
                                            start=False, stop=True)
                last.then_inc(s["scored"], 1)

            def pe_turn(pe, g, t):
                pe.wait_ge(s["exped"], OFF + g + 1)
                for half in range(2):
                    pe.wait_ge(s["copied"], 2 * (OFF + g) + half - 1)
                    for q in range(4):
                        k = half * 4 + q
                        last = nc.tensor.transpose(turn_ps[half][:, q * P:(q + 1) * P],
                                                   work[:, t % 4, k * P:(k + 1) * P], ident[:])
                    last.then_inc(s["turned"], 1)

            def pe_mix(pe, g, t, value):
                pe.wait_ge(s["copied"], 2 * (OFF + g + 1))
                pe.wait_ge(s["normed"], OFF + g)
                for mt in range(NT):
                    last = nc.tensor.matmul(mix_ps[:, (t % NT) * C:(t % NT + 1) * C].unsqueeze(1), probsT[:, t % 2, mt, :],
                                            value(mt), start=(mt == 0), stop=(mt == NT - 1))
                last.then_inc(s["mixed"], 1)

            def vec_weigh(vec, g, t):
                vec.wait_ge(s["scored"], OFF + g + 1)
                vec.wait_ge(s["turned"], 2 * (OFF + g - 3))
                nc.vector.tensor_tensor(work[:, t % 4, :], score_ps[t % 2][:], A[:, t % NT, :],
                                        ALU.mult).then_inc(s["weighted"], 1)

            def pool_zero(pool, g, t):
                pool.wait_ge(s["weighted"], OFF + g + 1)
                pool.wait_ge(s["shifted"], OFF + g - 1)
                pool.nop(nofuse=True)
                nc.gpsimd.tensor_scalar(masks[:, t % 2, ZCUT:N], work[:, t % 4, ZCUT:N], 0.0, MASKED,
                                        ALU.is_equal, ALU.mult).then_inc(s["zeroed"], 1)

            def vec_zero(vec, g, t):
                vec.wait_ge(s["weighted"], OFF + g + 1)
                nc.vector.tensor_scalar(masks[:, t % 2, 0:ZCUT], work[:, t % 4, 0:ZCUT], 0.0, MASKED,
                                        ALU.is_equal, ALU.mult).then_inc(s["zeroed_v"], 1)

            def vec_shift(vec, g, t):
                vec.wait_ge(s["zeroed"], OFF + g + 1)
                vec.wait_ge(s["zeroed_v"], OFF + g + 1)
                vec.wait_ge(s["exped"], OFF + g - 3)
                vec.nop(nofuse=True)
                nc.vector.tensor_tensor_reduce(work[:, t % 4, :], masks[:, t % 2, :], work[:, t % 4, :], -1.0, 3.0e38,
                                               ALU.add, ALU.min, nmax[:, t % 4:t % 4 + 1]).then_inc(s["shifted"], 1)

            def act_exp(act, g, t):
                act.wait_ge(s["shifted"], OFF + g + 1)
                act.wait_ge(s["normed"], OFF + g - 3)
                nc.scalar.activation(work[:, t % 4, :], work[:, t % 4, :], ACT.Exp, bias=nmax[:, t % 4:t % 4 + 1],
                                     scale=-1.0, accum_out=rowsum[:, t % 4:t % 4 + 1]).then_inc(s["exped"], 1)

            def act_copy(act, g, t):
                act.wait_ge(s["mixed"], OFF + g - 1)
                for half in range(2):
                    act.wait_ge(s["turned"], 2 * (OFF + g) + half + 1)
                    nc.scalar.copy(probsT[:, t % 2, half * 4:half * 4 + 4, :].rearrange("p a b -> p (a b)"),
                                   turn_ps[half][:]).then_inc(s["copied"], 1)

            def vec_norm(vec, g, t, out):
                vec.wait_ge(s["mixed"], OFF + g + 1)
                nc.vector.reciprocal(rinv[:, t % 4:t % 4 + 1], rowsum[:, t % 4:t % 4 + 1]).then_inc(inv, 1)
                vec.wait_ge(inv, 6 + g)
                nc.vector.tensor_scalar(out, mix_ps[:, (t % NT) * C:(t % NT + 1) * C].unsqueeze(1),
                                        rinv[:, t % 4:t % 4 + 1], None, ALU.mult).then_inc(s["normed"], 1)

            at = Pipeline()
            at.s, at.probsT, at.outs, at.Y2, at.Yl, at.SX = (
                s, probsT, outs, Y2, Yl, SX)
            at.turn_ps, at.mix_ps, at.misc_ps, at.score_ps, at.init_pool, at.init_vec = (
                turn_ps, mix_ps, misc_ps, score_ps, init_pool, init_vec)
            at.pe_scores, at.pe_turn, at.pe_mix, at.vec_weigh, at.pool_zero, at.vec_zero = (
                pe_scores, pe_turn, pe_mix, vec_weigh, pool_zero, vec_zero)
            at.vec_shift, at.act_exp, at.act_copy, at.vec_norm = (
                vec_shift, act_exp, act_copy, vec_norm)
            return at

        acc_scope = keep.enter_context(ExitStack())
        h2T = sb("h2T", [C, B + 1, N], F32, acc_scope)
        PAIRS = B * HEADS

        with ExitStack() as scope:
            at = attention(scope, "hid")
            s, Y2, Yl, SX, outs, misc_ps = at.s, at.Y2, at.Yl, at.SX, at.outs, at.misc_ps
            wh = sb("wh", [C, HEADS, HID], F32, scope)
            wo = sb("wo", [P, HEADS, C], F32, scope)
            bh = sb("bh", [P, HEADS], F32, scope)
            whT = sb("whT", [P, 2, 2, C], F32, scope)
            Mh = sb("Mh", [P, HEADS, 2, C], F32R, scope)
            Ml = sb("Ml", [C, HEADS, 2, C], F32R, scope)
            Mh_now = sb("Mh_now", [P, 2, 2 * C], F32R, scope)
            Ml_now = sb("Ml_now", [C, 2, 2 * C], F32R, scope)
            wh_now = sb("wh_now", [C, 2, HID], F32, scope)
            wo_now = sb("wo_now", [P, 2, C], F32, scope)
            onT = sb("onT", [C, HALF], F32, scope)
            biased = sb("biased", [P, HALF], F32, scope)
            leaky = sb("leaky", [P, HALF], F32, scope)
            loaded = sem("hid_loaded")
            w_turned, w_copied, m_made, m_split = (sem(f"hid_{n}") for n in ("w_turned", "w_copied", "m_made", "m_split"))
            sx_banked, sx_hi, sx_lo = sem("hid_sx_banked"), sem("hid_sx_hi"), sem("hid_sx_lo")
            misc_made, misc_read = sem("hid_misc_made"), sem("hid_misc_read")
            y_hi, biased_made, leaky_made = sem("hid_y_hi"), sem("hid_biased"), sem("hid_leaky")
            staged, cleared = sem("hid_staged"), sem("hid_cleared")

            def pe_small(pe, p, n, k):
                u, t = k // NT, k % NT
                pe.wait_ge(misc_read, OFF + n)
                if t < 2:
                    if t == 0:
                        pe.wait_ge(staged, p + 1)
                    b, cols = bass.ds((p + 1) // HEADS % B, 1), slice(t * HALF, (t + 1) * HALF)
                    o = misc_ps[:].unsqueeze(1)
                    nc.tensor.matmul(o, Mh_now[:, 1 - u, :], SX[:, b, cols], start=True, stop=False)
                    last = nc.tensor.matmul(o, Ml_now[:, 1 - u, :], SX[0:C, b, cols], start=False, stop=True)
                elif t % 3 == 2:
                    half = (t - 2) // 3
                    pe.wait_ge(s["normed"], OFF + NT * (p - 1) + 4 * half + 4)
                    pe.nop(nofuse=True)
                    for q in range(4):
                        last = nc.tensor.transpose(misc_ps[0:C, q * P:(q + 1) * P], outs[:, 1 - u, half * 4 + q, :],
                                                   ident[:])
                elif t % 3 == 0:
                    last = nc.tensor.matmul(misc_ps[:], wh_now[:, 1 - u, :], onT[:], start=True, stop=True)
                else:
                    pe.wait_ge(leaky_made, 2 * p + (t - 2) // 3 + 1)
                    last = nc.tensor.matmul(misc_ps[0:C, :], wo_now[:, 1 - u, :], leaky[:], start=True, stop=True)
                last.then_inc(misc_made, 1)

            def act_small(act, p, n, k):
                u, t = k // NT, k % NT
                if t < 2:
                    act.wait_ge(misc_made, OFF + n + 1)
                    nc.scalar.copy(Y2[:, 1 - u, t * HALF:(t + 1) * HALF], misc_ps[:]).then_inc(y_hi, 1)
                elif t % 3 == 2:
                    act.wait_ge(misc_made, OFF + n + 1)
                    nc.scalar.copy(onT[:], misc_ps[0:C, :]).then_inc(misc_read, 1)
                elif t % 3 == 0:
                    act.wait_ge(misc_made, OFF + n + 1)
                    act.nop(nofuse=True)
                    nc.scalar.activation(biased[:], misc_ps[:], ACT.Identity,
                                         bias=bh[:, bass.ds((p + HEADS - 1) % HEADS, 1)]).then_inc(misc_read, 1)

            def vec_small(vec, p, n, k):
                u, t = k // NT, k % NT
                if t < 2:
                    cols = slice(t * HALF, (t + 1) * HALF)
                    vec.wait_ge(y_hi, 2 * p + t + 3)
                    nc.vector.tensor_tensor(Yl[:, 1 - u, cols], misc_ps[0:C, :], Y2[0:C, 1 - u, cols],
                                            ALU.subtract).then_inc(misc_read, 1)
                elif t % 3 == 0:
                    vec.wait_ge(misc_read, OFF + n + 1)
                    nc.vector.scalar_tensor_tensor(out=leaky[:], in0=biased[:], scalar=0.01, in1=biased[:],
                                                   op0=ALU.mult, op1=ALU.max).then_inc(leaky_made, 1)
                elif t % 3 == 1:
                    half = (t - 2) // 3
                    acc = h2T[:, bass.ds((p + HEADS - 1) // HEADS, 1), half * HALF:(half + 1) * HALF]
                    vec.wait_ge(misc_made, OFF + n + 1)
                    nc.vector.tensor_tensor(acc, acc, misc_ps[0:C, :].unsqueeze(1), ALU.add).then_inc(misc_read, 1)

            def pe_step(pe, p, k, new=True):
                t = k % NT
                g = NT * p + t
                if new:
                    at.pe_scores(pe, g, k, k // NT, bass.ds(p // HEADS, 1))
                if new or t < 3:
                    at.pe_turn(pe, g - 3, (k - 3) % STEPS)
                if new or t < 4:
                    b = p // HEADS % B if t >= 4 else (p + PAIRS - 1) % PAIRS // HEADS
                    at.pe_mix(pe, g - 4, (k - 4) % STEPS, lambda mt: Xrows[:, bass.ds(row(b, mt), 1), :])
                if new or t >= 2:
                    pe_small(pe, p, g if new else g - 2, k)

            def act_step(act, p, k, new=True):
                t = k % NT
                g = NT * p + t
                if new or t < 2:
                    at.act_exp(act, g - 2, (k - 2) % STEPS)
                if new or t < 3:
                    at.act_copy(act, g - 3, (k - 3) % STEPS)
                if new or t >= 2:
                    act_small(act, p, g if new else g - 2, k)

            def vec_step(vec, p, k, new=True):
                t = k % NT
                g = NT * p + t
                if new or t < 5:
                    at.vec_norm(vec, g - 5, (k - 5) % STEPS, outs[:, (k - 5) % STEPS // NT, (k - 5) % NT, :].unsqueeze(1))
                if new:
                    at.vec_weigh(vec, g, k)
                if new or t < 1:
                    at.vec_shift(vec, g - 1, (k - 1) % STEPS)
                if new:
                    at.vec_zero(vec, g, k)
                if new or t >= 2:
                    vec_small(vec, p, g if new else g - 2, k)

            def stage_weights(pool, head_m, head_w, u):
                nc.gpsimd.tensor_copy(Mh_now[:, u, :].unsqueeze(1), Mh[:, head_m, :, :].rearrange("p a r c -> p a (r c)"))
                nc.gpsimd.tensor_copy(Ml_now[:, u, :].unsqueeze(1), Ml[:, head_m, :, :].rearrange("p a r c -> p a (r c)"))
                nc.gpsimd.tensor_copy(wh_now[:, u, :].unsqueeze(1), wh[:, head_w, :])
                return nc.gpsimd.tensor_copy(wo_now[:, u, :].unsqueeze(1), wo[:, head_w, :])

            block = scope.enter_context(nc.Block())

            @block.sync
            def _(sp):
                sp.dma_start(wh[:], L1_Wh.rearrange("h c d -> c h d")).then_inc(loaded, 16)
                sp.dma_start(wo[:], L1_W_out.rearrange("(h d) c -> d h c", d=HID)).then_inc(loaded, 16)
                sp.dma_start(bh[:], L1_bh.rearrange("h d -> d h"), allow_slow_non_contiguous=True).then_inc(loaded, 16)

            @block.gpsimd
            def _(pool):
                at.init_pool(pool)
                nc.gpsimd.memset(h2T[:], 0.0).then_inc(cleared, 1)
                pool.wait_ge(m_split, HEADS)
                stage_weights(pool, bass.ds(0, 1), bass.ds(0, 1), 0)
                stage_weights(pool, bass.ds(1, 1), bass.ds(HEADS - 1, 1), 1).then_inc(staged, 1)
                with pool.Fori(0, PAIRS // 2) as i:
                    for k in range(STEPS):
                        p = 2 * i + k // NT
                        at.pool_zero(pool, STEPS * i + k, k)
                        if k % NT == 2:
                            pool.wait_ge(misc_made, OFF + NT * p)
                            stage_weights(pool, bass.ds((p + 2) % HEADS, 1), bass.ds(p % HEADS, 1),
                                          k // NT).then_inc(staged, 1)

            @block.scalar
            def _(act):
                for b in range(B):
                    act.wait_ge(sx_banked, b + 1)
                    nc.scalar.copy(SX[0:C, b, :], at.score_ps[b % 2][0:C, :]).then_inc(sx_hi, 1)
                for half in range(2):
                    act.wait_ge(misc_made, OFF - 2 + half + 1)
                    nc.scalar.copy(Y2[:, 0, half * HALF:(half + 1) * HALF], misc_ps[:]).then_inc(y_hi, 1)
                act.wait_ge(s["filled"], 1)
                with act.Fori(0, PAIRS // 2) as i:
                    for k in range(STEPS):
                        act_step(act, 2 * i + k // NT, k)
                for t in range(NT):
                    act_step(act, PAIRS, t, new=False)

            @block.vector
            def _(vec):
                at.init_vec(vec)
                for h in range(HEADS):
                    vec.wait_ge(w_turned, h + 1)
                    nc.vector.tensor_copy(whT[:, h % 2, :, :], at.turn_ps[0][:, 0:C].unsqueeze(1).to_broadcast([P, 2, C])).then_inc(w_copied, 1)
                    vec.wait_ge(m_made, h + 1)
                    m = at.turn_ps[1][:, 0:C].unsqueeze(1).to_broadcast([P, 2, C])
                    nc.vector.tensor_copy(Mh[:, h, :, :], m).then_inc(w_copied, 1)
                    vec.wait_ge(w_copied, 2 * h + 2)
                    nc.vector.tensor_tensor(Ml[:, h, :, :], m[0:C], Mh[0:C, h, :, :], ALU.subtract).then_inc(m_split, 1)
                for b in range(B):
                    vec.wait_ge(sx_hi, b + 1)
                    nc.vector.tensor_tensor(SX[C:P, b, :], at.score_ps[b % 2][0:C, :], SX[0:C, b, :],
                                            ALU.subtract).then_inc(sx_lo, 1)
                for half in range(2):
                    cols = slice(half * HALF, (half + 1) * HALF)
                    vec.wait_ge(y_hi, half + 1)
                    nc.vector.tensor_tensor(Yl[:, 0, cols], misc_ps[0:C, :], Y2[0:C, 0, cols],
                                            ALU.subtract).then_inc(misc_read, OFF - 1 if half == 0 else 1)
                vec.wait_ge(cleared, 1)
                vec.wait_ge(s["filled"], 1)
                with vec.Fori(0, PAIRS // 2) as i:
                    for k in range(STEPS):
                        vec_step(vec, 2 * i + k // NT, k)
                for t in range(NT):
                    vec_step(vec, PAIRS, t, new=False)

            @block.tensor
            def _(pe):
                pe.wait_ge(loaded, 16 * 3)
                for h in range(HEADS):
                    if h:
                        pe.wait_ge(w_copied, 2 * h - 1)
                    nc.tensor.transpose(at.turn_ps[0][:, 0:C], wh[:, h, :], ident[0:C, 0:C]).then_inc(w_turned, 1)
                    pe.wait_ge(w_copied, 2 * h + 1)
                    if h:
                        pe.wait_ge(m_split, h)
                    nc.tensor.matmul(at.turn_ps[1][:, 0:C], whT[:, h % 2, :, :].rearrange("p r c -> p (r c)"),
                                     whT[:, h % 2, 0, :], start=True, stop=True).then_inc(m_made, 1)
                for b in range(B):
                    if b >= 2:
                        pe.wait_ge(sx_lo, b - 1)
                    for t in range(NT):
                        last = nc.tensor.transpose(at.score_ps[b % 2][0:C, t * P:(t + 1) * P], Xrows[:, row(b, t), :], ident[:])
                    last.then_inc(sx_banked, 1)
                pe.wait_ge(sx_lo, B)
                pe.wait_ge(staged, 1)
                for half in range(2):
                    if half:
                        pe.wait_ge(misc_read, OFF - 1)
                    cols = slice(half * HALF, (half + 1) * HALF)
                    nc.tensor.matmul(misc_ps[:], Mh_now[:, 0, :], SX[:, 0, cols], start=True, stop=False)
                    nc.tensor.matmul(misc_ps[:], Ml_now[:, 0, :], SX[0:C, 0, cols], start=False,
                                     stop=True).then_inc(misc_made, OFF - 1 if half == 0 else 1)
                pe.wait_ge(misc_read, OFF)
                pe.wait_ge(s["filled"], 1)
                with pe.Fori(0, PAIRS // 2) as i:
                    for k in range(STEPS):
                        pe_step(pe, 2 * i + k // NT, k)
                for t in range(NT):
                    pe_step(pe, PAIRS, t, new=False)

        with ExitStack() as scope:
            at = attention(scope, "fin")
            s, Y2, Yl, SX = at.s, at.Y2, at.Yl, at.SX
            V = sb("V", [P, B, NT, C], F32, scope)
            b_out = sb("b_out", [P, C], F32, scope)
            stats = sb("stats1", [P, 4, TOK], F32, scope)
            R = sb("R1", [P, TOK, C], F32, scope)
            loaded = sem("fin_loaded")
            v_banked, v_copied, sx_hi, sx_lo = sem("fin_v_banked"), sem("fin_v_copied"), sem("fin_sx_hi"), sem("fin_sx_lo")
            y_made = sem("fin_y_made")
            norm_v, norm_a, norm_steps = sem("fin_norm_v"), sem("fin_norm_a"), sem("fin_norm_steps")
            TILES = B * NT

            def make_y(pair, u):
                b = bass.ds(pair, 1)
                nc.vector.tensor_copy(Y2[0:C, u, :].unsqueeze(1), SX[0:C, b, :])
                nc.vector.tensor_copy(Y2[C:P, u, :].unsqueeze(1), SX[0:C, b, :])
                return nc.vector.tensor_copy(Yl[:, u, :].unsqueeze(1), SX[C:P, b, :])

            def out_row(p, k):
                t = k % NT
                r = row(p, t - 5) if t >= 5 else row((p + B - 1) % B, t - 5 + NT)
                return R[:, bass.ds(r, 1), :]

            def pe_step(pe, p, k, new=True):
                t = k % NT
                g = NT * p + t
                if new:
                    if t == 0:
                        pe.wait_ge(y_made, p + 1)
                    at.pe_scores(pe, g, k, k // NT, bass.ds(p, 1))
                if new or t < 3:
                    at.pe_turn(pe, g - 3, (k - 3) % STEPS)
                if new or t < 4:
                    b = bass.ds(p if t >= 4 else (p + B - 1) % B, 1)
                    at.pe_mix(pe, g - 4, (k - 4) % STEPS, lambda mt: V[:, b, mt, :])

            def act_step(act, p, k, new=True):
                t = k % NT
                g = NT * p + t
                if new or t < 2:
                    at.act_exp(act, g - 2, (k - 2) % STEPS)
                if new or t < 3:
                    at.act_copy(act, g - 3, (k - 3) % STEPS)

            def vec_step(vec, p, k, new=True):
                t = k % NT
                g = NT * p + t
                if new or t < 5:
                    at.vec_norm(vec, g - 5, (k - 5) % STEPS, out_row(p, k))
                if new:
                    at.vec_weigh(vec, g, k)
                    if t == 1:
                        make_y((p + 1) % B, 1 - k // NT).then_inc(y_made, 1)
                if new or t < 1:
                    at.vec_shift(vec, g - 1, (k - 1) % STEPS)
                if new:
                    at.vec_zero(vec, g, k)

            block = scope.enter_context(nc.Block())

            @block.sync
            def _(sp):
                sp.dma_start(b_out[:], L1_b_out.unsqueeze(0).to_broadcast([P, C])).then_inc(loaded, 16)

            @block.gpsimd
            def _(pool):
                at.init_pool(pool)
                with pool.Fori(0, B // 2) as i:
                    for k in range(STEPS):
                        at.pool_zero(pool, STEPS * i + k, k)

            @block.scalar
            def _(act):
                for b in range(B):
                    nc.scalar.copy(SX[0:C, b, :], h2T[:, b + 1, :]).then_inc(sx_hi, 1)
                for b in range(B):
                    act.wait_ge(v_banked, b + 1)
                    nc.scalar.copy(V[:, b, :, :].rearrange("p t c -> p (t c)"), at.turn_ps[b % 2][:]).then_inc(v_copied, 1)
                act.wait_ge(s["filled"], 1)
                with act.Fori(0, B // 2) as i:
                    for k in range(STEPS):
                        act_step(act, 2 * i + k // NT, k)
                for t in range(NT):
                    act_step(act, B, t, new=False)
                norm_root(act, norm_a, norm_v, stats)

            @block.vector
            def _(vec):
                at.init_vec(vec)
                for b in range(B):
                    vec.wait_ge(sx_hi, b + 1)
                    nc.vector.tensor_tensor(SX[C:P, b, :], h2T[:, b + 1, :], SX[0:C, b, :], ALU.subtract).then_inc(sx_lo, 1)
                vec.wait_ge(sx_lo, 1)
                make_y(0, 0).then_inc(y_made, 1)
                vec.wait_ge(s["filled"], 1)
                with vec.Fori(0, B // 2) as i:
                    for k in range(STEPS):
                        vec_step(vec, 2 * i + k // NT, k)
                for t in range(NT):
                    vec_step(vec, B, t, new=False)
                vec.wait_ge(loaded, 16)
                vec.wait_ge(s["normed"], OFF + TILES)
                nc.vector.tensor_tensor(R[:], R[:], b_out[:].unsqueeze(1).to_broadcast([P, TOK, C]),
                                        ALU.add).then_inc(norm_steps, 1)
                vec.wait_ge(norm_steps, 1)
                nc.vector.scalar_tensor_tensor(out=R[:], in0=R[:], scalar=0.01, in1=R[:], op0=ALU.mult,
                                               op1=ALU.max).then_inc(norm_steps, 1)
                vec.wait_ge(norm_steps, 2)
                residual_norm(vec, norm_a, norm_v, norm_steps, R[:], V[:].rearrange("p b t c -> p (b t) c"), stats, 2)

            @block.tensor
            def _(pe):
                for b in range(B):
                    if b >= 2:
                        pe.wait_ge(v_copied, b - 1)
                    for t in range(NT):
                        last = nc.tensor.transpose(at.turn_ps[b % 2][:, t * C:(t + 1) * C],
                                                   h2T[:, b + 1, t * P:(t + 1) * P], ident[0:C, 0:C])
                    last.then_inc(v_banked, 1)
                pe.wait_ge(v_copied, B)
                pe.wait_ge(sx_lo, B)
                pe.wait_ge(s["filled"], 1)
                with pe.Fori(0, B // 2) as i:
                    for k in range(STEPS):
                        pe_step(pe, 2 * i + k // NT, k)
                for t in range(NT):
                    pe_step(pe, B, t, new=False)
        acc_scope.close()

        NEG = -1.0e9
        Xj = X[:].rearrange("p j t h c -> p j t (h c)")
        l2_scope = keep.enter_context(ExitStack())
        ind = sb("ind", [P, J, NT, 2, C], F32, l2_scope)
        agg = sb("agg", [P, J, E], F32, l2_scope)
        gate = sb("gate", [P, J, N], F32, l2_scope)
        coefT = sb("coefT", [P, J, N], F32, l2_scope)
        hT_hi = sb("hT_hi", [P, J, N], F32R, l2_scope)
        hT_lo = sb("hT_lo", [P, J, N], F32R, l2_scope)
        fcw = sb("fcw", [P, P], F32, l2_scope)
        fcb = sb("fcb", [P, 1], F32, l2_scope)
        av = sb("av", [P, 1], F32, l2_scope)
        late_scope = ExitStack()
        hT = sb("hT", [P, J, N], F32, late_scope)
        hN = sb("hN", [P, J, NT, P], F32, late_scope)

        def couple_blocks(m):
            return m[0:C, 0:C], m[C:P, C:P]

        with ExitStack() as scope:
            AT = sb("AT2", [P, NT, N], F32, scope)
            AxT, xT = gate, coefT
            w2 = sb("w2", [P, P], F32, scope)
            wi2 = sb("wi2", [P, P], F32, scope)
            deg = sb("deg", [P, NT], F32, scope)
            rdeg = sb("rdeg", [P, NT], F32, scope)
            banks = [ps(f"l2_bank{k}", [P, HALF], scope) for k in range(2)]
            wide = [ps(f"l2_wide{k}", [P, N], scope) for k in range(3)]
            zeroed, loaded = sem("l2_zeroed"), sem("l2_loaded")
            at_banked, at_copied = sem("l2_at_banked"), sem("l2_at_copied")
            xt_banked, xt_copied = sem("l2_xt_banked"), sem("l2_xt_copied")
            ax_banked, ax_copied = sem("l2_ax_banked"), sem("l2_ax_copied")
            h_banked, h_copied = sem("l2_h_banked"), sem("l2_h_copied")
            deg_made = sem("l2_deg_made")

            block = scope.enter_context(nc.Block())

            @block.sync
            def _(sp):
                sp.wait_ge(zeroed, 2)
                for m, w in ((w2, L2_W), (wi2, L2_W_ind)):
                    for part in couple_blocks(m):
                        sp.dma_start(part, w).then_inc(loaded, 16)
                for half in range(2):
                    sp.dma_start(fcw[half * C:(half + 1) * C, :], L2_fcW).then_inc(loaded, 16)
                sp.dma_start(fcb[:], L2_fcb.unsqueeze(1)).then_inc(loaded, 16)
                sp.dma_start(av[:], L2_av.unsqueeze(1)).then_inc(loaded, 16)
                sp.wait_ge(loaded, 16 * 8)

            @block.gpsimd
            def _(pool):
                nc.gpsimd.memset(w2[:], 0.0).then_inc(zeroed, 1)
                nc.gpsimd.memset(wi2[:], 0.0).then_inc(zeroed, 1)

            @block.scalar
            def _(act):
                copy_adj(act, nc.scalar.copy, AT, banks, at_banked, at_copied)
                for j in range(J):
                    act.wait_ge(ax_banked, j + 1)
                    nc.scalar.copy(AxT[:, j, :], wide[j % 2][:]).then_inc(ax_copied, 1)
                for j in range(J):
                    act.wait_ge(h_banked, 3 * j + 2)
                    nc.scalar.copy(hN[:, j, :, :].rearrange("p t f -> p (t f)"), wide[1][:]).then_inc(h_copied, 1)

            @block.vector
            def _(vec):
                nc.vector.tensor_reduce(deg[:], A[:], AX.X, ALU.add).then_inc(deg_made, 1)
                vec.wait_ge(deg_made, 1)
                nc.vector.tensor_scalar(deg[:], deg[:], 1.0, None, ALU.max).then_inc(deg_made, 1)
                vec.wait_ge(deg_made, 2)
                nc.vector.reciprocal(rdeg[:], deg[:]).then_inc(deg_made, 1)
                for j in range(J):
                    vec.wait_ge(xt_banked, j + 1)
                    nc.vector.tensor_copy(xT[:, j, :], wide[2][:]).then_inc(xt_copied, 1)
                vec.wait_ge(deg_made, 3)
                for j in range(J):
                    vec.wait_ge(h_banked, 3 * j + 1)
                    nc.vector.tensor_copy(hT[:, j, :], wide[0][:]).then_inc(h_copied, 1)
                    vec.wait_ge(h_banked, 3 * j + 3)
                    nc.vector.tensor_tensor(ind[:, j].rearrange("p t h f -> p t (h f)"),
                                            wide[2][:].rearrange("p (t k) -> p t k", k=P),
                                            rdeg[:].unsqueeze(2).to_broadcast([P, NT, P]), ALU.mult).then_inc(h_copied, 1)

            @block.tensor
            def _(pe):
                for j in range(J):
                    if j:
                        pe.wait_ge(xt_copied, j)
                    for t in range(NT):
                        last = nc.tensor.transpose(wide[2][:, t * P:(t + 1) * P], Xj[:, j, t, :], ident[:])
                    last.then_inc(xt_banked, 1)
                transpose_adj(pe, AT, banks, at_banked, at_copied)
                pe.wait_ge(at_copied, 2 * NT)
                for j in range(J):
                    if j >= 2:
                        pe.wait_ge(ax_copied, j - 1)
                    for half in range(2):
                        cols = slice(half * HALF, (half + 1) * HALF)
                        for mt in range(NT):
                            last = nc.tensor.matmul(wide[j % 2][:, cols], Xj[:, j, mt, :], AT[:, mt, cols],
                                                    start=(mt == 0), stop=(mt == NT - 1))
                    last.then_inc(ax_banked, 1)
                pe.wait_ge(ax_copied, J)
                pe.wait_ge(xt_copied, J)
                pe.wait_ge(loaded, 16 * 8)
                for j in range(J):
                    if j:
                        pe.wait_ge(h_copied, 3 * j)
                    for half in range(2):
                        cols = slice(half * HALF, (half + 1) * HALF)
                        last = nc.tensor.matmul(wide[0][:, cols], w2[:], xT[:, j, cols], start=True, stop=True)
                    last.then_inc(h_banked, 1)
                    for out_ps, left, right in ((wide[1], xT, w2), (wide[2], AxT, wi2)):
                        for t in range(NT):
                            cols = slice(t * P, (t + 1) * P)
                            last = nc.tensor.matmul(out_ps[:, cols], left[:, j, cols], right[:], start=True, stop=True)
                        last.then_inc(h_banked, 1)

        with ExitStack() as scope:
            incid = sb("incid", [P, NT, 2, E], F32, scope)
            member = sb("member", [P, NT, E], F32, scope)
            outside = sb("outside", [P, NT, E], F32, scope)
            memberT = sb("memberT", [P, N], F32, scope)
            outsideT = sb("outsideT", [P, N], F32, scope)
            a_rows = sb("a_rows", [P, 3], F32, scope)
            a_node2 = sb("a_node2", [P, P], F32, scope)
            a_gn2 = sb("a_gn2", [P, P], F32, scope)
            a_ge = sb("a_ge", [P, C], F32, scope)
            sc = sb("sc", [P, N], F32, scope)
            lk = sb("lk", [P, N], F32, scope)
            alpha = sb("alpha", [P, N], F32, scope)
            alphaT = sb("alphaT", [P, NT, P], F32, scope)
            cells = hN[:].rearrange("p j t k -> p (j t k)").rearrange("p (t b e) -> p t b e", t=NT, b=B)
            small = sb("small", [P, 24], F32, scope)
            elu_a = sb("elu_a", [P, J, E], F32, scope)
            heT = sb("heT", [C, J * P], F32, scope)
            th = sb("th", [P, J * P], F32, scope)
            se = sb("se", [P, B, E], F32, scope)
            cmax = sb("cmax", [P, NT * B], F32, scope)
            crcp = sb("crcp", [P, NT * B], F32, scope)
            banks = [ps(f"l2b_bank{k}", [P, HALF], scope) for k in range(2)]
            wide = [ps(f"l2b_wide{k}", [P, N], scope) for k in range(3)]
            zeroed, loaded = sem("l2b_zeroed"), sem("l2b_loaded")
            (s_made, s_copied, s_turned, s_turn_copied, s_agg, s_exped, s_gn, s_gexp, v_steps, s_h, s_he, s_he_c, s_fc,
             s_tanh, s_se, s_elu, s_ct, s_ct_copied, s_cexp, s_ht) = (
                sem(f"l2b_{n}") for n in ("scored", "score_copied", "turned", "turn_copied", "agg_made", "exped",
                                          "gn_made", "gate_exped", "vector_steps", "incid_turned", "he_turned",
                                          "he_copied", "fc_made", "tanhed", "se_made", "elu_exped", "coef_turned",
                                          "coef_copied", "coef_exped", "logits_ready"))
            block = scope.enter_context(nc.Block())

            @block.sync
            def _(sp):
                Hn = L2_H.rearrange("(t p) e -> p t e", p=P)
                for half in range(2):
                    sp.dma_start(incid[:, :, half, :], Hn).then_inc(loaded, 16)
                for k, v in enumerate((L2_a_node, L2_a_gn)):
                    for half in range(2):
                        sp.dma_start(a_rows[half * C:(half + 1) * C, k:k + 1], v.unsqueeze(1)).then_inc(loaded, 16)
                sp.dma_start(a_ge[:], L2_a_ge.unsqueeze(0).to_broadcast([P, C])).then_inc(loaded, 16)
                sp.wait_ge(loaded, 16 * 7)

            @block.gpsimd
            def _(pool):
                nc.gpsimd.memset(a_node2[:], 0.0).then_inc(zeroed, 1)
                nc.gpsimd.memset(a_gn2[:], 0.0).then_inc(zeroed, 1)

            @block.scalar
            def _(act):
                for j in range(J):
                    act.wait_ge(s_made, j + 1)
                    if j:
                        act.wait_ge(s_ht, 2 * j)
                    nc.scalar.copy(sc[:], wide[0][:]).then_inc(s_copied, 1)
                    act.wait_ge(s_ht, 2 * j + 2)
                    nc.scalar.activation(alpha[:], lk[:], ACT.Exp, bias=small[:, j:j + 1], scale=-1.0,
                                         accum_out=small[:, 4 + j:5 + j]).then_inc(s_exped, 1)
                    act.wait_ge(s_turned, j + 1)
                    nc.scalar.copy(alphaT[:].rearrange("p t k -> p (t k)"), wide[1][:]).then_inc(s_turn_copied, 1)
                    act.wait_ge(s_gn, j + 1)
                    act.wait_ge(v_steps, 100 * (j + 1))
                    nc.scalar.activation(gate[:, j, :], wide[2][:], ACT.Exp, bias=small[:, 12 + j:13 + j],
                                         scale=-1.0).then_inc(s_gexp, 1)
                act.wait_ge(v_steps, 400)
                nc.scalar.activation(elu_a[:], agg[:], ACT.Exp).then_inc(s_elu, 1)
                act.wait_ge(s_fc, 1)
                nc.scalar.activation(th[:], banks[1][:], ACT.Tanh, bias=fcb[:]).then_inc(s_tanh, 1)
                act.wait_ge(s_h, 2)
                nc.scalar.activation(cells, cells, ACT.Exp).then_inc(s_cexp, 1)
                for j in range(J):
                    act.wait_ge(s_ct, j + 1)
                    nc.scalar.copy(coefT[:, j, :], wide[j % 2][:]).then_inc(s_ct_copied, 1)

            @block.vector
            def _(vec):
                count = [0]

                def step(instruction, to=None):
                    n = 1 if to is None else to - count[0]
                    instruction.then_inc(v_steps, n)
                    count[0] += n
                    vec.wait_ge(v_steps, count[0])

                vec.wait_ge(loaded, 16 * 7)
                vec.wait_ge(zeroed, 2)
                for m, k in ((a_node2, 0), (a_gn2, 1)):
                    for half in range(2):
                        rows = slice(half * C, (half + 1) * C)
                        last = nc.vector.tensor_copy(m[rows, rows], a_rows[rows, k:k + 1].to_broadcast([C, C]))
                step(last, 3)
                step(nc.vector.tensor_scalar(member[:], incid[:, :, 0, :], 0.0, None, ALU.is_gt))
                step(nc.vector.tensor_scalar(outside[:], member[:], -NEG, NEG, ALU.mult, ALU.add))
                vec.wait_ge(s_h, 1)
                step(nc.vector.tensor_scalar(memberT[:], wide[0][:], 0.0, None, ALU.is_gt))
                step(nc.vector.tensor_scalar(outsideT[:], memberT[:], -NEG, NEG, ALU.mult, ALU.add), 10)
                for j in range(J):
                    vec.wait_ge(s_copied, j + 1)
                    if j:
                        vec.wait_ge(s_exped, j)
                    nc.vector.scalar_tensor_tensor(out=lk[:], in0=sc[:], scalar=0.2, in1=sc[:], op0=ALU.mult,
                                                   op1=ALU.max).then_inc(s_ht, 1)
                    vec.wait_ge(s_ht, 2 * j + 1)
                    step(nc.vector.tensor_tensor(lk[:], lk[:], memberT[:], ALU.mult))
                    nc.vector.tensor_tensor_reduce(lk[:], lk[:], outsideT[:], -1.0, 3.0e38, ALU.add, ALU.min,
                                                   small[:, j:j + 1]).then_inc(s_ht, 1)
                    step(nc.vector.tensor_copy(hT_hi[:, j, :], hT[:, j, :]))
                    step(nc.vector.tensor_tensor(hT_lo[:, j, :], hT[:, j, :], hT_hi[:, j, :], ALU.subtract))
                    vec.wait_ge(s_exped, j + 1)
                    step(nc.vector.reciprocal(small[:, 8 + j:9 + j], small[:, 4 + j:5 + j]))
                    vec.wait_ge(s_agg, j + 1)
                    for half in range(2):
                        rows = slice(half * C, (half + 1) * C)
                        last = nc.vector.tensor_scalar(agg[rows, j, :], banks[0][rows, rows], small[rows, 8 + j:9 + j],
                                                       None, ALU.mult)
                    step(last)
                    step(nc.vector.tensor_tensor_reduce(elu_a[:, j, :], agg[:, j, :], a_ge[:], -1.0, 0.0, ALU.mult,
                                                        ALU.add, small[:, 12 + j:13 + j]), 100 * (j + 1))
                    vec.wait_ge(s_gexp, j + 1)
                    step(nc.vector.tensor_scalar(gate[:, j, :], gate[:, j, :], 1.0, None, ALU.add))
                    step(nc.vector.reciprocal(gate[:, j, :], gate[:, j, :]))
                vec.wait_ge(s_elu, 1)
                step(nc.vector.tensor_scalar(elu_a[:], elu_a[:], 1.0, -1.0, ALU.min, ALU.add))
                step(nc.vector.tensor_tensor(elu_a[:], elu_a[:], agg[:], ALU.max), 500)
                vec.wait_ge(s_he, 1)
                nc.vector.tensor_copy(heT[:], banks[0][0:C, :]).then_inc(s_he_c, 1)
                vec.wait_ge(s_se, 1)
                step(nc.vector.tensor_copy(se[:].rearrange("p b e -> p (b e)"), banks[0][:]))
                shape = [P, NT, B, E]
                step(nc.vector.tensor_tensor(cells, se[:].unsqueeze(1).to_broadcast(shape),
                                             member[:].unsqueeze(2).to_broadcast(shape), ALU.mult))
                step(nc.vector.tensor_tensor(cells, cells, outside[:].unsqueeze(2).to_broadcast(shape), ALU.add))
                flat = cells.rearrange("p t b e -> p (t b) e")
                step(nc.vector.tensor_reduce(cmax[:], flat, AX.X, ALU.max))
                nc.vector.tensor_tensor(flat, flat, cmax[:].unsqueeze(2).to_broadcast([P, NT * B, E]),
                                        ALU.subtract).then_inc(s_h, 1)
                vec.wait_ge(s_cexp, 1)
                step(nc.vector.tensor_reduce(cmax[:], flat, AX.X, ALU.add))
                step(nc.vector.reciprocal(crcp[:], cmax[:]))
                step(nc.vector.tensor_tensor(flat, flat, crcp[:].unsqueeze(2).to_broadcast([P, NT * B, E]), ALU.mult), 600)

            @block.tensor
            def _(pe):
                pe.wait_ge(loaded, 16 * 7)
                for t in range(NT):
                    last = nc.tensor.transpose(wide[0][:, t * P:(t + 1) * P], incid[:, t, :, :].rearrange("p h e -> p (h e)"),
                                               ident[:])
                last.then_inc(s_h, 1)
                pe.wait_ge(v_steps, 10)
                for j in range(J):
                    if j:
                        pe.wait_ge(s_copied, j)
                    for half in range(2):
                        cols = slice(half * HALF, (half + 1) * HALF)
                        last = nc.tensor.matmul(wide[0][:, cols], a_node2[:], hT[:, j, cols], start=True, stop=True)
                    last.then_inc(s_made, 1)
                    if j:
                        pe.wait_ge(s_gexp, j)
                    for half in range(2):
                        cols = slice(half * HALF, (half + 1) * HALF)
                        last = nc.tensor.matmul(wide[2][:, cols], a_gn2[:], hT[:, j, cols], start=True, stop=True)
                    last.then_inc(s_gn, 1)
                    pe.wait_ge(s_exped, j + 1)
                    for t in range(NT):
                        last = nc.tensor.transpose(wide[1][:, t * P:(t + 1) * P], alpha[:, t * P:(t + 1) * P], ident[:])
                    last.then_inc(s_turned, 1)
                    pe.wait_ge(s_turn_copied, j + 1)
                    if j:
                        pe.wait_ge(v_steps, 100 * j)
                    for t in range(NT):
                        last = nc.tensor.matmul(banks[0][:, 0:P], alphaT[:, t, :], hN[:, j, t, :], start=(t == 0),
                                                stop=(t == NT - 1))
                    last.then_inc(s_agg, 1)
                pe.wait_ge(v_steps, 500)
                for j in range(J):
                    last = nc.tensor.transpose(banks[0][0:C, j * P:(j + 1) * P], elu_a[:, j, :], ident[:])
                last.then_inc(s_he, 1)
                pe.wait_ge(s_he_c, 1)
                nc.tensor.matmul(banks[1][:], fcw[0:C, :], heT[:], start=True, stop=True).then_inc(s_fc, 1)
                pe.wait_ge(s_tanh, 1)
                nc.tensor.matmul(banks[0][:], av[:].to_broadcast([P, P]), th[:], start=True, stop=True).then_inc(s_se, 1)
                pe.wait_ge(v_steps, 600)
                for j in range(J):
                    if j >= 2:
                        pe.wait_ge(s_ct_copied, j - 1)
                    for t in range(NT):
                        last = nc.tensor.transpose(wide[j % 2][:, t * P:(t + 1) * P],
                                                   cells[:, t, 2 * j:2 * j + 2, :].rearrange("p b e -> p (b e)"), ident[:])
                    last.then_inc(s_ct, 1)
        late_scope.close()

        GF = 8
        GROUPS = J * C // GF
        PER = C // GF
        gT = sb("gT_acc", [P, J, N], F32, l2_scope)
        with ExitStack() as scope:
            agg1 = sb("agg1", [P, J, E], F32, scope)
            ident_r = sb("ident_r", [P, 2, C], F32R, scope)
            window = sb("window", [P, 2 * P], F32, scope)
            pick = sb("pick", [P, 2, GF, 2, E], F32R, scope)
            place = sb("place", [P, 2, P + GF], F32, scope)
            a_now = sb("a_now", [P, 2, GF], F32, scope)
            a1_now = sb("a1_now", [P, 2, GF], F32, scope)
            u_buf = sb("u_buf", [P, 2, N], F32, scope)
            ex = sb("ex", [P, 2, N], F32, scope)
            lin = sb("lin", [P, 2, N], F32, scope)
            el = sb("el", [P, 2, N], F32, scope)
            spread = [ps(f"spread{k}", [P, N], scope) for k in range(2)]
            summed = [ps(f"summed{k}", [P, N], scope) for k in range(2)]
            made, ready, staged, picked = (sem(f"l2c_{n}") for n in ("made", "ready", "staged", "picked"))
            s_spread, s_u, s_ex, s_lin, s_el, s_weighted, s_summed, s_added = (
                sem(f"l2c_{n}") for n in ("spread", "u", "ex", "lin", "elu", "weighted", "summed", "added"))
            block = scope.enter_context(nc.Block())

            def stage_group(pool, group, par):
                g = group % PER
                nc.gpsimd.tensor_copy(place[:, par, :], window[:, bass.ds(P - GF - g * GF, P + GF)])
                nc.gpsimd.tensor_copy(a_now[:, par, :], agg[:].rearrange("p j f -> p (j f)")[:, bass.ds(group * GF, GF)])
                return nc.gpsimd.tensor_copy(a1_now[:, par, :],
                                             agg1[:].rearrange("p j f -> p (j f)")[:, bass.ds(group * GF, GF)])

            def pick_group(group, par):
                cols = ident_r[:, :, bass.ds(group % PER * GF, GF)].rearrange("p h f -> p f h")
                return nc.vector.tensor_copy(pick[:, par], cols.unsqueeze(3).to_broadcast([P, GF, 2, E]))

            def pe_spread(pe, q, k, couple):
                k = k % (2 * GF)
                par, f = k // GF, k % GF
                stay = pick[:, par, f].rearrange("p h e -> p (h e)")
                for half in range(2):
                    cols = slice(half * HALF, (half + 1) * HALF)
                    o = spread[k % 2][:, cols].unsqueeze(1)
                    nc.tensor.matmul(o, stay, hT_hi[:, bass.ds(couple, 1), cols], start=True, stop=False)
                    last = nc.tensor.matmul(o, stay, hT_lo[:, bass.ds(couple, 1), cols], start=False, stop=True)
                last.then_inc(s_spread, 1)

            def vec_u(vec, q, k, couple):
                k = k % (2 * GF)
                vec.wait_ge(s_spread, q + 1)
                vec.wait_ge(s_lin, q + 1)
                nc.vector.scalar_tensor_tensor(out=u_buf[:, k % 2, :].unsqueeze(1), in0=spread[k % 2][:].unsqueeze(1),
                                               scalar=a_now[:, k // GF, k % GF:k % GF + 1],
                                               in1=gate[:, bass.ds(couple, 1), :],
                                               op0=ALU.subtract, op1=ALU.mult).then_inc(s_u, 1)

            @block.gpsimd
            def _(pool):
                nc.gpsimd.memset(gT[:], 0.0).then_inc(s_lin, 2)
                nc.gpsimd.memset(window[:], 0.0).then_inc(s_el, 2)
                nc.gpsimd.memset(u_buf[:], 0.0).then_inc(s_summed, 2)
                pool.wait_ge(s_el, 2)
                pool.wait_ge(s_lin, 2)
                pool.wait_ge(s_summed, 2)
                nc.gpsimd.memset(window[0:C, P - 1:P], 1.0)
                nc.gpsimd.memset(window[C:P, P + C - 1:P + C], 1.0).then_inc(made, 1)
                pool.wait_ge(ready, 2)
                pool.wait_ge(made, 1)
                stage_group(pool, 0, 0).then_inc(staged, 1)
                with pool.Fori(0, GROUPS // 2) as i:
                    for k in range(2 * GF):
                        q = 2 * GF * i + k
                        couple = (2 * i + k // GF) // PER
                        if k % GF == 2:
                            pool.wait_ge(s_summed, q - 2 + 2)
                            stage_group(pool, (2 * i + k // GF + 1) % GROUPS, 1 - k // GF).then_inc(staged, 1)
                        pool.wait_ge(s_el, q + 3)
                        pool.nop(nofuse=True)
                        nc.gpsimd.tensor_tensor(el[:, k % 2, :].unsqueeze(1), el[:, k % 2, :].unsqueeze(1),
                                                coefT[:, bass.ds(couple, 1), :], ALU.mult).then_inc(s_weighted, 1)

            @block.scalar
            def _(act):
                act.wait_ge(staged, 1)
                with act.Fori(0, GROUPS // 2) as i:
                    for k in range(2 * GF):
                        q = 2 * GF * i + k
                        act.wait_ge(s_u, q + 1)
                        act.wait_ge(s_el, q + 1)
                        nc.scalar.activation(ex[:, k % 2, :], u_buf[:, k % 2, :], ACT.Exp,
                                             bias=a_now[:, k // GF, k % GF:k % GF + 1]).then_inc(s_ex, 1)
                        nc.scalar.activation(lin[:, k % 2, :], u_buf[:, k % 2, :], ACT.Identity,
                                             bias=a1_now[:, k // GF, k % GF:k % GF + 1]).then_inc(s_lin, 1)

            @block.vector
            def _(vec):
                nc.vector.tensor_scalar(agg1[:], agg[:], 1.0, None, ALU.add).then_inc(ready, 1)
                nc.vector.tensor_copy(ident_r[:].rearrange("p h f -> p (h f)"), ident[:]).then_inc(ready, 1)
                nc.vector.memset(summed[1][:], 0.0).then_inc(s_added, 1)
                vec.wait_ge(staged, 1)
                vec.wait_ge(ready, 2)
                pick_group(0, 0).then_inc(picked, 1)
                vec_u(vec, 0, 0, 0)

                def add_group(group, par):
                    acc = gT[:, bass.ds(group // PER, 1), :]
                    nc.vector.tensor_tensor(acc, acc, summed[par][:].unsqueeze(1), ALU.add).then_inc(s_added, 1)

                with vec.Fori(0, GROUPS // 2) as i:
                    for k in range(2 * GF):
                        q = 2 * GF * i + k
                        nxt = k + 1
                        if nxt % GF == 0:
                            vec.wait_ge(staged, 2 * i + nxt // GF + 1)
                        vec_u(vec, q + 1, nxt, (2 * i + nxt // GF) // PER % J)
                        vec.wait_ge(s_lin, q + 3)
                        vec.wait_ge(s_summed, q + 1)
                        nc.vector.scalar_tensor_tensor(out=el[:, k % 2, :], in0=ex[:, k % 2, :], scalar=1.0,
                                                       in1=lin[:, k % 2, :], op0=ALU.min, op1=ALU.max).then_inc(s_el, 1)
                        if k % GF == 4:
                            vec.wait_ge(s_summed, q - 4 + 2)
                            add_group((2 * i + k // GF + GROUPS - 1) % GROUPS, 1 - k // GF)
                            pick_group((2 * i + k // GF + 1) % GROUPS, 1 - k // GF).then_inc(picked, 1)
                vec.wait_ge(s_summed, GROUPS * GF + 2)
                add_group(GROUPS - 1, 1)

            @block.tensor
            def _(pe):
                pe.wait_ge(staged, 1)
                pe.wait_ge(picked, 1)
                for q in range(2):
                    pe_spread(pe, q, q, 0)
                with pe.Fori(0, GROUPS // 2) as i:
                    for k in range(2 * GF):
                        q = 2 * GF * i + k
                        par, f = k // GF, k % GF
                        pe.wait_ge(s_weighted, q + 1)
                        if f == 0:
                            pe.wait_ge(s_added, 2 * i + par + 1)
                        for half in range(2):
                            cols = slice(half * HALF, (half + 1) * HALF)
                            last = nc.tensor.matmul(summed[par][:, cols], place[:, par, GF - 1 - f:GF - 1 - f + P],
                                                    el[:, k % 2, cols], start=(f == 0), stop=(f == GF - 1))
                        last.then_inc(s_summed, 1)
                        nxt = k + 2
                        if nxt % GF == 0:
                            pe.wait_ge(staged, 2 * i + nxt // GF + 1)
                            pe.wait_ge(picked, 2 * i + nxt // GF + 1)
                        pe.wait_ge(s_u, q + 1)
                        pe_spread(pe, q + 2, nxt, (2 * i + nxt // GF) // PER % J)

        with ExitStack() as scope:
            indT = sb("indT", [P, J, N], F32, scope)
            gN = sb("gN", [P, J, NT, 2, C], F32, scope)
            th = [sb(f"th{k}", [P, HALF], F32, scope) for k in range(2)]
            score = sb("score", [P, 2, TOK], F32, scope)
            smax = sb("smax", [P, TOK], F32, scope)
            stats = sb("stats2", [P, 4, TOK], F32, scope)
            R = sb("R2", [P, TOK, C], F32, scope)
            wide = [ps(f"l2d_wide{k}", [P, N], scope) for k in range(2)]
            fc = [ps(f"l2d_fc{k}", [P, HALF], scope) for k in range(2)]
            score_ps = ps("l2d_score", [P, 2 * TOK], scope)
            shifted, turned, copied, fc_made, tanhed, scored, exped, steps = (
                sem(f"l2d_{n}") for n in ("shifted", "turned", "copied", "fc_made", "tanhed", "scored", "exped", "steps"))
            norm_v, norm_a = sem("l2d_norm_v"), sem("l2d_norm_a")
            block = scope.enter_context(nc.Block())
            slabs = [(kind, j, h, half) for kind in range(2) for j in range(J) for h in range(2) for half in range(2)]

            @block.scalar
            def _(act):
                for n in range(len(slabs)):
                    act.wait_ge(fc_made, n + 1)
                    if n >= 2:
                        act.wait_ge(scored, n - 1)
                    nc.scalar.activation(th[n % 2][:], fc[n % 2][:], ACT.Tanh, bias=fcb[:]).then_inc(tanhed, 1)
                act.wait_ge(steps, 4)
                nc.scalar.activation(score[:], score[:], ACT.Exp).then_inc(exped, 1)
                norm_root(act, norm_a, norm_v, stats)

            @block.vector
            def _(vec):
                nc.vector.tensor_scalar(gT[:], gT[:], -1.0, None, ALU.add).then_inc(shifted, 1)
                for n in range(2 * J):
                    j = n // 2
                    vec.wait_ge(turned, n + 1)
                    if n % 2 == 0:
                        nc.vector.tensor_copy(indT[:, j, :], wide[0][:]).then_inc(copied, 1)
                    else:
                        nc.vector.tensor_copy(gN[:, j].rearrange("p t h f -> p (t h f)"), wide[1][:]).then_inc(copied, 1)
                vec.wait_ge(scored, len(slabs))
                flat = score[:].rearrange("p k r -> p (k r)")
                count = [0]

                def step(instruction):
                    instruction.then_inc(steps, 1)
                    count[0] += 1
                    vec.wait_ge(steps, count[0])

                step(nc.vector.tensor_copy(flat, score_ps[:]))
                step(nc.vector.tensor_tensor(smax[:], score[:, 0], score[:, 1], ALU.max))
                step(nc.vector.tensor_tensor(score[:, 0], score[:, 0], smax[:], ALU.subtract))
                step(nc.vector.tensor_tensor(score[:, 1], score[:, 1], smax[:], ALU.subtract))
                vec.wait_ge(exped, 1)
                step(nc.vector.tensor_tensor(smax[:], score[:, 0], score[:, 1], ALU.add))
                step(nc.vector.reciprocal(smax[:], smax[:]))
                step(nc.vector.tensor_tensor(score[:, 0], score[:, 0], smax[:], ALU.mult))
                step(nc.vector.tensor_tensor(score[:, 1], score[:, 1], smax[:], ALU.mult))
                wide_shape = [P, TOK, C]
                weight = [score[:, k].unsqueeze(2).to_broadcast(wide_shape) for k in range(2)]
                indf, gf = (m[:].rearrange("p j t h c -> p (j t h) c") for m in (ind, gN))
                step(nc.vector.tensor_tensor(R[:], indf, weight[0], ALU.mult))
                step(nc.vector.tensor_tensor(gf, gf, weight[1], ALU.mult))
                step(nc.vector.tensor_tensor(R[:], R[:], gf, ALU.add))
                residual_norm(vec, norm_a, norm_v, steps, R[:], gf, stats, count[0])

            @block.tensor
            def _(pe):
                indj = ind[:].rearrange("p j t h f -> p j t (h f)")
                for j in range(J):
                    if j:
                        pe.wait_ge(copied, 2 * j)
                    for t in range(NT):
                        last = nc.tensor.transpose(wide[0][:, t * P:(t + 1) * P], indj[:, j, t, :], ident[:])
                    last.then_inc(turned, 1)
                    if j == 0:
                        pe.wait_ge(shifted, 1)
                    for t in range(NT):
                        last = nc.tensor.transpose(wide[1][:, t * P:(t + 1) * P], gT[:, j, t * P:(t + 1) * P], ident[:])
                    last.then_inc(turned, 1)
                pe.wait_ge(copied, 2 * J)

                def scores_of(n):
                    kind, j, h, half = slabs[n]
                    pe.wait_ge(tanhed, n + 1)
                    for q in range(4):
                        col = kind * TOK + row(2 * j + h, 4 * half + q)
                        last = nc.tensor.matmul(score_ps[:, col:col + 1], th[n % 2][:, q * P:(q + 1) * P], av[:],
                                                start=True, stop=True)
                    last.then_inc(scored, 1)

                for n, (kind, j, h, half) in enumerate(slabs):
                    if n >= 2:
                        pe.wait_ge(tanhed, n - 1)
                    rows, cols = slice(h * C, (h + 1) * C), slice(half * HALF, (half + 1) * HALF)
                    nc.tensor.matmul(fc[n % 2][:], fcw[rows, :], (gT if kind else indT)[rows, j, cols], start=True,
                                     stop=True).then_inc(fc_made, 1)
                    if n:
                        scores_of(n - 1)
                scores_of(len(slabs) - 1)
        l2_scope.close()

        with ExitStack() as scope:
            AT = sb("AT3", [P, NT, N], F32, scope)
            AxT = sb("AxT3", [P, J, N], F32, scope)
            w_nl = sb("w_nl", [P, 2], F32, scope)
            b_nl = sb("b_nl", [C, 1], F32, scope)
            w_out = sb("w_out", [C, 2, C], F32, scope)
            w_outT = sb("w_outT", [P, C], F32, scope)
            mix = sb("mix", [P, P], F32, scope)
            b_out = sb("b_out3", [P, C], F32, scope)
            v = sb("v", [P, 1], F32, scope)
            const = sb("const", [P, C], F32, scope)
            R = sb("R3", [P, TOK, C], F32, scope)
            T = sb("T3", [P, TOK, C], F32, scope)
            stats = sb("stats3", [P, 4, TOK], F32, scope)
            banks = [ps(f"l3_bank{k}", [P, HALF], scope) for k in range(2)]
            wide = [ps(f"l3_wide{k}", [P, N], scope) for k in range(3)]
            loaded, cleared, prep, prep_t = sem("l3_loaded"), sem("l3_cleared"), sem("l3_prep"), sem("l3_prep_t")
            at_banked, at_copied = sem("l3_at_banked"), sem("l3_at_copied")
            ax_banked, ax_copied = sem("l3_ax_banked"), sem("l3_ax_copied")
            out_banked, out_taken = sem("l3_out_banked"), sem("l3_out_taken")
            norm_v, norm_a, norm_steps = sem("l3_norm_v"), sem("l3_norm_a"), sem("l3_norm_steps")
            block = scope.enter_context(nc.Block())

            @block.sync
            def _(sp):
                for half in range(2):
                    sp.dma_start(w_nl[half * C:(half + 1) * C, :], L3_w_nl).then_inc(loaded, 16)
                    sp.dma_start(w_out[:, half, :], L3_w_out).then_inc(loaded, 16)
                sp.dma_start(b_nl[:], L3_b_nl.unsqueeze(1)).then_inc(loaded, 16)
                sp.dma_start(b_out[:], L3_b_out.unsqueeze(0).to_broadcast([P, C])).then_inc(loaded, 16)
                sp.wait_ge(loaded, 16 * 6)

            @block.gpsimd
            def _(pool):
                nc.gpsimd.memset(mix[:], 0.0).then_inc(cleared, 1)

            @block.scalar
            def _(act):
                copy_adj(act, nc.scalar.copy, AT, banks, at_banked, at_copied)
                for j in range(J):
                    act.wait_ge(ax_banked, j + 1)
                    nc.scalar.copy(AxT[:, j, :], wide[j % 2][:]).then_inc(ax_copied, 1)
                norm_root(act, norm_a, norm_v, stats)

            @block.vector
            def _(vec):
                vec.wait_ge(loaded, 16 * 6)
                vec.wait_ge(cleared, 1)
                nc.vector.tensor_scalar(v[:], w_nl[:, 0:1], w_nl[:, 1:2], 1.0 / 2.0 ** 0.5, ALU.add,
                                        ALU.mult).then_inc(prep, 1)
                vec.wait_ge(prep_t, 1)
                nc.vector.tensor_copy(w_outT[:], wide[2][:, 0:C]).then_inc(prep, 1)
                vec.wait_ge(prep, 2)
                for half in range(2):
                    rows = slice(half * C, (half + 1) * C)
                    last = nc.vector.tensor_scalar(mix[rows, rows], w_outT[rows, :], v[rows, :], None, ALU.mult)
                last.then_inc(prep, 1)
                vec.wait_ge(prep_t, 2)
                nc.vector.tensor_tensor(const[:], wide[2][:, 0:C], b_out[:], ALU.add).then_inc(prep, 1)
                vec.wait_ge(prep, 4)
                for j in range(J):
                    vec.wait_ge(out_banked, j + 1)
                    nc.vector.tensor_tensor(R[:, 2 * NT * j:2 * NT * (j + 1), :],
                                            wide[j % 2][:].rearrange("p (r c) -> p r c", c=C),
                                            const[:].unsqueeze(1).to_broadcast([P, 2 * NT, C]), ALU.add).then_inc(out_taken, 1)
                vec.wait_ge(out_taken, J)
                residual_norm(vec, norm_a, norm_v, norm_steps, R[:], T[:], stats, 0)

            @block.tensor
            def _(pe):
                pe.wait_ge(loaded, 16 * 6)
                nc.tensor.transpose(wide[2][:, 0:C], w_out[:].rearrange("o h f -> o (h f)"),
                                    ident[0:C, 0:C]).then_inc(prep_t, 1)
                pe.wait_ge(prep, 2)
                nc.tensor.matmul(wide[2][:, 0:C], b_nl[:].to_broadcast([C, P]), w_outT[0:C, :], start=True,
                                 stop=True).then_inc(prep_t, 1)
                transpose_adj(pe, AT, banks, at_banked, at_copied)
                pe.wait_ge(at_copied, 2 * NT)
                for j in range(J):
                    if j >= 2:
                        pe.wait_ge(ax_copied, j - 1)
                    for half in range(2):
                        cols = slice(half * HALF, (half + 1) * HALF)
                        for mt in range(NT):
                            last = nc.tensor.matmul(wide[j % 2][:, cols], Xj[:, j, mt, :], AT[:, mt, cols],
                                                    start=(mt == 0), stop=(mt == NT - 1))
                    last.then_inc(ax_banked, 1)
                pe.wait_ge(ax_copied, J)
                pe.wait_ge(prep, 3)
                for j in range(J):
                    if j >= 2:
                        pe.wait_ge(out_taken, j - 1)
                    for t in range(NT):
                        cols = slice(t * P, (t + 1) * P)
                        last = nc.tensor.matmul(wide[j % 2][:, cols], AxT[:, j, cols], mix[:], start=True, stop=True)
                    last.then_inc(out_banked, 1)

        with ExitStack() as scope:
            stored = sem("stored")
            block = scope.enter_context(nc.Block())

            @block.sync
            def _(sp):
                for b in range(B):
                    sp.dma_start(out[b].rearrange("(t p) c -> p t c", p=P), X[:, b // 2, :, b % 2, :]).then_inc(stored, 16)
                sp.wait_ge(stored, 16 * B)


_INS = ["x", "adj", "L0_gnn_embedding", "L0_gnn_weight", "L0_gnn_bias", "L1_gnn_Wh", "L1_gnn_bh", "L1_gnn_W_out",
        "L1_gnn_b_out", "L2_gnn_H", "L2_gnn_W", "L2_gnn_W_ind", "L2_gnn_a_node", "L2_gnn_a_gn", "L2_gnn_a_ge",
        "L2_gnn_fcW", "L2_gnn_fcb", "L2_gnn_av", "L3_gnn_w_nl", "L3_gnn_b_nl", "L3_gnn_w_out", "L3_gnn_b_out"]


def kernel(**inputs):
    import numpy as _np
    import concourse.bacc as _bacc
    from concourse.bass_utils import run_bass_kernel_spmd as _run

    nc = _bacc.Bacc("TRN2", target_bir_lowering=False, num_devices=1)
    arrays, args = {}, []
    for name in _INS:
        a = _np.ascontiguousarray(inputs[name])
        arrays[f"in_{name}_dram"] = a
        args.append(nc.dram_tensor(f"in_{name}_dram", a.shape, mybir.dt.from_np(a.dtype), kind="ExternalInput").ap())
    args.append(nc.dram_tensor("out_dram", inputs["x"].shape, F32, kind="ExternalOutput").ap())
    adjacency_stack_kernel(nc, *args)
    return _run(nc, [arrays], core_ids=[0]).results[0]["out_dram"]
```

```python
from contextlib import ExitStack

import concourse.bass as bass
from concourse import mybir

ALU = mybir.AluOpType
ACT = mybir.ActivationFunctionType
AX = mybir.AxisListType
F32 = mybir.dt.float32
F32R = mybir.dt.float32r

P = 128
HALF = 512
EPS = 1e-5


class Pipeline:
    pass


def adjacency_stack_kernel(nc, x, adj, L0_embedding, L0_weight, L0_bias, L1_Wh, L1_bh, L1_W_out,
                           L1_b_out, L2_H, L2_W, L2_W_ind, L2_a_node, L2_a_gn, L2_a_ge, L2_fcW,
                           L2_fcb, L2_av, L3_w_nl, L3_b_nl, L3_w_out, L3_b_out, out):
    B, N, C = x.shape
    NT = N // P
    TOK = B * NT
    D = L0_embedding.shape[1]
    HEADS, _, HID = L1_Wh.shape
    E = L2_H.shape[1]
    assert N == 1024 and C == 64 and HID == P and E == 64 and B % 2 == 0

    keep = ExitStack()
    with keep:
        def sem(name):
            return keep.enter_context(nc.semaphore(name))

        def sb(name, shape, dtype=F32, scope=keep):
            return scope.enter_context(nc.sbuf_tensor(name, shape, dtype))

        def ps(name, shape, scope, dtype=F32):
            return scope.enter_context(nc.psum_tensor(name, shape, dtype))

        A = sb("A", [P, NT, N])
        J = B // 2
        X = sb("X", [P, J, NT, 2, C])
        Xrows = X[:].rearrange("p j t h c -> p (j t h) c")
        ident = sb("ident", [P, P])

        def row(b, t):
            return b // 2 * (2 * NT) + 2 * t + b % 2

        def transpose_adj(pe, AT, banks, at_banked, at_copied):
            for k in range(2 * NT):
                mt, half = k // 2, k % 2
                if k >= 2:
                    pe.wait_ge(at_copied, k - 1)
                for q in range(4):
                    last = nc.tensor.transpose(banks[k % 2][:, q * P:(q + 1) * P],
                                               A[:, half * 4 + q, mt * P:(mt + 1) * P], ident[:])
                last.then_inc(at_banked, 1)

        def copy_adj(engine, copy, AT, banks, at_banked, at_copied):
            for k in range(2 * NT):
                mt, half = k // 2, k % 2
                engine.wait_ge(at_banked, k + 1)
                copy(AT[:, mt, half * HALF:(half + 1) * HALF], banks[k % 2][:]).then_inc(at_copied, 1)

        def residual_norm(vec, act_sem, vec_sem, done, R, T, stats, base=0):
            Xf = Xrows
            mean, var, sd, rstd = (stats[:, k, :] for k in range(4))
            count = [base]

            def step(instruction):
                instruction.then_inc(done, 1)
                count[0] += 1
                vec.wait_ge(done, count[0])

            def wide(s):
                return s.unsqueeze(2).to_broadcast([P, TOK, C])

            step(nc.vector.tensor_tensor(R, R, Xf, ALU.add))
            step(nc.vector.tensor_reduce(mean, R, AX.X, ALU.add))
            step(nc.vector.tensor_scalar(mean, mean, 1.0 / C, None, ALU.mult))
            step(nc.vector.tensor_tensor(R, R, wide(mean), ALU.subtract))
            step(nc.vector.tensor_tensor(T, R, R, ALU.mult))
            step(nc.vector.tensor_reduce(var, T, AX.X, ALU.add))
            nc.vector.tensor_scalar(var, var, 1.0 / C, EPS, ALU.mult, ALU.add).then_inc(vec_sem, 1)
            vec.wait_ge(act_sem, 1)
            step(nc.vector.reciprocal(rstd, sd))
            step(nc.vector.tensor_tensor(Xf, R, wide(rstd), ALU.mult))
            return count[0]

        def norm_root(act, act_sem, vec_sem, stats):
            act.wait_ge(vec_sem, 1)
            nc.scalar.activation(stats[:, 2, :], stats[:, 1, :], ACT.Sqrt).then_inc(act_sem, 1)

        with ExitStack() as scope:
            AT = sb("AT0", [P, NT, N], F32, scope)
            XG = sb("XG", [P, TOK, 3 * C], F32, scope)
            tile_in = sb("tile_in", [P, 2, 4 * C], F32, scope)
            emb = sb("emb", [P, NT, D], F32, scope)
            embT = sb("embT", [D, N], F32, scope)
            biasw = sb("biasw", [D, C], F32, scope)
            Eb = sb("Eb", [P, NT, C], F32, scope)
            wa = sb("wa", [P, D * C], F32, scope)
            wb = sb("wb", [P, D * C], F32, scope)
            wa_hi = sb("wa_hi", [P, D * C], F32R, scope)
            wa_lo = sb("wa_lo", [P, D * C], F32R, scope)
            wb_both = sb("wb_both", [P, D * C], F32R, scope)
            gT = sb("gT", [P, 2, 2 * P], F32R, scope)
            gTl = sb("gTl", [P, 2, 2 * P], F32R, scope)
            g_whole = sb("g_whole", [P, 2, 2 * P], F32, scope)
            zE = sb("zE", [P, 4, D * C], F32, scope)
            R = sb("R0", [P, TOK, C], F32, scope)
            stats = sb("stats0", [P, 4, TOK], F32, scope)
            banks = [ps(f"l0_bank{k}", [P, HALF], scope) for k in range(2)]
            zps = [ps(f"l0_z{k}", [P, D * C], scope) for k in range(2)]

            loaded_adj, loaded_x, loaded_w = sem("l0_loaded_adj"), sem("l0_loaded_x"), sem("l0_loaded_w")
            ident_made = sem("ident_made")
            at_banked, at_copied = sem("l0_at_banked"), sem("l0_at_copied")
            x_placed, split_w = sem("l0_x_placed"), sem("l0_split_w")
            t_summed, t_copied = sem("l0_t_summed"), sem("l0_t_copied")
            emb_banked, emb_copied = sem("l0_emb_banked"), sem("l0_emb_copied")
            staged = sem("l0_staged")
            g_banked, g_hi, g_lo = sem("l0_g_banked"), sem("l0_g_hi"), sem("l0_g_lo")
            z_summed, z_weighted, z_reduced = sem("l0_z_summed"), sem("l0_z_weighted"), sem("l0_z_reduced")
            norm_v, norm_a, norm_steps = sem("l0_norm_v"), sem("l0_norm_a"), sem("l0_norm_steps")

            def bodies(engine, step):
                for k in range(4):
                    step(engine, 0, k, peeled=True)
                with engine.Fori(1, TOK // 4) as i:
                    for k in range(4):
                        step(engine, i, k)

            def pool_step(pool, i, k, peeled=False):
                g, u = 4 * i + k, k % 2
                if not peeled or k >= 2:
                    pool.wait_ge(g_banked, g - 1)
                nc.gpsimd.tensor_copy(tile_in[:, u, 0:3 * C].unsqueeze(1), XG[:, bass.ds(g, 1), :])
                nc.gpsimd.tensor_copy(tile_in[:, u, 3 * C:4 * C].unsqueeze(1),
                                      XG[:, bass.ds(g, 1), 2 * C:3 * C]).then_inc(staged, 1)
                if not peeled or k >= 1:
                    pool_split(pool, g, u)

            def pool_split(pool, g, u):
                pool.wait_ge(g_hi, g)
                nc.gpsimd.tensor_tensor(gTl[:, 1 - u, :], g_whole[:, 1 - u, :], gT[:, 1 - u, :],
                                        ALU.subtract).then_inc(g_lo, 1)

            def act_step(act, i, k, peeled=False):
                g, u = 4 * i + k, k % 2
                act.wait_ge(g_banked, g + 1)
                if not peeled or k >= 2:
                    act.wait_ge(z_summed, g - 1)
                nc.scalar.copy(gT[:, u, :], banks[u][:, 0:2 * P])
                nc.scalar.copy(g_whole[:, u, :], banks[u][:, 0:2 * P]).then_inc(g_hi, 1)

            def vec_step(vec, i, k, peeled=False):
                if not peeled or k >= 2:
                    vec_weigh(vec, 4 * i + k - 2, (k - 2) % 4, peeled)
                if not peeled or k >= 3:
                    vec_reduce(vec, 4 * i + k - 3, (k - 3) % 4)

            def vec_weigh(vec, tile, k, first=False):
                vec.wait_ge(z_summed, tile + 1)
                if not first:
                    vec.wait_ge(z_reduced, tile - 1)
                coef = emb[:, bass.ds(tile // 2 % NT, 1), :].rearrange("p a d -> p (a d)")
                nc.vector.tensor_tensor(zE[:, k, :].rearrange("p (d o) -> p d o", o=C),
                                        zps[k % 2][:].rearrange("p (d o) -> p d o", o=C),
                                        coef.unsqueeze(2).to_broadcast([P, D, C]), ALU.mult).then_inc(z_weighted, 1)

            def vec_reduce(vec, tile, k):
                vec.wait_ge(z_weighted, tile + 1)
                nc.vector.tensor_reduce(R[:, bass.ds(tile, 1), :].rearrange("p a c -> p (a c)"),
                                        zE[:, k, :].rearrange("p (d o) -> p o d", o=C), AX.X, ALU.add).then_inc(z_reduced, 1)

            def pe_step(pe, i, k, peeled=False):
                g, u = 4 * i + k, k % 2
                pe.wait_ge(staged, g + 1)
                if not peeled or k >= 2:
                    pe.wait_ge(g_hi, g - 1)
                for q in range(2):
                    last = nc.tensor.transpose(banks[u][:, q * P:(q + 1) * P], tile_in[:, u, q * P:(q + 1) * P], ident[:])
                last.then_inc(g_banked, 1)
                if not peeled or k >= 1:
                    pe_products(pe, g, u, peeled and k < 3)

            def pe_products(pe, g, u, first=False):
                v = 1 - u
                pe.wait_ge(g_lo, g)
                if not first:
                    pe.wait_ge(z_weighted, g - 2)
                for half in range(2):
                    cols = slice(half * HALF, (half + 1) * HALF)
                    terms = ((gT[:, v, 0:P], wa_hi[:, cols]), (gT[:, v, 0:P], wa_lo[:, cols]),
                             (gTl[:, v, 0:P], wa_hi[:, cols]), (gT[:, v, P:2 * P], wb_both[:, cols]),
                             (gTl[0:C, v, P:2 * P], wb_both[0:C, cols]))
                    for n, (stay, move) in enumerate(terms):
                        last = nc.tensor.matmul(zps[v][:, cols], stay, move, start=(n == 0), stop=(n == len(terms) - 1))
                last.then_inc(z_summed, 1)

            block = scope.enter_context(nc.Block())

            @block.sync
            def _(sp):
                for q in range(4):
                    sp.dma_start(A[:, 2 * q:2 * q + 2, :],
                                 adj.rearrange("(t p) m -> p t m", p=P)[:, 2 * q:2 * q + 2, :]).then_inc(loaded_adj, 16)
                for b in range(B):
                    sp.dma_start(X[:, b // 2, :, b % 2, :], x[b].rearrange("(t p) c -> p t c", p=P)).then_inc(loaded_x, 16)

            @block.gpsimd
            def _(pool):
                nc.gpsimd.memset(ident[:], 0.0).then_inc(ident_made, 1)
                pool.wait_ge(ident_made, 1)
                nc.gpsimd.affine_select(out=ident[:], in_=ident[:], compare_op=ALU.not_equal, fill=1.0, base=0,
                                        pattern=[[-1, P]], channel_multiplier=1).then_inc(ident_made, 1)
                pool.wait_ge(t_copied, 2 * NT)
                bodies(pool, pool_step)
                pool_split(pool, 4 * (TOK // 4), 0)

            @block.scalar
            def _(act):
                wk = L0_weight.rearrange("d k i o -> k i d o")
                for k in range(2):
                    act.dma_start(wa[k * C:(k + 1) * C, :].rearrange("p (d o) -> p d o", o=C), wk[k]).then_inc(loaded_w, 16)
                for k in range(2):
                    act.dma_start(wb[k * C:(k + 1) * C, :].rearrange("p (d o) -> p d o", o=C), wk[2]).then_inc(loaded_w, 16)
                act.dma_start(emb[:], L0_embedding.rearrange("(t p) d -> p t d", p=P)).then_inc(loaded_w, 16)
                act.dma_start(biasw[:], L0_bias).then_inc(loaded_w, 16)
                copy_adj(act, nc.scalar.copy, AT, banks, at_banked, at_copied)
                bodies(act, act_step)
                norm_root(act, norm_a, norm_v, stats)

            @block.vector
            def _(vec):
                vec.wait_ge(loaded_x, 16 * B)
                nc.vector.tensor_copy(XG[:, :, 0:C], Xrows).then_inc(x_placed, 1)
                vec.wait_ge(loaded_w, 16 * 6)
                nc.vector.tensor_copy(wa_hi[:], wa[:]).then_inc(split_w, 1)
                nc.vector.tensor_copy(wb_both[:], wb[:]).then_inc(split_w, 1)
                vec.wait_ge(split_w, 2)
                nc.vector.tensor_tensor(wa_lo[:], wa[:], wa_hi[:], ALU.subtract).then_inc(split_w, 1)
                nc.vector.tensor_tensor(wb_both[C:P, :], wb[C:P, :], wb_both[C:P, :], ALU.subtract).then_inc(split_w, 1)
                XGj = XG[:].rearrange("p (j t h) c -> p j t h c", j=J, h=2)
                for t in range(NT):
                    vec.wait_ge(t_summed, t + 1)
                    nc.vector.tensor_copy(XGj[:, :, t, :, C:2 * C],
                                          banks[t % 2][:].rearrange("p (j h c) -> p j h c", h=2, c=C)).then_inc(t_copied, 1)
                for t in range(NT):
                    vec.wait_ge(t_summed, NT + t + 1)
                    for h in range(2):
                        last = nc.vector.scalar_tensor_tensor(
                            out=XGj[:, :, t, h, 2 * C:3 * C],
                            in0=banks[t % 2][:].rearrange("p (j h c) -> p j h c", h=2, c=C)[:, :, h, :],
                            scalar=2.0, in1=XGj[:, :, t, h, 0:C], op0=ALU.mult, op1=ALU.subtract)
                    last.then_inc(t_copied, 1)
                vec.wait_ge(emb_banked, 1)
                nc.vector.tensor_copy(embT[:], zps[0][0:D, :]).then_inc(emb_copied, 1)
                vec.wait_ge(emb_banked, 2)
                nc.vector.tensor_copy(Eb[:].rearrange("p t c -> p (t c)"), zps[1][:, 0:HALF]).then_inc(emb_copied, 1)
                nc.vector.memset(stats[:, 0, :], 0.0).then_inc(z_reduced, 2)
                bodies(vec, vec_step)
                vec_weigh(vec, TOK - 2, 2)
                vec_reduce(vec, TOK - 3, 1)
                vec_weigh(vec, TOK - 1, 3)
                vec_reduce(vec, TOK - 2, 2)
                vec_reduce(vec, TOK - 1, 3)
                vec.wait_ge(z_reduced, TOK + 2)
                Rj = R[:].rearrange("p (j t h) c -> p j t h c", j=J, h=2)
                for j in range(J):
                    last = nc.vector.tensor_tensor(Rj[:, j], Rj[:, j], Eb[:].unsqueeze(2).to_broadcast([P, NT, 2, C]), ALU.add)
                last.then_inc(norm_steps, 1)
                vec.wait_ge(norm_steps, 1)
                residual_norm(vec, norm_a, norm_v, norm_steps, R[:], XG[:, :, 0:C], stats, 1)

            @block.tensor
            def _(pe):
                pe.wait_ge(ident_made, 2)
                pe.wait_ge(loaded_adj, 16 * 4)
                transpose_adj(pe, AT, banks, at_banked, at_copied)
                XGj = XG[:].rearrange("p (j t h) c -> p j t h c", j=J, h=2)
                pe.wait_ge(x_placed, 1)
                pe.wait_ge(at_copied, 2 * NT)
                for k in range(2):
                    if k == 1:
                        pe.wait_ge(t_copied, NT)
                    for t in range(NT):
                        if k * NT + t >= 2:
                            pe.wait_ge(t_copied, k * NT + t - 1)
                        for mt in range(NT):
                            last = nc.tensor.matmul(banks[t % 2][:].rearrange("p (j h c) -> p j h c", h=2, c=C),
                                                    AT[:, mt, t * P:(t + 1) * P],
                                                    XGj[:, :, mt, :, k * C:(k + 1) * C],
                                                    start=(mt == 0), stop=(mt == NT - 1))
                        last.then_inc(t_summed, 1)
                for t in range(NT):
                    last = nc.tensor.transpose(zps[0][0:D, t * P:(t + 1) * P], emb[:, t, :], ident[:])
                last.then_inc(emb_banked, 1)
                pe.wait_ge(emb_copied, 1)
                for t in range(NT):
                    last = nc.tensor.matmul(zps[1][:, t * C:(t + 1) * C], embT[:, t * P:(t + 1) * P], biasw[:],
                                            start=True, stop=True)
                last.then_inc(emb_banked, 1)
                pe.wait_ge(emb_copied, 2)
                pe.wait_ge(t_copied, 2 * NT)
                pe.wait_ge(split_w, 4)

                bodies(pe, pe_step)
                pe_products(pe, TOK, 0)

        MASKED = -1.0e16
        OFF = 8
        ZCUT = N // 2
        STEPS = 2 * NT

        def attention(scope, tag):
            s = {}
            for name in ("scored", "weighted", "zeroed", "zeroed_v", "shifted", "exped", "turned", "copied", "mixed",
                         "normed", "filled"):
                s[name] = sem(f"{tag}_{name}")
            work = sb(f"{tag}_work", [P, 4, N], F32, scope)
            masks = sb(f"{tag}_masks", [P, 2, N], F32, scope)
            weighted_start = sb(f"{tag}_weighted_start", [P, 1], F32, scope)
            filled = sb(f"{tag}_filled", [P, 1], F32, scope)
            copied_start = sb(f"{tag}_copied_start", [P, 1], F32, scope)
            probsT = sb(f"{tag}_probsT", [P, 2, NT, P], F32, scope)
            nmax = sb(f"{tag}_nmax", [P, 4], F32, scope)
            rowsum = sb(f"{tag}_rowsum", [P, 4], F32, scope)
            rinv = sb(f"{tag}_rinv", [P, 4], F32, scope)
            outs = sb(f"{tag}_outs", [P, 2, NT, C], F32, scope)
            Y2 = sb(f"{tag}_Y2", [P, 2, N], F32R, scope)
            Yl = sb(f"{tag}_Yl", [C, 2, N], F32R, scope)
            SX = sb(f"{tag}_SX", [P, B, N], F32R, scope)
            score_ps = [ps(f"{tag}_score_ps{k}", [P, N], scope) for k in range(2)]
            turn_ps = [ps(f"{tag}_turn_ps{k}", [P, HALF], scope) for k in range(2)]
            mix_ps = ps(f"{tag}_mix_ps", [P, HALF], scope)
            misc_ps = ps(f"{tag}_misc_ps", [P, HALF], scope)
            inv = sem(f"{tag}_inv")

            def init_pool(pool):
                nc.gpsimd.memset(weighted_start[:], 0.0).then_inc(s["weighted"], OFF)
                nc.gpsimd.memset(work[:], 0.0).then_inc(s["scored"], OFF)
                nc.gpsimd.memset(masks[:], 0.0).then_inc(s["zeroed"], OFF)
                nc.gpsimd.memset(nmax[:], 0.0).then_inc(s["shifted"], OFF - 1)
                nc.gpsimd.memset(rowsum[:], 1.0).then_inc(s["exped"], OFF - 2)
                nc.gpsimd.memset(probsT[:], 0.0).then_inc(s["turned"], 2 * (OFF - 3))
                nc.gpsimd.memset(copied_start[:], 0.0).then_inc(s["copied"], 2 * (OFF - 3))
                nc.gpsimd.memset(outs[:], 0.0).then_inc(s["mixed"], OFF - 4)
                nc.gpsimd.memset(filled[:], 0.0).then_inc(s["filled"], 1)

            def init_vec(vec):
                nc.vector.memset(mix_ps[:], 0.0).then_inc(s["normed"], OFF - 5)
                nc.vector.memset(rinv[:], 0.0).then_inc(s["zeroed_v"], OFF)

            def pe_scores(pe, g, t, u, x_cols):
                pe.wait_ge(s["weighted"], OFF + g - 1)
                rows = slice(t % NT * P, (t % NT + 1) * P)
                for half in range(2):
                    o = score_ps[t % 2][:, half * HALF:(half + 1) * HALF].unsqueeze(1)
                    nc.tensor.matmul(o, Y2[:, u, rows], SX[:, x_cols, half * HALF:(half + 1) * HALF], start=True, stop=False)
                    last = nc.tensor.matmul(o, Yl[:, u, rows], SX[0:C, x_cols, half * HALF:(half + 1) * HALF],
                                            start=False, stop=True)
                last.then_inc(s["scored"], 1)

            def pe_turn(pe, g, t):
                pe.wait_ge(s["exped"], OFF + g + 1)
                for half in range(2):
                    pe.wait_ge(s["copied"], 2 * (OFF + g) + half - 1)
                    for q in range(4):
                        k = half * 4 + q
                        last = nc.tensor.transpose(turn_ps[half][:, q * P:(q + 1) * P],
                                                   work[:, t % 4, k * P:(k + 1) * P], ident[:])
                    last.then_inc(s["turned"], 1)

            def pe_mix(pe, g, t, value):
                pe.wait_ge(s["copied"], 2 * (OFF + g + 1))
                pe.wait_ge(s["normed"], OFF + g)
                for mt in range(NT):
                    last = nc.tensor.matmul(mix_ps[:, (t % NT) * C:(t % NT + 1) * C].unsqueeze(1), probsT[:, t % 2, mt, :],
                                            value(mt), start=(mt == 0), stop=(mt == NT - 1))
                last.then_inc(s["mixed"], 1)

            def vec_weigh(vec, g, t):
                vec.wait_ge(s["scored"], OFF + g + 1)
                vec.wait_ge(s["turned"], 2 * (OFF + g - 3))
                nc.vector.tensor_tensor(work[:, t % 4, :], score_ps[t % 2][:], A[:, t % NT, :],
                                        ALU.mult).then_inc(s["weighted"], 1)

            def pool_zero(pool, g, t):
                pool.wait_ge(s["weighted"], OFF + g + 1)
                pool.wait_ge(s["shifted"], OFF + g - 1)
                pool.nop(nofuse=True)
                nc.gpsimd.tensor_scalar(masks[:, t % 2, ZCUT:N], work[:, t % 4, ZCUT:N], 0.0, MASKED,
                                        ALU.is_equal, ALU.mult).then_inc(s["zeroed"], 1)

            def vec_zero(vec, g, t):
                vec.wait_ge(s["weighted"], OFF + g + 1)
                nc.vector.tensor_scalar(masks[:, t % 2, 0:ZCUT], work[:, t % 4, 0:ZCUT], 0.0, MASKED,
                                        ALU.is_equal, ALU.mult).then_inc(s["zeroed_v"], 1)

            def vec_shift(vec, g, t):
                vec.wait_ge(s["zeroed"], OFF + g + 1)
                vec.wait_ge(s["zeroed_v"], OFF + g + 1)
                vec.wait_ge(s["exped"], OFF + g - 3)
                vec.nop(nofuse=True)
                nc.vector.tensor_tensor_reduce(work[:, t % 4, :], masks[:, t % 2, :], work[:, t % 4, :], -1.0, 3.0e38,
                                               ALU.add, ALU.min, nmax[:, t % 4:t % 4 + 1]).then_inc(s["shifted"], 1)

            def act_exp(act, g, t):
                act.wait_ge(s["shifted"], OFF + g + 1)
                act.wait_ge(s["normed"], OFF + g - 3)
                nc.scalar.activation(work[:, t % 4, :], work[:, t % 4, :], ACT.Exp, bias=nmax[:, t % 4:t % 4 + 1],
                                     scale=-1.0, accum_out=rowsum[:, t % 4:t % 4 + 1]).then_inc(s["exped"], 1)

            def act_copy(act, g, t):
                act.wait_ge(s["mixed"], OFF + g - 1)
                for half in range(2):
                    act.wait_ge(s["turned"], 2 * (OFF + g) + half + 1)
                    nc.scalar.copy(probsT[:, t % 2, half * 4:half * 4 + 4, :].rearrange("p a b -> p (a b)"),
                                   turn_ps[half][:]).then_inc(s["copied"], 1)

            def vec_norm(vec, g, t, out):
                vec.wait_ge(s["mixed"], OFF + g + 1)
                nc.vector.reciprocal(rinv[:, t % 4:t % 4 + 1], rowsum[:, t % 4:t % 4 + 1]).then_inc(inv, 1)
                vec.wait_ge(inv, 6 + g)
                nc.vector.tensor_scalar(out, mix_ps[:, (t % NT) * C:(t % NT + 1) * C].unsqueeze(1),
                                        rinv[:, t % 4:t % 4 + 1], None, ALU.mult).then_inc(s["normed"], 1)

            at = Pipeline()
            at.s, at.probsT, at.outs, at.Y2, at.Yl, at.SX = (
                s, probsT, outs, Y2, Yl, SX)
            at.turn_ps, at.mix_ps, at.misc_ps, at.score_ps, at.init_pool, at.init_vec = (
                turn_ps, mix_ps, misc_ps, score_ps, init_pool, init_vec)
            at.pe_scores, at.pe_turn, at.pe_mix, at.vec_weigh, at.pool_zero, at.vec_zero = (
                pe_scores, pe_turn, pe_mix, vec_weigh, pool_zero, vec_zero)
            at.vec_shift, at.act_exp, at.act_copy, at.vec_norm = (
                vec_shift, act_exp, act_copy, vec_norm)
            return at

        acc_scope = keep.enter_context(ExitStack())
        h2T = sb("h2T", [C, B + 1, N], F32, acc_scope)
        PAIRS = B * HEADS

        with ExitStack() as scope:
            at = attention(scope, "hid")
            s, Y2, Yl, SX, outs, misc_ps = at.s, at.Y2, at.Yl, at.SX, at.outs, at.misc_ps
            wh = sb("wh", [C, HEADS, HID], F32, scope)
            wo = sb("wo", [P, HEADS, C], F32, scope)
            bh = sb("bh", [P, HEADS], F32, scope)
            whT = sb("whT", [P, 2, 2, C], F32, scope)
            Mh = sb("Mh", [P, HEADS, 2, C], F32R, scope)
            Ml = sb("Ml", [C, HEADS, 2, C], F32R, scope)
            Mh_now = sb("Mh_now", [P, 2, 2 * C], F32R, scope)
            Ml_now = sb("Ml_now", [C, 2, 2 * C], F32R, scope)
            wh_now = sb("wh_now", [C, 2, HID], F32, scope)
            wo_now = sb("wo_now", [P, 2, C], F32, scope)
            onT = sb("onT", [C, HALF], F32, scope)
            biased = sb("biased", [P, HALF], F32, scope)
            leaky = sb("leaky", [P, HALF], F32, scope)
            loaded = sem("hid_loaded")
            w_turned, w_copied, m_made, m_split = (sem(f"hid_{n}") for n in ("w_turned", "w_copied", "m_made", "m_split"))
            sx_banked, sx_hi, sx_lo = sem("hid_sx_banked"), sem("hid_sx_hi"), sem("hid_sx_lo")
            misc_made, misc_read = sem("hid_misc_made"), sem("hid_misc_read")
            y_hi, biased_made, leaky_made = sem("hid_y_hi"), sem("hid_biased"), sem("hid_leaky")
            staged, cleared = sem("hid_staged"), sem("hid_cleared")

            def pe_small(pe, p, n, k):
                u, t = k // NT, k % NT
                pe.wait_ge(misc_read, OFF + n)
                if t < 2:
                    if t == 0:
                        pe.wait_ge(staged, p + 1)
                    b, cols = bass.ds((p + 1) // HEADS % B, 1), slice(t * HALF, (t + 1) * HALF)
                    o = misc_ps[:].unsqueeze(1)
                    nc.tensor.matmul(o, Mh_now[:, 1 - u, :], SX[:, b, cols], start=True, stop=False)
                    last = nc.tensor.matmul(o, Ml_now[:, 1 - u, :], SX[0:C, b, cols], start=False, stop=True)
                elif t % 3 == 2:
                    half = (t - 2) // 3
                    pe.wait_ge(s["normed"], OFF + NT * (p - 1) + 4 * half + 4)
                    pe.nop(nofuse=True)
                    for q in range(4):
                        last = nc.tensor.transpose(misc_ps[0:C, q * P:(q + 1) * P], outs[:, 1 - u, half * 4 + q, :],
                                                   ident[:])
                elif t % 3 == 0:
                    last = nc.tensor.matmul(misc_ps[:], wh_now[:, 1 - u, :], onT[:], start=True, stop=True)
                else:
                    pe.wait_ge(leaky_made, 2 * p + (t - 2) // 3 + 1)
                    last = nc.tensor.matmul(misc_ps[0:C, :], wo_now[:, 1 - u, :], leaky[:], start=True, stop=True)
                last.then_inc(misc_made, 1)

            def act_small(act, p, n, k):
                u, t = k // NT, k % NT
                if t < 2:
                    act.wait_ge(misc_made, OFF + n + 1)
                    nc.scalar.copy(Y2[:, 1 - u, t * HALF:(t + 1) * HALF], misc_ps[:]).then_inc(y_hi, 1)
                elif t % 3 == 2:
                    act.wait_ge(misc_made, OFF + n + 1)
                    nc.scalar.copy(onT[:], misc_ps[0:C, :]).then_inc(misc_read, 1)
                elif t % 3 == 0:
                    act.wait_ge(misc_made, OFF + n + 1)
                    act.nop(nofuse=True)
                    nc.scalar.activation(biased[:], misc_ps[:], ACT.Identity,
                                         bias=bh[:, bass.ds((p + HEADS - 1) % HEADS, 1)]).then_inc(misc_read, 1)

            def vec_small(vec, p, n, k):
                u, t = k // NT, k % NT
                if t < 2:
                    cols = slice(t * HALF, (t + 1) * HALF)
                    vec.wait_ge(y_hi, 2 * p + t + 3)
                    nc.vector.tensor_tensor(Yl[:, 1 - u, cols], misc_ps[0:C, :], Y2[0:C, 1 - u, cols],
                                            ALU.subtract).then_inc(misc_read, 1)
                elif t % 3 == 0:
                    vec.wait_ge(misc_read, OFF + n + 1)
                    nc.vector.scalar_tensor_tensor(out=leaky[:], in0=biased[:], scalar=0.01, in1=biased[:],
                                                   op0=ALU.mult, op1=ALU.max).then_inc(leaky_made, 1)
                elif t % 3 == 1:
                    half = (t - 2) // 3
                    acc = h2T[:, bass.ds((p + HEADS - 1) // HEADS, 1), half * HALF:(half + 1) * HALF]
                    vec.wait_ge(misc_made, OFF + n + 1)
                    nc.vector.tensor_tensor(acc, acc, misc_ps[0:C, :].unsqueeze(1), ALU.add).then_inc(misc_read, 1)

            def pe_step(pe, p, k, new=True):
                t = k % NT
                g = NT * p + t
                if new:
                    at.pe_scores(pe, g, k, k // NT, bass.ds(p // HEADS, 1))
                if new or t < 3:
                    at.pe_turn(pe, g - 3, (k - 3) % STEPS)
                if new or t < 4:
                    b = p // HEADS % B if t >= 4 else (p + PAIRS - 1) % PAIRS // HEADS
                    at.pe_mix(pe, g - 4, (k - 4) % STEPS, lambda mt: Xrows[:, bass.ds(row(b, mt), 1), :])
                if new or t < NT - 1:
                    pe_small(pe, p + (t + 1) // NT, g + 1, (k + 1) % STEPS)

            def act_step(act, p, k, new=True):
                t = k % NT
                g = NT * p + t
                act_small(act, p, g, k)
                if new or t < 2:
                    at.act_exp(act, g - 2, (k - 2) % STEPS)
                if new or t < 3:
                    at.act_copy(act, g - 3, (k - 3) % STEPS)

            def vec_step(vec, p, k, new=True):
                t = k % NT
                g = NT * p + t
                if new or t < 5:
                    at.vec_norm(vec, g - 5, (k - 5) % STEPS, outs[:, (k - 5) % STEPS // NT, (k - 5) % NT, :].unsqueeze(1))
                if new:
                    at.vec_weigh(vec, g, k)
                vec_small(vec, p, g, k)
                if new or t < 1:
                    at.vec_shift(vec, g - 1, (k - 1) % STEPS)
                if new:
                    at.vec_zero(vec, g, k)

            def stage_weights(pool, head_m, head_w, u):
                nc.gpsimd.tensor_copy(Mh_now[:, u, :].unsqueeze(1), Mh[:, head_m, :, :].rearrange("p a r c -> p a (r c)"))
                nc.gpsimd.tensor_copy(Ml_now[:, u, :].unsqueeze(1), Ml[:, head_m, :, :].rearrange("p a r c -> p a (r c)"))
                nc.gpsimd.tensor_copy(wh_now[:, u, :].unsqueeze(1), wh[:, head_w, :])
                return nc.gpsimd.tensor_copy(wo_now[:, u, :].unsqueeze(1), wo[:, head_w, :])

            block = scope.enter_context(nc.Block())

            @block.sync
            def _(sp):
                sp.dma_start(wh[:], L1_Wh.rearrange("h c d -> c h d")).then_inc(loaded, 16)
                sp.dma_start(wo[:], L1_W_out.rearrange("(h d) c -> d h c", d=HID)).then_inc(loaded, 16)
                sp.dma_start(bh[:], L1_bh.rearrange("h d -> d h"), allow_slow_non_contiguous=True).then_inc(loaded, 16)

            @block.gpsimd
            def _(pool):
                at.init_pool(pool)
                nc.gpsimd.memset(h2T[:], 0.0).then_inc(cleared, 1)
                pool.wait_ge(m_split, HEADS)
                stage_weights(pool, bass.ds(0, 1), bass.ds(0, 1), 0)
                stage_weights(pool, bass.ds(1, 1), bass.ds(HEADS - 1, 1), 1).then_inc(staged, 1)
                with pool.Fori(0, PAIRS // 2) as i:
                    for k in range(STEPS):
                        p = 2 * i + k // NT
                        at.pool_zero(pool, STEPS * i + k, k)
                        if k % NT == 2:
                            pool.wait_ge(misc_made, OFF + NT * p)
                            stage_weights(pool, bass.ds((p + 2) % HEADS, 1), bass.ds(p % HEADS, 1),
                                          k // NT).then_inc(staged, 1)

            @block.scalar
            def _(act):
                for b in range(B):
                    act.wait_ge(sx_banked, b + 1)
                    nc.scalar.copy(SX[0:C, b, :], at.score_ps[b % 2][0:C, :]).then_inc(sx_hi, 1)
                for half in range(2):
                    act.wait_ge(misc_made, OFF - 2 + half + 1)
                    nc.scalar.copy(Y2[:, 0, half * HALF:(half + 1) * HALF], misc_ps[:]).then_inc(y_hi, 1)
                act.wait_ge(s["filled"], 1)
                with act.Fori(0, PAIRS // 2) as i:
                    for k in range(STEPS):
                        act_step(act, 2 * i + k // NT, k)
                for t in range(NT):
                    act_step(act, PAIRS, t, new=False)

            @block.vector
            def _(vec):
                at.init_vec(vec)
                for h in range(HEADS):
                    vec.wait_ge(w_turned, h + 1)
                    nc.vector.tensor_copy(whT[:, h % 2, :, :], at.turn_ps[0][:, 0:C].unsqueeze(1).to_broadcast([P, 2, C])).then_inc(w_copied, 1)
                    vec.wait_ge(m_made, h + 1)
                    m = at.turn_ps[1][:, 0:C].unsqueeze(1).to_broadcast([P, 2, C])
                    nc.vector.tensor_copy(Mh[:, h, :, :], m).then_inc(w_copied, 1)
                    vec.wait_ge(w_copied, 2 * h + 2)
                    nc.vector.tensor_tensor(Ml[:, h, :, :], m[0:C], Mh[0:C, h, :, :], ALU.subtract).then_inc(m_split, 1)
                for b in range(B):
                    vec.wait_ge(sx_hi, b + 1)
                    nc.vector.tensor_tensor(SX[C:P, b, :], at.score_ps[b % 2][0:C, :], SX[0:C, b, :],
                                            ALU.subtract).then_inc(sx_lo, 1)
                for half in range(2):
                    cols = slice(half * HALF, (half + 1) * HALF)
                    vec.wait_ge(y_hi, half + 1)
                    nc.vector.tensor_tensor(Yl[:, 0, cols], misc_ps[0:C, :], Y2[0:C, 0, cols],
                                            ALU.subtract).then_inc(misc_read, OFF - 1 if half == 0 else 1)
                vec.wait_ge(cleared, 1)
                vec.wait_ge(s["filled"], 1)
                with vec.Fori(0, PAIRS // 2) as i:
                    for k in range(STEPS):
                        vec_step(vec, 2 * i + k // NT, k)
                for t in range(NT):
                    vec_step(vec, PAIRS, t, new=False)

            @block.tensor
            def _(pe):
                pe.wait_ge(loaded, 16 * 3)
                for h in range(HEADS):
                    if h:
                        pe.wait_ge(w_copied, 2 * h - 1)
                    nc.tensor.transpose(at.turn_ps[0][:, 0:C], wh[:, h, :], ident[0:C, 0:C]).then_inc(w_turned, 1)
                    pe.wait_ge(w_copied, 2 * h + 1)
                    if h:
                        pe.wait_ge(m_split, h)
                    nc.tensor.matmul(at.turn_ps[1][:, 0:C], whT[:, h % 2, :, :].rearrange("p r c -> p (r c)"),
                                     whT[:, h % 2, 0, :], start=True, stop=True).then_inc(m_made, 1)
                for b in range(B):
                    if b >= 2:
                        pe.wait_ge(sx_lo, b - 1)
                    for t in range(NT):
                        last = nc.tensor.transpose(at.score_ps[b % 2][0:C, t * P:(t + 1) * P], Xrows[:, row(b, t), :], ident[:])
                    last.then_inc(sx_banked, 1)
                pe.wait_ge(sx_lo, B)
                pe.wait_ge(staged, 1)
                for half in range(2):
                    if half:
                        pe.wait_ge(misc_read, OFF - 1)
                    cols = slice(half * HALF, (half + 1) * HALF)
                    nc.tensor.matmul(misc_ps[:], Mh_now[:, 0, :], SX[:, 0, cols], start=True, stop=False)
                    nc.tensor.matmul(misc_ps[:], Ml_now[:, 0, :], SX[0:C, 0, cols], start=False,
                                     stop=True).then_inc(misc_made, OFF - 1 if half == 0 else 1)
                pe.wait_ge(misc_read, OFF)
                pe.wait_ge(s["filled"], 1)
                pe_small(pe, 0, 0, 0)
                with pe.Fori(0, PAIRS // 2) as i:
                    for k in range(STEPS):
                        pe_step(pe, 2 * i + k // NT, k)
                for t in range(NT):
                    pe_step(pe, PAIRS, t, new=False)

        with ExitStack() as scope:
            at = attention(scope, "fin")
            s, Y2, Yl, SX = at.s, at.Y2, at.Yl, at.SX
            V = sb("V", [P, B, NT, C], F32, scope)
            b_out = sb("b_out", [P, C], F32, scope)
            stats = sb("stats1", [P, 4, TOK], F32, scope)
            R = sb("R1", [P, TOK, C], F32, scope)
            loaded = sem("fin_loaded")
            v_banked, v_copied, sx_hi, sx_lo = sem("fin_v_banked"), sem("fin_v_copied"), sem("fin_sx_hi"), sem("fin_sx_lo")
            y_made = sem("fin_y_made")
            norm_v, norm_a, norm_steps = sem("fin_norm_v"), sem("fin_norm_a"), sem("fin_norm_steps")
            TILES = B * NT

            def make_y(pair, u):
                b = bass.ds(pair, 1)
                nc.vector.tensor_copy(Y2[0:C, u, :].unsqueeze(1), SX[0:C, b, :])
                nc.vector.tensor_copy(Y2[C:P, u, :].unsqueeze(1), SX[0:C, b, :])
                return nc.vector.tensor_copy(Yl[:, u, :].unsqueeze(1), SX[C:P, b, :])

            def out_row(p, k):
                t = k % NT
                r = row(p, t - 5) if t >= 5 else row((p + B - 1) % B, t - 5 + NT)
                return R[:, bass.ds(r, 1), :]

            def pe_step(pe, p, k, new=True):
                t = k % NT
                g = NT * p + t
                if new:
                    if t == 0:
                        pe.wait_ge(y_made, p + 1)
                    at.pe_scores(pe, g, k, k // NT, bass.ds(p, 1))
                if new or t < 3:
                    at.pe_turn(pe, g - 3, (k - 3) % STEPS)
                if new or t < 4:
                    b = bass.ds(p if t >= 4 else (p + B - 1) % B, 1)
                    at.pe_mix(pe, g - 4, (k - 4) % STEPS, lambda mt: V[:, b, mt, :])

            def act_step(act, p, k, new=True):
                t = k % NT
                g = NT * p + t
                if new or t < 2:
                    at.act_exp(act, g - 2, (k - 2) % STEPS)
                if new or t < 3:
                    at.act_copy(act, g - 3, (k - 3) % STEPS)

            def vec_step(vec, p, k, new=True):
                t = k % NT
                g = NT * p + t
                if new or t < 5:
                    at.vec_norm(vec, g - 5, (k - 5) % STEPS, out_row(p, k))
                if new:
                    at.vec_weigh(vec, g, k)
                    if t == 1:
                        make_y((p + 1) % B, 1 - k // NT).then_inc(y_made, 1)
                if new or t < 1:
                    at.vec_shift(vec, g - 1, (k - 1) % STEPS)
                if new:
                    at.vec_zero(vec, g, k)

            block = scope.enter_context(nc.Block())

            @block.sync
            def _(sp):
                sp.dma_start(b_out[:], L1_b_out.unsqueeze(0).to_broadcast([P, C])).then_inc(loaded, 16)

            @block.gpsimd
            def _(pool):
                at.init_pool(pool)
                with pool.Fori(0, B // 2) as i:
                    for k in range(STEPS):
                        at.pool_zero(pool, STEPS * i + k, k)

            @block.scalar
            def _(act):
                for b in range(B):
                    nc.scalar.copy(SX[0:C, b, :], h2T[:, b + 1, :]).then_inc(sx_hi, 1)
                for b in range(B):
                    act.wait_ge(v_banked, b + 1)
                    nc.scalar.copy(V[:, b, :, :].rearrange("p t c -> p (t c)"), at.turn_ps[b % 2][:]).then_inc(v_copied, 1)
                act.wait_ge(s["filled"], 1)
                with act.Fori(0, B // 2) as i:
                    for k in range(STEPS):
                        act_step(act, 2 * i + k // NT, k)
                for t in range(NT):
                    act_step(act, B, t, new=False)
                norm_root(act, norm_a, norm_v, stats)

            @block.vector
            def _(vec):
                at.init_vec(vec)
                for b in range(B):
                    vec.wait_ge(sx_hi, b + 1)
                    nc.vector.tensor_tensor(SX[C:P, b, :], h2T[:, b + 1, :], SX[0:C, b, :], ALU.subtract).then_inc(sx_lo, 1)
                vec.wait_ge(sx_lo, 1)
                make_y(0, 0).then_inc(y_made, 1)
                vec.wait_ge(s["filled"], 1)
                with vec.Fori(0, B // 2) as i:
                    for k in range(STEPS):
                        vec_step(vec, 2 * i + k // NT, k)
                for t in range(NT):
                    vec_step(vec, B, t, new=False)
                vec.wait_ge(loaded, 16)
                vec.wait_ge(s["normed"], OFF + TILES)
                nc.vector.tensor_tensor(R[:], R[:], b_out[:].unsqueeze(1).to_broadcast([P, TOK, C]),
                                        ALU.add).then_inc(norm_steps, 1)
                vec.wait_ge(norm_steps, 1)
                nc.vector.scalar_tensor_tensor(out=R[:], in0=R[:], scalar=0.01, in1=R[:], op0=ALU.mult,
                                               op1=ALU.max).then_inc(norm_steps, 1)
                vec.wait_ge(norm_steps, 2)
                residual_norm(vec, norm_a, norm_v, norm_steps, R[:], V[:].rearrange("p b t c -> p (b t) c"), stats, 2)

            @block.tensor
            def _(pe):
                for b in range(B):
                    if b >= 2:
                        pe.wait_ge(v_copied, b - 1)
                    for t in range(NT):
                        last = nc.tensor.transpose(at.turn_ps[b % 2][:, t * C:(t + 1) * C],
                                                   h2T[:, b + 1, t * P:(t + 1) * P], ident[0:C, 0:C])
                    last.then_inc(v_banked, 1)
                pe.wait_ge(v_copied, B)
                pe.wait_ge(sx_lo, B)
                pe.wait_ge(s["filled"], 1)
                with pe.Fori(0, B // 2) as i:
                    for k in range(STEPS):
                        pe_step(pe, 2 * i + k // NT, k)
                for t in range(NT):
                    pe_step(pe, B, t, new=False)
        acc_scope.close()

        NEG = -1.0e9
        Xj = X[:].rearrange("p j t h c -> p j t (h c)")
        l2_scope = keep.enter_context(ExitStack())
        ind = sb("ind", [P, J, NT, 2, C], F32, l2_scope)
        agg = sb("agg", [P, J, E], F32, l2_scope)
        gate = sb("gate", [P, J, N], F32, l2_scope)
        coefT = sb("coefT", [P, J, N], F32, l2_scope)
        hT_hi = sb("hT_hi", [P, J, N], F32R, l2_scope)
        hT_lo = sb("hT_lo", [P, J, N], F32R, l2_scope)
        fcw = sb("fcw", [P, P], F32, l2_scope)
        fcb = sb("fcb", [P, 1], F32, l2_scope)
        av = sb("av", [P, 1], F32, l2_scope)
        late_scope = ExitStack()
        hT = sb("hT", [P, J, N], F32, late_scope)
        hN = sb("hN", [P, J, NT, P], F32, late_scope)

        def couple_blocks(m):
            return m[0:C, 0:C], m[C:P, C:P]

        with ExitStack() as scope:
            AT = sb("AT2", [P, NT, N], F32, scope)
            AxT, xT = gate, coefT
            w2 = sb("w2", [P, P], F32, scope)
            wi2 = sb("wi2", [P, P], F32, scope)
            deg = sb("deg", [P, NT], F32, scope)
            rdeg = sb("rdeg", [P, NT], F32, scope)
            banks = [ps(f"l2_bank{k}", [P, HALF], scope) for k in range(2)]
            wide = [ps(f"l2_wide{k}", [P, N], scope) for k in range(3)]
            zeroed, loaded = sem("l2_zeroed"), sem("l2_loaded")
            at_banked, at_copied = sem("l2_at_banked"), sem("l2_at_copied")
            xt_banked, xt_copied = sem("l2_xt_banked"), sem("l2_xt_copied")
            ax_banked, ax_copied = sem("l2_ax_banked"), sem("l2_ax_copied")
            h_banked, h_copied = sem("l2_h_banked"), sem("l2_h_copied")
            deg_made = sem("l2_deg_made")

            block = scope.enter_context(nc.Block())

            @block.sync
            def _(sp):
                sp.wait_ge(zeroed, 2)
                for m, w in ((w2, L2_W), (wi2, L2_W_ind)):
                    for part in couple_blocks(m):
                        sp.dma_start(part, w).then_inc(loaded, 16)
                for half in range(2):
                    sp.dma_start(fcw[half * C:(half + 1) * C, :], L2_fcW).then_inc(loaded, 16)
                sp.dma_start(fcb[:], L2_fcb.unsqueeze(1)).then_inc(loaded, 16)
                sp.dma_start(av[:], L2_av.unsqueeze(1)).then_inc(loaded, 16)
                sp.wait_ge(loaded, 16 * 8)

            @block.gpsimd
            def _(pool):
                nc.gpsimd.memset(w2[:], 0.0).then_inc(zeroed, 1)
                nc.gpsimd.memset(wi2[:], 0.0).then_inc(zeroed, 1)

            @block.scalar
            def _(act):
                copy_adj(act, nc.scalar.copy, AT, banks, at_banked, at_copied)
                for j in range(J):
                    act.wait_ge(ax_banked, j + 1)
                    nc.scalar.copy(AxT[:, j, :], wide[j % 2][:]).then_inc(ax_copied, 1)
                for j in range(J):
                    act.wait_ge(h_banked, 3 * j + 2)
                    nc.scalar.copy(hN[:, j, :, :].rearrange("p t f -> p (t f)"), wide[1][:]).then_inc(h_copied, 1)

            @block.vector
            def _(vec):
                nc.vector.tensor_reduce(deg[:], A[:], AX.X, ALU.add).then_inc(deg_made, 1)
                vec.wait_ge(deg_made, 1)
                nc.vector.tensor_scalar(deg[:], deg[:], 1.0, None, ALU.max).then_inc(deg_made, 1)
                vec.wait_ge(deg_made, 2)
                nc.vector.reciprocal(rdeg[:], deg[:]).then_inc(deg_made, 1)
                for j in range(J):
                    vec.wait_ge(xt_banked, j + 1)
                    nc.vector.tensor_copy(xT[:, j, :], wide[2][:]).then_inc(xt_copied, 1)
                vec.wait_ge(deg_made, 3)
                for j in range(J):
                    vec.wait_ge(h_banked, 3 * j + 1)
                    nc.vector.tensor_copy(hT[:, j, :], wide[0][:]).then_inc(h_copied, 1)
                    vec.wait_ge(h_banked, 3 * j + 3)
                    nc.vector.tensor_tensor(ind[:, j].rearrange("p t h f -> p t (h f)"),
                                            wide[2][:].rearrange("p (t k) -> p t k", k=P),
                                            rdeg[:].unsqueeze(2).to_broadcast([P, NT, P]), ALU.mult).then_inc(h_copied, 1)

            @block.tensor
            def _(pe):
                for j in range(J):
                    if j:
                        pe.wait_ge(xt_copied, j)
                    for t in range(NT):
                        last = nc.tensor.transpose(wide[2][:, t * P:(t + 1) * P], Xj[:, j, t, :], ident[:])
                    last.then_inc(xt_banked, 1)
                transpose_adj(pe, AT, banks, at_banked, at_copied)
                pe.wait_ge(at_copied, 2 * NT)
                for j in range(J):
                    if j >= 2:
                        pe.wait_ge(ax_copied, j - 1)
                    for half in range(2):
                        cols = slice(half * HALF, (half + 1) * HALF)
                        for mt in range(NT):
                            last = nc.tensor.matmul(wide[j % 2][:, cols], Xj[:, j, mt, :], AT[:, mt, cols],
                                                    start=(mt == 0), stop=(mt == NT - 1))
                    last.then_inc(ax_banked, 1)
                pe.wait_ge(ax_copied, J)
                pe.wait_ge(xt_copied, J)
                pe.wait_ge(loaded, 16 * 8)
                for j in range(J):
                    if j:
                        pe.wait_ge(h_copied, 3 * j)
                    for half in range(2):
                        cols = slice(half * HALF, (half + 1) * HALF)
                        last = nc.tensor.matmul(wide[0][:, cols], w2[:], xT[:, j, cols], start=True, stop=True)
                    last.then_inc(h_banked, 1)
                    for out_ps, left, right in ((wide[1], xT, w2), (wide[2], AxT, wi2)):
                        for t in range(NT):
                            cols = slice(t * P, (t + 1) * P)
                            last = nc.tensor.matmul(out_ps[:, cols], left[:, j, cols], right[:], start=True, stop=True)
                        last.then_inc(h_banked, 1)

        with ExitStack() as scope:
            incid = sb("incid", [P, NT, 2, E], F32, scope)
            member = sb("member", [P, NT, E], F32, scope)
            outside = sb("outside", [P, NT, E], F32, scope)
            memberT = sb("memberT", [P, N], F32, scope)
            outsideT = sb("outsideT", [P, N], F32, scope)
            a_rows = sb("a_rows", [P, 3], F32, scope)
            a_node2 = sb("a_node2", [P, P], F32, scope)
            a_gn2 = sb("a_gn2", [P, P], F32, scope)
            a_ge = sb("a_ge", [P, C], F32, scope)
            sc = sb("sc", [P, N], F32, scope)
            lk = sb("lk", [P, N], F32, scope)
            alpha = sb("alpha", [P, N], F32, scope)
            alphaT = sb("alphaT", [P, NT, P], F32, scope)
            cells = hN[:].rearrange("p j t k -> p (j t k)").rearrange("p (t b e) -> p t b e", t=NT, b=B)
            small = sb("small", [P, 24], F32, scope)
            elu_a = sb("elu_a", [P, J, E], F32, scope)
            heT = sb("heT", [C, J * P], F32, scope)
            th = sb("th", [P, J * P], F32, scope)
            se = sb("se", [P, B, E], F32, scope)
            cmax = sb("cmax", [P, NT * B], F32, scope)
            crcp = sb("crcp", [P, NT * B], F32, scope)
            banks = [ps(f"l2b_bank{k}", [P, HALF], scope) for k in range(2)]
            wide = [ps(f"l2b_wide{k}", [P, N], scope) for k in range(3)]
            zeroed, loaded = sem("l2b_zeroed"), sem("l2b_loaded")
            (s_made, s_copied, s_turned, s_turn_copied, s_agg, s_exped, s_gn, s_gexp, v_steps, s_h, s_he, s_he_c, s_fc,
             s_tanh, s_se, s_elu, s_ct, s_ct_copied, s_cexp, s_ht) = (
                sem(f"l2b_{n}") for n in ("scored", "score_copied", "turned", "turn_copied", "agg_made", "exped",
                                          "gn_made", "gate_exped", "vector_steps", "incid_turned", "he_turned",
                                          "he_copied", "fc_made", "tanhed", "se_made", "elu_exped", "coef_turned",
                                          "coef_copied", "coef_exped", "logits_ready"))
            block = scope.enter_context(nc.Block())

            @block.sync
            def _(sp):
                Hn = L2_H.rearrange("(t p) e -> p t e", p=P)
                for half in range(2):
                    sp.dma_start(incid[:, :, half, :], Hn).then_inc(loaded, 16)
                for k, v in enumerate((L2_a_node, L2_a_gn)):
                    for half in range(2):
                        sp.dma_start(a_rows[half * C:(half + 1) * C, k:k + 1], v.unsqueeze(1)).then_inc(loaded, 16)
                sp.dma_start(a_ge[:], L2_a_ge.unsqueeze(0).to_broadcast([P, C])).then_inc(loaded, 16)
                sp.wait_ge(loaded, 16 * 7)

            @block.gpsimd
            def _(pool):
                nc.gpsimd.memset(a_node2[:], 0.0).then_inc(zeroed, 1)
                nc.gpsimd.memset(a_gn2[:], 0.0).then_inc(zeroed, 1)

            @block.scalar
            def _(act):
                for j in range(J):
                    act.wait_ge(s_made, j + 1)
                    if j:
                        act.wait_ge(s_ht, 2 * j)
                    nc.scalar.copy(sc[:], wide[0][:]).then_inc(s_copied, 1)
                    act.wait_ge(s_ht, 2 * j + 2)
                    nc.scalar.activation(alpha[:], lk[:], ACT.Exp, bias=small[:, j:j + 1], scale=-1.0,
                                         accum_out=small[:, 4 + j:5 + j]).then_inc(s_exped, 1)
                    act.wait_ge(s_turned, j + 1)
                    nc.scalar.copy(alphaT[:].rearrange("p t k -> p (t k)"), wide[1][:]).then_inc(s_turn_copied, 1)
                    act.wait_ge(s_gn, j + 1)
                    act.wait_ge(v_steps, 100 * (j + 1))
                    nc.scalar.activation(gate[:, j, :], wide[2][:], ACT.Exp, bias=small[:, 12 + j:13 + j],
                                         scale=-1.0).then_inc(s_gexp, 1)
                act.wait_ge(v_steps, 400)
                nc.scalar.activation(elu_a[:], agg[:], ACT.Exp).then_inc(s_elu, 1)
                act.wait_ge(s_fc, 1)
                nc.scalar.activation(th[:], banks[1][:], ACT.Tanh, bias=fcb[:]).then_inc(s_tanh, 1)
                act.wait_ge(s_h, 2)
                nc.scalar.activation(cells, cells, ACT.Exp).then_inc(s_cexp, 1)
                for j in range(J):
                    act.wait_ge(s_ct, j + 1)
                    nc.scalar.copy(coefT[:, j, :], wide[j % 2][:]).then_inc(s_ct_copied, 1)

            @block.vector
            def _(vec):
                count = [0]

                def step(instruction, to=None):
                    n = 1 if to is None else to - count[0]
                    instruction.then_inc(v_steps, n)
                    count[0] += n
                    vec.wait_ge(v_steps, count[0])

                vec.wait_ge(loaded, 16 * 7)
                vec.wait_ge(zeroed, 2)
                for m, k in ((a_node2, 0), (a_gn2, 1)):
                    for half in range(2):
                        rows = slice(half * C, (half + 1) * C)
                        last = nc.vector.tensor_copy(m[rows, rows], a_rows[rows, k:k + 1].to_broadcast([C, C]))
                step(last, 3)
                step(nc.vector.tensor_scalar(member[:], incid[:, :, 0, :], 0.0, None, ALU.is_gt))
                step(nc.vector.tensor_scalar(outside[:], member[:], -NEG, NEG, ALU.mult, ALU.add))
                vec.wait_ge(s_h, 1)
                step(nc.vector.tensor_scalar(memberT[:], wide[0][:], 0.0, None, ALU.is_gt))
                step(nc.vector.tensor_scalar(outsideT[:], memberT[:], -NEG, NEG, ALU.mult, ALU.add), 10)
                for j in range(J):
                    vec.wait_ge(s_copied, j + 1)
                    if j:
                        vec.wait_ge(s_exped, j)
                    nc.vector.scalar_tensor_tensor(out=lk[:], in0=sc[:], scalar=0.2, in1=sc[:], op0=ALU.mult,
                                                   op1=ALU.max).then_inc(s_ht, 1)
                    vec.wait_ge(s_ht, 2 * j + 1)
                    step(nc.vector.tensor_tensor(lk[:], lk[:], memberT[:], ALU.mult))
                    nc.vector.tensor_tensor_reduce(lk[:], lk[:], outsideT[:], -1.0, 3.0e38, ALU.add, ALU.min,
                                                   small[:, j:j + 1]).then_inc(s_ht, 1)
                    step(nc.vector.tensor_copy(hT_hi[:, j, :], hT[:, j, :]))
                    step(nc.vector.tensor_tensor(hT_lo[:, j, :], hT[:, j, :], hT_hi[:, j, :], ALU.subtract))
                    vec.wait_ge(s_exped, j + 1)
                    step(nc.vector.reciprocal(small[:, 8 + j:9 + j], small[:, 4 + j:5 + j]))
                    vec.wait_ge(s_agg, j + 1)
                    for half in range(2):
                        rows = slice(half * C, (half + 1) * C)
                        last = nc.vector.tensor_scalar(agg[rows, j, :], banks[0][rows, rows], small[rows, 8 + j:9 + j],
                                                       None, ALU.mult)
                    step(last)
                    step(nc.vector.tensor_tensor_reduce(elu_a[:, j, :], agg[:, j, :], a_ge[:], -1.0, 0.0, ALU.mult,
                                                        ALU.add, small[:, 12 + j:13 + j]), 100 * (j + 1))
                    vec.wait_ge(s_gexp, j + 1)
                    step(nc.vector.tensor_scalar(gate[:, j, :], gate[:, j, :], 1.0, None, ALU.add))
                    step(nc.vector.reciprocal(gate[:, j, :], gate[:, j, :]))
                vec.wait_ge(s_elu, 1)
                step(nc.vector.tensor_scalar(elu_a[:], elu_a[:], 1.0, -1.0, ALU.min, ALU.add))
                step(nc.vector.tensor_tensor(elu_a[:], elu_a[:], agg[:], ALU.max), 500)
                vec.wait_ge(s_he, 1)
                nc.vector.tensor_copy(heT[:], banks[0][0:C, :]).then_inc(s_he_c, 1)
                vec.wait_ge(s_se, 1)
                step(nc.vector.tensor_copy(se[:].rearrange("p b e -> p (b e)"), banks[0][:]))
                shape = [P, NT, B, E]
                step(nc.vector.tensor_tensor(cells, se[:].unsqueeze(1).to_broadcast(shape),
                                             member[:].unsqueeze(2).to_broadcast(shape), ALU.mult))
                step(nc.vector.tensor_tensor(cells, cells, outside[:].unsqueeze(2).to_broadcast(shape), ALU.add))
                flat = cells.rearrange("p t b e -> p (t b) e")
                step(nc.vector.tensor_reduce(cmax[:], flat, AX.X, ALU.max))
                nc.vector.tensor_tensor(flat, flat, cmax[:].unsqueeze(2).to_broadcast([P, NT * B, E]),
                                        ALU.subtract).then_inc(s_h, 1)
                vec.wait_ge(s_cexp, 1)
                step(nc.vector.tensor_reduce(cmax[:], flat, AX.X, ALU.add))
                step(nc.vector.reciprocal(crcp[:], cmax[:]))
                step(nc.vector.tensor_tensor(flat, flat, crcp[:].unsqueeze(2).to_broadcast([P, NT * B, E]), ALU.mult), 600)

            @block.tensor
            def _(pe):
                pe.wait_ge(loaded, 16 * 7)
                for t in range(NT):
                    last = nc.tensor.transpose(wide[0][:, t * P:(t + 1) * P], incid[:, t, :, :].rearrange("p h e -> p (h e)"),
                                               ident[:])
                last.then_inc(s_h, 1)
                pe.wait_ge(v_steps, 10)
                for j in range(J):
                    if j:
                        pe.wait_ge(s_copied, j)
                    for half in range(2):
                        cols = slice(half * HALF, (half + 1) * HALF)
                        last = nc.tensor.matmul(wide[0][:, cols], a_node2[:], hT[:, j, cols], start=True, stop=True)
                    last.then_inc(s_made, 1)
                    if j:
                        pe.wait_ge(s_gexp, j)
                    for half in range(2):
                        cols = slice(half * HALF, (half + 1) * HALF)
                        last = nc.tensor.matmul(wide[2][:, cols], a_gn2[:], hT[:, j, cols], start=True, stop=True)
                    last.then_inc(s_gn, 1)
                    pe.wait_ge(s_exped, j + 1)
                    for t in range(NT):
                        last = nc.tensor.transpose(wide[1][:, t * P:(t + 1) * P], alpha[:, t * P:(t + 1) * P], ident[:])
                    last.then_inc(s_turned, 1)
                    pe.wait_ge(s_turn_copied, j + 1)
                    if j:
                        pe.wait_ge(v_steps, 100 * j)
                    for t in range(NT):
                        last = nc.tensor.matmul(banks[0][:, 0:P], alphaT[:, t, :], hN[:, j, t, :], start=(t == 0),
                                                stop=(t == NT - 1))
                    last.then_inc(s_agg, 1)
                pe.wait_ge(v_steps, 500)
                for j in range(J):
                    last = nc.tensor.transpose(banks[0][0:C, j * P:(j + 1) * P], elu_a[:, j, :], ident[:])
                last.then_inc(s_he, 1)
                pe.wait_ge(s_he_c, 1)
                nc.tensor.matmul(banks[1][:], fcw[0:C, :], heT[:], start=True, stop=True).then_inc(s_fc, 1)
                pe.wait_ge(s_tanh, 1)
                nc.tensor.matmul(banks[0][:], av[:].to_broadcast([P, P]), th[:], start=True, stop=True).then_inc(s_se, 1)
                pe.wait_ge(v_steps, 600)
                for j in range(J):
                    if j >= 2:
                        pe.wait_ge(s_ct_copied, j - 1)
                    for t in range(NT):
                        last = nc.tensor.transpose(wide[j % 2][:, t * P:(t + 1) * P],
                                                   cells[:, t, 2 * j:2 * j + 2, :].rearrange("p b e -> p (b e)"), ident[:])
                    last.then_inc(s_ct, 1)
        late_scope.close()

        GF = 8
        GROUPS = J * C // GF
        PER = C // GF
        BODY = 2 * GF
        LAST_LAG = 5
        gT = sb("gT_acc", [P, J, N], F32, l2_scope)
        with ExitStack() as scope:
            agg1 = sb("agg1", [P, J, E], F32, scope)
            ident_r = sb("ident_r", [P, 2, C], F32R, scope)
            window = sb("window", [P, 2 * P], F32, scope)
            pick = sb("pick", [P, 2, GF, 2, E], F32R, scope)
            place = sb("place", [P, 2, P + GF], F32, scope)
            a_now = sb("a_now", [P, 2, GF], F32, scope)
            a1_now = sb("a1_now", [P, 2, GF], F32, scope)
            u_buf = sb("u_buf", [P, 2, N], F32, scope)
            ex = sb("ex", [P, 2, N], F32, scope)
            lin = sb("lin", [P, 2, N], F32, scope)
            el = sb("el", [P, 4, N], F32, scope)
            spread = [ps(f"spread{k}", [P, N], scope) for k in range(2)]
            summed = [ps(f"summed{k}", [P, N], scope) for k in range(2)]
            cleared, made, ready, staged, picked = (sem(f"l2c_{n}") for n in ("cleared", "made", "ready", "staged", "picked"))
            s_spread, s_u, s_ex, s_lin, s_el, s_weighted, s_summed, s_added = (
                sem(f"l2c_{n}") for n in ("spread", "u", "ex", "lin", "elu", "weighted", "summed", "added"))
            block = scope.enter_context(nc.Block())

            def at_lag(i, k, lag):
                group = BODY // GF * i + (k - lag) // GF
                return BODY * i + k - lag, (k - lag) % BODY, group, group // PER

            def stage_group(pool, group, par):
                nc.gpsimd.tensor_copy(place[:, par, :], window[:, bass.ds(P - GF - group % PER * GF, P + GF)])
                cols = bass.ds(group * GF, GF)
                nc.gpsimd.tensor_copy(a_now[:, par, :], agg[:].rearrange("p j f -> p (j f)")[:, cols])
                nc.gpsimd.tensor_copy(a1_now[:, par, :], agg1[:].rearrange("p j f -> p (j f)")[:, cols]).then_inc(staged, 1)

            def pick_group(vec, group, par):
                cols = ident_r[:, :, bass.ds(group % PER * GF, GF)].rearrange("p h f -> p f h")
                nc.vector.tensor_copy(pick[:, par], cols.unsqueeze(3).to_broadcast([P, GF, 2, E])).then_inc(picked, 1)

            def add_group(vec, group, par):
                acc = gT[:, bass.ds(group // PER, 1), :]
                nc.vector.tensor_tensor(acc, acc, summed[par][:].unsqueeze(1), ALU.add).then_inc(s_added, 1)

            def pe_step(pe, i, k, peeled=False, spreads=True):
                if spreads:
                    q, kk, group, couple = at_lag(i, k, 0)
                    par, f = kk // GF, kk % GF
                    if f == 0:
                        pe.wait_ge(picked, group + 1)
                    if not peeled or q >= 2:
                        pe.wait_ge(s_u, q - 1)
                    stay = pick[:, par, f].rearrange("p h e -> p (h e)")
                    for half in range(2):
                        cols = slice(half * HALF, (half + 1) * HALF)
                        o = spread[k % 2][:, cols].unsqueeze(1)
                        nc.tensor.matmul(o, stay, hT_hi[:, bass.ds(couple, 1), cols], start=True, stop=False)
                        last = nc.tensor.matmul(o, stay, hT_lo[:, bass.ds(couple, 1), cols], start=False, stop=True)
                    last.then_inc(s_spread, 1)
                q, kk, group, couple = at_lag(i, k, 5)
                if not peeled or q >= 0:
                    par, f = kk // GF, kk % GF
                    pe.wait_ge(s_weighted, q + 1)
                    if f == 0:
                        pe.wait_ge(staged, group + 1)
                        if not peeled or group >= 2:
                            pe.wait_ge(s_added, group - 1)
                    for half in range(2):
                        cols = slice(half * HALF, (half + 1) * HALF)
                        last = nc.tensor.matmul(summed[par][:, cols], place[:, par, GF - 1 - f:GF - 1 - f + P],
                                                el[:, kk % 4, cols], start=(f == 0), stop=(f == GF - 1))
                    last.then_inc(s_summed, 1)

            def vec_step(vec, i, k, peeled=False, until=LAST_LAG):
                q, kk, group, couple = at_lag(i, k, 1)
                if (not peeled or q >= 0) and until > 0:
                    par, f = kk // GF, kk % GF
                    if f == 0:
                        vec.wait_ge(staged, group + 1)
                    vec.wait_ge(s_spread, q + 1)
                    if not peeled or q >= 2:
                        vec.wait_ge(s_lin, q - 1)
                    nc.vector.scalar_tensor_tensor(out=u_buf[:, kk % 2, :].unsqueeze(1), in0=spread[kk % 2][:].unsqueeze(1),
                                                   scalar=a_now[:, par, f:f + 1], in1=gate[:, bass.ds(couple, 1), :],
                                                   op0=ALU.subtract, op1=ALU.mult).then_inc(s_u, 1)
                q, kk, group, couple = at_lag(i, k, 3)
                if not peeled or q >= 0:
                    vec.wait_ge(s_lin, q + 1)
                    if not peeled or q >= 4:
                        vec.wait_ge(s_summed, q - 3)
                    nc.vector.scalar_tensor_tensor(out=el[:, kk % 4, :], in0=ex[:, kk % 2, :], scalar=1.0,
                                                   in1=lin[:, kk % 2, :], op0=ALU.min, op1=ALU.max).then_inc(s_el, 1)
                if until < LAST_LAG:
                    return
                q, kk, group, couple = at_lag(i, k, 0)
                if kk % GF == 3:
                    vec.wait_ge(s_spread, GF * group + 1)
                    pick_group(vec, (group + 1) % GROUPS, 1 - kk // GF)
                if kk % GF == 7 and (not peeled or group >= 1):
                    vec.wait_ge(s_summed, GF * group)
                    add_group(vec, group - 1, 1 - kk // GF)

            def act_step(act, i, k, peeled=False):
                q, kk, group, couple = at_lag(i, k, 2)
                if not peeled or q >= 0:
                    bias = slice(kk % GF, kk % GF + 1)
                    act.wait_ge(s_u, q + 1)
                    if not peeled or q >= 2:
                        act.wait_ge(s_el, q - 1)
                    nc.scalar.activation(ex[:, kk % 2, :], u_buf[:, kk % 2, :], ACT.Exp,
                                         bias=a_now[:, kk // GF, bias]).then_inc(s_ex, 1)
                    nc.scalar.activation(lin[:, kk % 2, :], u_buf[:, kk % 2, :], ACT.Identity,
                                         bias=a1_now[:, kk // GF, bias]).then_inc(s_lin, 1)

            def pool_step(pool, i, k, peeled=False, stages=True):
                q, kk, group, couple = at_lag(i, k, 4)
                if not peeled or q >= 0:
                    pool.wait_ge(s_el, q + 1)
                    pool.nop(nofuse=True)
                    nc.gpsimd.tensor_tensor(el[:, kk % 4, :].unsqueeze(1), el[:, kk % 4, :].unsqueeze(1),
                                            coefT[:, bass.ds(couple, 1), :], ALU.mult).then_inc(s_weighted, 1)
                q, kk, group, couple = at_lag(i, k, 0)
                if stages and kk % GF == 6:
                    if not peeled or group >= 1:
                        pool.wait_ge(s_summed, GF * group)
                    stage_group(pool, (group + 1) % GROUPS, 1 - kk // GF)

            def bodies(engine, step):
                for k in range(BODY):
                    step(engine, 0, k, peeled=True)
                with engine.Fori(1, GROUPS * GF // BODY) as i:
                    for k in range(BODY):
                        step(engine, i, k)

            END = GROUPS * GF // BODY

            @block.gpsimd
            def _(pool):
                nc.gpsimd.memset(gT[:], 0.0).then_inc(cleared, 1)
                nc.gpsimd.memset(window[:], 0.0).then_inc(cleared, 1)
                pool.wait_ge(cleared, 2)
                nc.gpsimd.memset(window[0:C, P - 1:P], 1.0)
                nc.gpsimd.memset(window[C:P, P + C - 1:P + C], 1.0).then_inc(made, 1)
                pool.wait_ge(ready, 2)
                pool.wait_ge(made, 1)
                stage_group(pool, 0, 0)
                bodies(pool, pool_step)
                for k in range(4):
                    pool_step(pool, END, k, stages=False)

            @block.scalar
            def _(act):
                act.wait_ge(staged, 1)
                bodies(act, act_step)
                for k in range(2):
                    act_step(act, END, k)

            @block.vector
            def _(vec):
                nc.vector.tensor_scalar(agg1[:], agg[:], 1.0, None, ALU.add).then_inc(ready, 1)
                nc.vector.tensor_copy(ident_r[:].rearrange("p h f -> p (h f)"), ident[:]).then_inc(ready, 1)
                vec.wait_ge(ready, 2)
                pick_group(vec, 0, 0)
                vec.wait_ge(cleared, 2)
                bodies(vec, vec_step)
                for k in range(3):
                    vec_step(vec, END, k, until=1 - k)
                vec.wait_ge(s_summed, GROUPS * GF)
                add_group(vec, GROUPS - 1, 1)

            @block.tensor
            def _(pe):
                bodies(pe, pe_step)
                for k in range(5):
                    pe_step(pe, END, k, spreads=False)

        with ExitStack() as scope:
            indT = sb("indT", [P, J, N], F32, scope)
            gN = sb("gN", [P, J, NT, 2, C], F32, scope)
            th = [sb(f"th{k}", [P, HALF], F32, scope) for k in range(2)]
            score = sb("score", [P, 2, TOK], F32, scope)
            smax = sb("smax", [P, TOK], F32, scope)
            stats = sb("stats2", [P, 4, TOK], F32, scope)
            R = sb("R2", [P, TOK, C], F32, scope)
            wide = [ps(f"l2d_wide{k}", [P, N], scope) for k in range(2)]
            fc = [ps(f"l2d_fc{k}", [P, HALF], scope) for k in range(2)]
            score_ps = ps("l2d_score", [P, 2 * TOK], scope)
            shifted, turned, copied, fc_made, tanhed, scored, exped, steps = (
                sem(f"l2d_{n}") for n in ("shifted", "turned", "copied", "fc_made", "tanhed", "scored", "exped", "steps"))
            norm_v, norm_a = sem("l2d_norm_v"), sem("l2d_norm_a")
            block = scope.enter_context(nc.Block())
            slabs = [(kind, j, h, half) for kind in range(2) for j in range(J) for h in range(2) for half in range(2)]

            @block.scalar
            def _(act):
                for n in range(len(slabs)):
                    act.wait_ge(fc_made, n + 1)
                    if n >= 2:
                        act.wait_ge(scored, n - 1)
                    nc.scalar.activation(th[n % 2][:], fc[n % 2][:], ACT.Tanh, bias=fcb[:]).then_inc(tanhed, 1)
                act.wait_ge(steps, 4)
                nc.scalar.activation(score[:], score[:], ACT.Exp).then_inc(exped, 1)
                norm_root(act, norm_a, norm_v, stats)

            @block.vector
            def _(vec):
                nc.vector.tensor_scalar(gT[:], gT[:], -1.0, None, ALU.add).then_inc(shifted, 1)
                for n in range(2 * J):
                    j = n // 2
                    vec.wait_ge(turned, n + 1)
                    if n % 2 == 0:
                        nc.vector.tensor_copy(indT[:, j, :], wide[0][:]).then_inc(copied, 1)
                    else:
                        nc.vector.tensor_copy(gN[:, j].rearrange("p t h f -> p (t h f)"), wide[1][:]).then_inc(copied, 1)
                vec.wait_ge(scored, len(slabs))
                flat = score[:].rearrange("p k r -> p (k r)")
                count = [0]

                def step(instruction):
                    instruction.then_inc(steps, 1)
                    count[0] += 1
                    vec.wait_ge(steps, count[0])

                step(nc.vector.tensor_copy(flat, score_ps[:]))
                step(nc.vector.tensor_tensor(smax[:], score[:, 0], score[:, 1], ALU.max))
                step(nc.vector.tensor_tensor(score[:, 0], score[:, 0], smax[:], ALU.subtract))
                step(nc.vector.tensor_tensor(score[:, 1], score[:, 1], smax[:], ALU.subtract))
                vec.wait_ge(exped, 1)
                step(nc.vector.tensor_tensor(smax[:], score[:, 0], score[:, 1], ALU.add))
                step(nc.vector.reciprocal(smax[:], smax[:]))
                step(nc.vector.tensor_tensor(score[:, 0], score[:, 0], smax[:], ALU.mult))
                step(nc.vector.tensor_tensor(score[:, 1], score[:, 1], smax[:], ALU.mult))
                wide_shape = [P, TOK, C]
                weight = [score[:, k].unsqueeze(2).to_broadcast(wide_shape) for k in range(2)]
                indf, gf = (m[:].rearrange("p j t h c -> p (j t h) c") for m in (ind, gN))
                step(nc.vector.tensor_tensor(R[:], indf, weight[0], ALU.mult))
                step(nc.vector.tensor_tensor(gf, gf, weight[1], ALU.mult))
                step(nc.vector.tensor_tensor(R[:], R[:], gf, ALU.add))
                residual_norm(vec, norm_a, norm_v, steps, R[:], gf, stats, count[0])

            @block.tensor
            def _(pe):
                indj = ind[:].rearrange("p j t h f -> p j t (h f)")
                for j in range(J):
                    if j:
                        pe.wait_ge(copied, 2 * j)
                    for t in range(NT):
                        last = nc.tensor.transpose(wide[0][:, t * P:(t + 1) * P], indj[:, j, t, :], ident[:])
                    last.then_inc(turned, 1)
                    if j == 0:
                        pe.wait_ge(shifted, 1)
                    for t in range(NT):
                        last = nc.tensor.transpose(wide[1][:, t * P:(t + 1) * P], gT[:, j, t * P:(t + 1) * P], ident[:])
                    last.then_inc(turned, 1)
                pe.wait_ge(copied, 2 * J)

                def scores_of(n):
                    kind, j, h, half = slabs[n]
                    pe.wait_ge(tanhed, n + 1)
                    for q in range(4):
                        col = kind * TOK + row(2 * j + h, 4 * half + q)
                        last = nc.tensor.matmul(score_ps[:, col:col + 1], th[n % 2][:, q * P:(q + 1) * P], av[:],
                                                start=True, stop=True)
                    last.then_inc(scored, 1)

                for n, (kind, j, h, half) in enumerate(slabs):
                    if n >= 2:
                        pe.wait_ge(tanhed, n - 1)
                    rows, cols = slice(h * C, (h + 1) * C), slice(half * HALF, (half + 1) * HALF)
                    nc.tensor.matmul(fc[n % 2][:], fcw[rows, :], (gT if kind else indT)[rows, j, cols], start=True,
                                     stop=True).then_inc(fc_made, 1)
                    if n:
                        scores_of(n - 1)
                scores_of(len(slabs) - 1)
        l2_scope.close()

        with ExitStack() as scope:
            AT = sb("AT3", [P, NT, N], F32, scope)
            AxT = sb("AxT3", [P, J, N], F32, scope)
            w_nl = sb("w_nl", [P, 2], F32, scope)
            b_nl = sb("b_nl", [C, 1], F32, scope)
            w_out = sb("w_out", [C, 2, C], F32, scope)
            w_outT = sb("w_outT", [P, C], F32, scope)
            mix = sb("mix", [P, P], F32, scope)
            b_out = sb("b_out3", [P, C], F32, scope)
            v = sb("v", [P, 1], F32, scope)
            const = sb("const", [P, C], F32, scope)
            R = sb("R3", [P, TOK, C], F32, scope)
            T = sb("T3", [P, TOK, C], F32, scope)
            stats = sb("stats3", [P, 4, TOK], F32, scope)
            banks = [ps(f"l3_bank{k}", [P, HALF], scope) for k in range(2)]
            wide = [ps(f"l3_wide{k}", [P, N], scope) for k in range(3)]
            loaded, cleared, prep, prep_t = sem("l3_loaded"), sem("l3_cleared"), sem("l3_prep"), sem("l3_prep_t")
            at_banked, at_copied = sem("l3_at_banked"), sem("l3_at_copied")
            ax_banked, ax_copied = sem("l3_ax_banked"), sem("l3_ax_copied")
            out_banked, out_taken = sem("l3_out_banked"), sem("l3_out_taken")
            norm_v, norm_a, norm_steps = sem("l3_norm_v"), sem("l3_norm_a"), sem("l3_norm_steps")
            block = scope.enter_context(nc.Block())

            @block.sync
            def _(sp):
                for half in range(2):
                    sp.dma_start(w_nl[half * C:(half + 1) * C, :], L3_w_nl).then_inc(loaded, 16)
                    sp.dma_start(w_out[:, half, :], L3_w_out).then_inc(loaded, 16)
                sp.dma_start(b_nl[:], L3_b_nl.unsqueeze(1)).then_inc(loaded, 16)
                sp.dma_start(b_out[:], L3_b_out.unsqueeze(0).to_broadcast([P, C])).then_inc(loaded, 16)
                sp.wait_ge(loaded, 16 * 6)

            @block.gpsimd
            def _(pool):
                nc.gpsimd.memset(mix[:], 0.0).then_inc(cleared, 1)

            @block.scalar
            def _(act):
                copy_adj(act, nc.scalar.copy, AT, banks, at_banked, at_copied)
                for j in range(J):
                    act.wait_ge(ax_banked, j + 1)
                    nc.scalar.copy(AxT[:, j, :], wide[j % 2][:]).then_inc(ax_copied, 1)
                norm_root(act, norm_a, norm_v, stats)

            @block.vector
            def _(vec):
                vec.wait_ge(loaded, 16 * 6)
                vec.wait_ge(cleared, 1)
                nc.vector.tensor_scalar(v[:], w_nl[:, 0:1], w_nl[:, 1:2], 1.0 / 2.0 ** 0.5, ALU.add,
                                        ALU.mult).then_inc(prep, 1)
                vec.wait_ge(prep_t, 1)
                nc.vector.tensor_copy(w_outT[:], wide[2][:, 0:C]).then_inc(prep, 1)
                vec.wait_ge(prep, 2)
                for half in range(2):
                    rows = slice(half * C, (half + 1) * C)
                    last = nc.vector.tensor_scalar(mix[rows, rows], w_outT[rows, :], v[rows, :], None, ALU.mult)
                last.then_inc(prep, 1)
                vec.wait_ge(prep_t, 2)
                nc.vector.tensor_tensor(const[:], wide[2][:, 0:C], b_out[:], ALU.add).then_inc(prep, 1)
                vec.wait_ge(prep, 4)
                for j in range(J):
                    vec.wait_ge(out_banked, j + 1)
                    nc.vector.tensor_tensor(R[:, 2 * NT * j:2 * NT * (j + 1), :],
                                            wide[j % 2][:].rearrange("p (r c) -> p r c", c=C),
                                            const[:].unsqueeze(1).to_broadcast([P, 2 * NT, C]), ALU.add).then_inc(out_taken, 1)
                vec.wait_ge(out_taken, J)
                residual_norm(vec, norm_a, norm_v, norm_steps, R[:], T[:], stats, 0)

            @block.tensor
            def _(pe):
                pe.wait_ge(loaded, 16 * 6)
                nc.tensor.transpose(wide[2][:, 0:C], w_out[:].rearrange("o h f -> o (h f)"),
                                    ident[0:C, 0:C]).then_inc(prep_t, 1)
                pe.wait_ge(prep, 2)
                nc.tensor.matmul(wide[2][:, 0:C], b_nl[:].to_broadcast([C, P]), w_outT[0:C, :], start=True,
                                 stop=True).then_inc(prep_t, 1)
                transpose_adj(pe, AT, banks, at_banked, at_copied)
                pe.wait_ge(at_copied, 2 * NT)
                for j in range(J):
                    if j >= 2:
                        pe.wait_ge(ax_copied, j - 1)
                    for half in range(2):
                        cols = slice(half * HALF, (half + 1) * HALF)
                        for mt in range(NT):
                            last = nc.tensor.matmul(wide[j % 2][:, cols], Xj[:, j, mt, :], AT[:, mt, cols],
                                                    start=(mt == 0), stop=(mt == NT - 1))
                    last.then_inc(ax_banked, 1)
                pe.wait_ge(ax_copied, J)
                pe.wait_ge(prep, 3)
                for j in range(J):
                    if j >= 2:
                        pe.wait_ge(out_taken, j - 1)
                    for t in range(NT):
                        cols = slice(t * P, (t + 1) * P)
                        last = nc.tensor.matmul(wide[j % 2][:, cols], AxT[:, j, cols], mix[:], start=True, stop=True)
                    last.then_inc(out_banked, 1)

        with ExitStack() as scope:
            stored = sem("stored")
            block = scope.enter_context(nc.Block())

            @block.sync
            def _(sp):
                for b in range(B):
                    sp.dma_start(out[b].rearrange("(t p) c -> p t c", p=P), X[:, b // 2, :, b % 2, :]).then_inc(stored, 16)
                sp.wait_ge(stored, 16 * B)


_INS = ["x", "adj", "L0_gnn_embedding", "L0_gnn_weight", "L0_gnn_bias", "L1_gnn_Wh", "L1_gnn_bh", "L1_gnn_W_out",
        "L1_gnn_b_out", "L2_gnn_H", "L2_gnn_W", "L2_gnn_W_ind", "L2_gnn_a_node", "L2_gnn_a_gn", "L2_gnn_a_ge",
        "L2_gnn_fcW", "L2_gnn_fcb", "L2_gnn_av", "L3_gnn_w_nl", "L3_gnn_b_nl", "L3_gnn_w_out", "L3_gnn_b_out"]


def kernel(**inputs):
    import numpy as _np
    import concourse.bacc as _bacc
    from concourse.bass_utils import run_bass_kernel_spmd as _run

    nc = _bacc.Bacc("TRN2", target_bir_lowering=False, num_devices=1)
    arrays, args = {}, []
    for name in _INS:
        a = _np.ascontiguousarray(inputs[name])
        arrays[f"in_{name}_dram"] = a
        args.append(nc.dram_tensor(f"in_{name}_dram", a.shape, mybir.dt.from_np(a.dtype), kind="ExternalInput").ap())
    args.append(nc.dram_tensor("out_dram", inputs["x"].shape, F32, kind="ExternalOutput").ap())
    adjacency_stack_kernel(nc, *args)
    return _run(nc, [arrays], core_ids=[0]).results[0]["out_dram"]
```

```python
from contextlib import ExitStack

import concourse.bass as bass
from concourse import mybir

ALU = mybir.AluOpType
ACT = mybir.ActivationFunctionType
AX = mybir.AxisListType
F32 = mybir.dt.float32
F32R = mybir.dt.float32r

P = 128
HALF = 512
EPS = 1e-5


class Pipeline:
    pass


def adjacency_stack_kernel(nc, x, adj, L0_embedding, L0_weight, L0_bias, L1_Wh, L1_bh, L1_W_out,
                           L1_b_out, L2_H, L2_W, L2_W_ind, L2_a_node, L2_a_gn, L2_a_ge, L2_fcW,
                           L2_fcb, L2_av, L3_w_nl, L3_b_nl, L3_w_out, L3_b_out, out):
    B, N, C = x.shape
    NT = N // P
    TOK = B * NT
    D = L0_embedding.shape[1]
    HEADS, _, HID = L1_Wh.shape
    E = L2_H.shape[1]
    assert N == 1024 and C == 64 and HID == P and E == 64 and B % 2 == 0

    keep = ExitStack()
    with keep:
        def sem(name):
            return keep.enter_context(nc.semaphore(name))

        def sb(name, shape, dtype=F32, scope=keep):
            return scope.enter_context(nc.sbuf_tensor(name, shape, dtype))

        def ps(name, shape, scope, dtype=F32):
            return scope.enter_context(nc.psum_tensor(name, shape, dtype))

        A = sb("A", [P, NT, N])
        J = B // 2
        X = sb("X", [P, J, NT, 2, C])
        Xrows = X[:].rearrange("p j t h c -> p (j t h) c")
        ident = sb("ident", [P, P])

        def row(b, t):
            return b // 2 * (2 * NT) + 2 * t + b % 2

        def transpose_adj(pe, AT, banks, at_banked, at_copied, steps=range(2 * NT)):
            for k in steps:
                mt, half = k // 2, k % 2
                if k >= 2:
                    pe.wait_ge(at_copied, k - 1)
                for q in range(4):
                    last = nc.tensor.transpose(banks[k % 2][:, q * P:(q + 1) * P],
                                               A[:, half * 4 + q, mt * P:(mt + 1) * P], ident[:])
                last.then_inc(at_banked, 1)

        def copy_adj(engine, copy, AT, banks, at_banked, at_copied):
            for k in range(2 * NT):
                mt, half = k // 2, k % 2
                engine.wait_ge(at_banked, k + 1)
                copy(AT[:, mt, half * HALF:(half + 1) * HALF], banks[k % 2][:]).then_inc(at_copied, 1)

        added, meaned, centred, squared, varied, rooted, inverted, normed = (
            sem(f"norm_{n}") for n in ("added", "meaned", "centred", "squared", "varied", "rooted", "inverted", "done"))

        def residual_norm(layer, R, T, scope):
            BASE = J * layer
            stats = sb(f"norm_stats{layer}", [P, 3, TOK], F32, scope)
            mean, sd, rstd = (stats[:, k, :] for k in range(3))
            def rows(c):
                return slice(2 * NT * c, 2 * NT * (c + 1))

            def wide(s, c):
                return s[:, rows(c)].unsqueeze(2).to_broadcast([P, 2 * NT, C])

            def vec_mean(vec, c):
                r = rows(c)
                nc.vector.tensor_tensor(R[:, r], R[:, r], Xrows[:, r], ALU.add).then_inc(added, 1)
                vec.wait_ge(added, BASE + c + 1)
                nc.vector.tensor_reduce(mean[:, r], R[:, r], AX.X, ALU.add).then_inc(meaned, 1)
                vec.wait_ge(meaned, 2 * (BASE + c) + 1)
                nc.vector.tensor_scalar(mean[:, r], mean[:, r], 1.0 / C, None, ALU.mult).then_inc(meaned, 1)

            def vec_variance(vec, c):
                r = rows(c)
                vec.wait_ge(squared, BASE + c + 1)
                nc.vector.tensor_reduce(sd[:, r], T[:, r], AX.X, ALU.add).then_inc(varied, 1)
                vec.wait_ge(varied, 2 * (BASE + c) + 1)
                nc.vector.tensor_scalar(sd[:, r], sd[:, r], 1.0 / C, EPS, ALU.mult, ALU.add).then_inc(varied, 1)

            def vec_scale(vec, c):
                r = rows(c)
                vec.wait_ge(rooted, BASE + c + 1)
                nc.vector.reciprocal(rstd[:, r], sd[:, r]).then_inc(inverted, 1)
                vec.wait_ge(inverted, BASE + c + 1)
                nc.vector.tensor_tensor(Xrows[:, r], R[:, r], wide(rstd, c), ALU.mult).then_inc(normed, 1)

            def vec_part(vec, before):
                for c in range(J + 2):
                    if c < J:
                        before(c)
                        vec_mean(vec, c)
                    if 1 <= c <= J:
                        vec_variance(vec, c - 1)
                    if c >= 2:
                        vec_scale(vec, c - 2)

            def pool_part(pool, c):
                pool.wait_ge(meaned, 2 * (BASE + c) + 2)
                nc.gpsimd.tensor_tensor(R[:, rows(c)], R[:, rows(c)], wide(mean, c), ALU.subtract).then_inc(centred, 1)

            def act_step(act, c):
                if c < J:
                    act.wait_ge(centred, BASE + c + 1)
                    nc.scalar.activation(T[:, rows(c)], R[:, rows(c)], ACT.Square).then_inc(squared, 1)
                if c >= 1:
                    act.wait_ge(varied, 2 * (BASE + c))
                    nc.scalar.activation(sd[:, rows(c - 1)], sd[:, rows(c - 1)], ACT.Sqrt).then_inc(rooted, 1)

            def act_part(act):
                for c in range(J + 1):
                    act_step(act, c)

            norm = Pipeline()
            norm.vec_part, norm.pool_part, norm.act_part, norm.rows = vec_part, pool_part, act_part, rows
            norm.done, norm.BASE, norm.act_step = normed, BASE, act_step
            return norm

        with ExitStack() as scope:
            AT = sb("AT0", [P, NT, N], F32, scope)
            XG = sb("XG", [P, TOK, 3 * C], F32, scope)
            tile_in = sb("tile_in", [P, 2, 4 * C], F32, scope)
            emb = sb("emb", [P, NT, D], F32, scope)
            embT = sb("embT", [D, N], F32, scope)
            biasw = sb("biasw", [D, C], F32, scope)
            Eb = sb("Eb", [P, NT, C], F32, scope)
            wa = sb("wa", [P, D * C], F32, scope)
            wb = sb("wb", [P, D * C], F32, scope)
            wa_hi = sb("wa_hi", [P, D * C], F32R, scope)
            wa_lo = sb("wa_lo", [P, D * C], F32R, scope)
            wb_both = sb("wb_both", [P, D * C], F32R, scope)
            gT = sb("gT", [P, 2, 2 * P], F32R, scope)
            gTl = sb("gTl", [P, 2, 2 * P], F32R, scope)
            g_whole = sb("g_whole", [P, 2, 2 * P], F32, scope)
            zE = sb("zE", [P, 4, D * C], F32, scope)
            R = sb("R0", [P, TOK, C], F32, scope)
            norm = residual_norm(0, R[:], XG[:, :, 0:C], scope)
            banks = [ps(f"l0_bank{k}", [P, HALF], scope) for k in range(2)]
            zps = [ps(f"l0_z{k}", [P, D * C], scope) for k in range(2)]

            loaded_adj, loaded_x, loaded_w = sem("l0_loaded_adj"), sem("l0_loaded_x"), sem("l0_loaded_w")
            ident_made = sem("ident_made")
            at_banked, at_copied = sem("l0_at_banked"), sem("l0_at_copied")
            x_placed, split_w = sem("l0_x_placed"), sem("l0_split_w")
            t_summed, t_copied = sem("l0_t_summed"), sem("l0_t_copied")
            emb_banked, emb_copied = sem("l0_emb_banked"), sem("l0_emb_copied")
            staged = sem("l0_staged")
            g_banked, g_hi, g_lo = sem("l0_g_banked"), sem("l0_g_hi"), sem("l0_g_lo")
            z_summed, z_weighted, z_reduced = sem("l0_z_summed"), sem("l0_z_weighted"), sem("l0_z_reduced")
            based = sem("l0_based")

            def bodies(engine, step):
                for k in range(4):
                    step(engine, 0, k, peeled=True)
                with engine.Fori(1, TOK // 4) as i:
                    for k in range(4):
                        step(engine, i, k)

            def pool_step(pool, i, k, peeled=False):
                g, u = 4 * i + k, k % 2
                if not peeled or k >= 2:
                    pool.wait_ge(g_banked, g - 1)
                nc.gpsimd.tensor_copy(tile_in[:, u, 0:3 * C].unsqueeze(1), XG[:, bass.ds(g, 1), :])
                nc.gpsimd.tensor_copy(tile_in[:, u, 3 * C:4 * C].unsqueeze(1),
                                      XG[:, bass.ds(g, 1), 2 * C:3 * C]).then_inc(staged, 1)
                if not peeled or k >= 1:
                    pool_split(pool, g, u)

            def pool_split(pool, g, u):
                pool.wait_ge(g_hi, g)
                nc.gpsimd.tensor_tensor(gTl[:, 1 - u, :], g_whole[:, 1 - u, :], gT[:, 1 - u, :],
                                        ALU.subtract).then_inc(g_lo, 1)

            def act_step(act, i, k, peeled=False):
                g, u = 4 * i + k, k % 2
                act.wait_ge(g_banked, g + 1)
                if not peeled or k >= 2:
                    act.wait_ge(z_summed, g - 1)
                nc.scalar.copy(gT[:, u, :], banks[u][:, 0:2 * P])
                nc.scalar.copy(g_whole[:, u, :], banks[u][:, 0:2 * P]).then_inc(g_hi, 1)

            def vec_step(vec, i, k, peeled=False):
                if not peeled or k >= 2:
                    vec_weigh(vec, 4 * i + k - 2, (k - 2) % 4, peeled)
                if not peeled or k >= 3:
                    vec_reduce(vec, 4 * i + k - 3, (k - 3) % 4)

            def vec_weigh(vec, tile, k, first=False):
                vec.wait_ge(z_summed, tile + 1)
                if not first:
                    vec.wait_ge(z_reduced, tile - 1)
                coef = emb[:, bass.ds(tile // 2 % NT, 1), :].rearrange("p a d -> p (a d)")
                nc.vector.tensor_tensor(zE[:, k, :].rearrange("p (d o) -> p d o", o=C),
                                        zps[k % 2][:].rearrange("p (d o) -> p d o", o=C),
                                        coef.unsqueeze(2).to_broadcast([P, D, C]), ALU.mult).then_inc(z_weighted, 1)

            def vec_reduce(vec, tile, k):
                vec.wait_ge(z_weighted, tile + 1)
                nc.vector.tensor_reduce(R[:, bass.ds(tile, 1), :].rearrange("p a c -> p (a c)"),
                                        zE[:, k, :].rearrange("p (d o) -> p o d", o=C), AX.X, ALU.add).then_inc(z_reduced, 1)

            def pe_step(pe, i, k, peeled=False):
                g, u = 4 * i + k, k % 2
                pe.wait_ge(staged, g + 1)
                if not peeled or k >= 2:
                    pe.wait_ge(g_hi, g - 1)
                for q in range(2):
                    last = nc.tensor.transpose(banks[u][:, q * P:(q + 1) * P], tile_in[:, u, q * P:(q + 1) * P], ident[:])
                last.then_inc(g_banked, 1)
                if not peeled or k >= 1:
                    pe_products(pe, g, u, peeled and k < 3)

            def pe_products(pe, g, u, first=False):
                v = 1 - u
                pe.wait_ge(g_lo, g)
                if not first:
                    pe.wait_ge(z_weighted, g - 2)
                for half in range(2):
                    cols = slice(half * HALF, (half + 1) * HALF)
                    terms = ((gT[:, v, 0:P], wa_hi[:, cols]), (gT[:, v, 0:P], wa_lo[:, cols]),
                             (gTl[:, v, 0:P], wa_hi[:, cols]), (gT[:, v, P:2 * P], wb_both[:, cols]),
                             (gTl[0:C, v, P:2 * P], wb_both[0:C, cols]))
                    for n, (stay, move) in enumerate(terms):
                        last = nc.tensor.matmul(zps[v][:, cols], stay, move, start=(n == 0), stop=(n == len(terms) - 1))
                last.then_inc(z_summed, 1)

            block = scope.enter_context(nc.Block())

            @block.sync
            def _(sp):
                for q in range(4):
                    sp.dma_start(A[:, 2 * q:2 * q + 2, :],
                                 adj.rearrange("(t p) m -> p t m", p=P)[:, 2 * q:2 * q + 2, :]).then_inc(loaded_adj, 16)
                for b in range(B):
                    sp.dma_start(X[:, b // 2, :, b % 2, :], x[b].rearrange("(t p) c -> p t c", p=P)).then_inc(loaded_x, 16)

            @block.gpsimd
            def _(pool):
                nc.gpsimd.memset(ident[:], 0.0).then_inc(ident_made, 1)
                pool.wait_ge(ident_made, 1)
                nc.gpsimd.affine_select(out=ident[:], in_=ident[:], compare_op=ALU.not_equal, fill=1.0, base=0,
                                        pattern=[[-1, P]], channel_multiplier=1).then_inc(ident_made, 1)
                pool.wait_ge(t_copied, 2 * NT)
                bodies(pool, pool_step)
                pool_split(pool, 4 * (TOK // 4), 0)
                Rj = R[:].rearrange("p (j t h) c -> p j t h c", j=J, h=2)
                for c in range(J + 1):
                    if c < J:
                        pool.wait_ge(z_reduced, 2 * NT * (c + 1) + 2)
                        nc.gpsimd.tensor_tensor(Rj[:, c], Rj[:, c], Eb[:].unsqueeze(2).to_broadcast([P, NT, 2, C]),
                                                ALU.add).then_inc(based, 1)
                    if c >= 1:
                        norm.pool_part(pool, c - 1)

            @block.scalar
            def _(act):
                wk = L0_weight.rearrange("d k i o -> k i d o")
                for k in range(2):
                    act.dma_start(wa[k * C:(k + 1) * C, :].rearrange("p (d o) -> p d o", o=C), wk[k]).then_inc(loaded_w, 16)
                for k in range(2):
                    act.dma_start(wb[k * C:(k + 1) * C, :].rearrange("p (d o) -> p d o", o=C), wk[2]).then_inc(loaded_w, 16)
                act.dma_start(emb[:], L0_embedding.rearrange("(t p) d -> p t d", p=P)).then_inc(loaded_w, 16)
                act.dma_start(biasw[:], L0_bias).then_inc(loaded_w, 16)
                copy_adj(act, nc.scalar.copy, AT, banks, at_banked, at_copied)
                bodies(act, act_step)
                norm.act_part(act)

            @block.vector
            def _(vec):
                vec.wait_ge(loaded_x, 16 * B)
                nc.vector.tensor_copy(XG[:, :, 0:C], Xrows).then_inc(x_placed, 1)
                vec.wait_ge(loaded_w, 16 * 6)
                nc.vector.tensor_copy(wa_hi[:], wa[:]).then_inc(split_w, 1)
                nc.vector.tensor_copy(wb_both[:], wb[:]).then_inc(split_w, 1)
                vec.wait_ge(split_w, 2)
                nc.vector.tensor_tensor(wa_lo[:], wa[:], wa_hi[:], ALU.subtract).then_inc(split_w, 1)
                nc.vector.tensor_tensor(wb_both[C:P, :], wb[C:P, :], wb_both[C:P, :], ALU.subtract).then_inc(split_w, 1)
                XGj = XG[:].rearrange("p (j t h) c -> p j t h c", j=J, h=2)
                for t in range(NT):
                    vec.wait_ge(t_summed, t + 1)
                    nc.vector.tensor_copy(XGj[:, :, t, :, C:2 * C],
                                          banks[t % 2][:].rearrange("p (j h c) -> p j h c", h=2, c=C)).then_inc(t_copied, 1)
                for t in range(NT):
                    vec.wait_ge(t_summed, NT + t + 1)
                    for h in range(2):
                        last = nc.vector.scalar_tensor_tensor(
                            out=XGj[:, :, t, h, 2 * C:3 * C],
                            in0=banks[t % 2][:].rearrange("p (j h c) -> p j h c", h=2, c=C)[:, :, h, :],
                            scalar=2.0, in1=XGj[:, :, t, h, 0:C], op0=ALU.mult, op1=ALU.subtract)
                    last.then_inc(t_copied, 1)
                vec.wait_ge(emb_banked, 1)
                nc.vector.tensor_copy(embT[:], zps[0][0:D, :]).then_inc(emb_copied, 1)
                vec.wait_ge(emb_banked, 2)
                nc.vector.tensor_copy(Eb[:].rearrange("p t c -> p (t c)"), zps[1][:, 0:HALF]).then_inc(emb_copied, 1)
                nc.vector.memset(zE[:, 0, :], 0.0).then_inc(z_reduced, 2)
                vec.wait_ge(z_reduced, 2)
                bodies(vec, vec_step)
                vec_weigh(vec, TOK - 2, 2)
                vec_reduce(vec, TOK - 3, 1)
                vec_weigh(vec, TOK - 1, 3)
                vec_reduce(vec, TOK - 2, 2)
                vec_reduce(vec, TOK - 1, 3)
                norm.vec_part(vec, lambda c: vec.wait_ge(based, c + 1))

            @block.tensor
            def _(pe):
                pe.wait_ge(ident_made, 2)
                pe.wait_ge(loaded_adj, 16 * 4)
                transpose_adj(pe, AT, banks, at_banked, at_copied)
                XGj = XG[:].rearrange("p (j t h) c -> p j t h c", j=J, h=2)
                pe.wait_ge(x_placed, 1)
                pe.wait_ge(at_copied, 2 * NT)
                for k in range(2):
                    if k == 1:
                        pe.wait_ge(t_copied, NT)
                    for t in range(NT):
                        if k * NT + t >= 2:
                            pe.wait_ge(t_copied, k * NT + t - 1)
                        for mt in range(NT):
                            last = nc.tensor.matmul(banks[t % 2][:].rearrange("p (j h c) -> p j h c", h=2, c=C),
                                                    AT[:, mt, t * P:(t + 1) * P],
                                                    XGj[:, :, mt, :, k * C:(k + 1) * C],
                                                    start=(mt == 0), stop=(mt == NT - 1))
                        last.then_inc(t_summed, 1)
                for t in range(NT):
                    last = nc.tensor.transpose(zps[0][0:D, t * P:(t + 1) * P], emb[:, t, :], ident[:])
                last.then_inc(emb_banked, 1)
                pe.wait_ge(emb_copied, 1)
                for t in range(NT):
                    last = nc.tensor.matmul(zps[1][:, t * C:(t + 1) * C], embT[:, t * P:(t + 1) * P], biasw[:],
                                            start=True, stop=True)
                last.then_inc(emb_banked, 1)
                pe.wait_ge(emb_copied, 2)
                pe.wait_ge(t_copied, 2 * NT)
                pe.wait_ge(split_w, 4)

                bodies(pe, pe_step)
                pe_products(pe, TOK, 0)

        MASKED = -1.0e16
        OFF = 8
        ZCUT = N // 2
        STEPS = 2 * NT

        def attention(scope, tag):
            s = {}
            for name in ("scored", "weighted", "zeroed", "zeroed_v", "shifted", "exped", "turned", "copied", "mixed",
                         "normed", "filled"):
                s[name] = sem(f"{tag}_{name}")
            work = sb(f"{tag}_work", [P, 4, N], F32, scope)
            masks = sb(f"{tag}_masks", [P, 2, N], F32, scope)
            weighted_start = sb(f"{tag}_weighted_start", [P, 1], F32, scope)
            filled = sb(f"{tag}_filled", [P, 1], F32, scope)
            zeroed_start = sb(f"{tag}_zeroed_start", [P, 1], F32, scope)
            copied_start = sb(f"{tag}_copied_start", [P, 1], F32, scope)
            probsT = sb(f"{tag}_probsT", [P, 2, NT, P], F32, scope)
            nmax = sb(f"{tag}_nmax", [P, 4], F32, scope)
            rowsum = sb(f"{tag}_rowsum", [P, 4], F32, scope)
            rinv = sb(f"{tag}_rinv", [P, 4], F32, scope)
            outs = sb(f"{tag}_outs", [P, 2, NT, C], F32, scope)
            Y2 = sb(f"{tag}_Y2", [P, 2, N], F32R, scope)
            Yl = sb(f"{tag}_Yl", [C, 2, N], F32R, scope)
            SX = sb(f"{tag}_SX", [P, B, N], F32R, scope)
            score_ps = [ps(f"{tag}_score_ps{k}", [P, N], scope) for k in range(2)]
            turn_ps = [ps(f"{tag}_turn_ps{k}", [P, HALF], scope) for k in range(2)]
            mix_ps = ps(f"{tag}_mix_ps", [P, HALF], scope)
            misc_ps = ps(f"{tag}_misc_ps", [P, HALF], scope)
            inv = sem(f"{tag}_inv")

            def init_pool(pool):
                nc.gpsimd.memset(weighted_start[:], 0.0).then_inc(s["weighted"], OFF)
                nc.gpsimd.memset(work[:], 0.0).then_inc(s["scored"], OFF)
                nc.gpsimd.memset(masks[:], 0.0).then_inc(s["zeroed"], OFF)
                nc.gpsimd.memset(nmax[:], 0.0).then_inc(s["shifted"], OFF - 1)
                nc.gpsimd.memset(rowsum[:], 1.0).then_inc(s["exped"], OFF - 2)
                nc.gpsimd.memset(probsT[:], 0.0).then_inc(s["turned"], 2 * (OFF - 3))
                nc.gpsimd.memset(copied_start[:], 0.0).then_inc(s["copied"], 2 * (OFF - 3))
                nc.gpsimd.memset(outs[:], 0.0).then_inc(s["mixed"], OFF - 4)
                nc.gpsimd.memset(filled[:], 0.0).then_inc(s["filled"], 1)

            def init_vec(vec):
                nc.vector.memset(mix_ps[:], 0.0).then_inc(s["normed"], OFF - 5)
                nc.vector.memset(rinv[:], 0.0).then_inc(inv, 2)
                nc.vector.memset(zeroed_start[:], 0.0).then_inc(s["zeroed_v"], OFF)

            def pe_scores(pe, g, t, u, x_cols):
                pe.wait_ge(s["weighted"], OFF + g - 1)
                rows = slice(t % NT * P, (t % NT + 1) * P)
                for half in range(2):
                    o = score_ps[t % 2][:, half * HALF:(half + 1) * HALF].unsqueeze(1)
                    nc.tensor.matmul(o, Y2[:, u, rows], SX[:, x_cols, half * HALF:(half + 1) * HALF], start=True, stop=False)
                    last = nc.tensor.matmul(o, Yl[:, u, rows], SX[0:C, x_cols, half * HALF:(half + 1) * HALF],
                                            start=False, stop=True)
                last.then_inc(s["scored"], 1)

            def pe_turn(pe, g, t):
                pe.wait_ge(s["exped"], OFF + g + 1)
                for half in range(2):
                    pe.wait_ge(s["copied"], 2 * (OFF + g) + half - 1)
                    for q in range(4):
                        k = half * 4 + q
                        last = nc.tensor.transpose(turn_ps[half][:, q * P:(q + 1) * P],
                                                   work[:, t % 4, k * P:(k + 1) * P], ident[:])
                    last.then_inc(s["turned"], 1)

            def pe_mix(pe, g, t, value):
                pe.wait_ge(s["copied"], 2 * (OFF + g + 1))
                pe.wait_ge(s["normed"], OFF + g)
                for mt in range(NT):
                    last = nc.tensor.matmul(mix_ps[:, (t % NT) * C:(t % NT + 1) * C].unsqueeze(1), probsT[:, t % 2, mt, :],
                                            value(mt), start=(mt == 0), stop=(mt == NT - 1))
                last.then_inc(s["mixed"], 1)

            def vec_weigh(vec, g, t):
                vec.wait_ge(s["scored"], OFF + g + 1)
                vec.wait_ge(s["turned"], 2 * (OFF + g - 3))
                nc.vector.tensor_tensor(work[:, t % 4, :], score_ps[t % 2][:], A[:, t % NT, :],
                                        ALU.mult).then_inc(s["weighted"], 1)

            def pool_zero(pool, g, t):
                pool.wait_ge(s["weighted"], OFF + g + 1)
                pool.wait_ge(s["shifted"], OFF + g - 1)
                pool.nop(nofuse=True)
                nc.gpsimd.tensor_scalar(masks[:, t % 2, ZCUT:N], work[:, t % 4, ZCUT:N], 0.0, MASKED,
                                        ALU.is_equal, ALU.mult).then_inc(s["zeroed"], 1)

            def vec_zero(vec, g, t):
                vec.wait_ge(s["weighted"], OFF + g + 1)
                nc.vector.tensor_scalar(masks[:, t % 2, 0:ZCUT], work[:, t % 4, 0:ZCUT], 0.0, MASKED,
                                        ALU.is_equal, ALU.mult).then_inc(s["zeroed_v"], 1)

            def vec_shift(vec, g, t):
                vec.wait_ge(s["zeroed"], OFF + g + 1)
                vec.wait_ge(s["zeroed_v"], OFF + g + 1)
                vec.wait_ge(s["exped"], OFF + g - 3)
                vec.nop(nofuse=True)
                nc.vector.tensor_tensor_reduce(work[:, t % 4, :], masks[:, t % 2, :], work[:, t % 4, :], -1.0, 3.0e38,
                                               ALU.add, ALU.min, nmax[:, t % 4:t % 4 + 1]).then_inc(s["shifted"], 1)

            def act_exp(act, g, t):
                act.wait_ge(s["shifted"], OFF + g + 1)
                act.wait_ge(s["normed"], OFF + g - 3)
                nc.scalar.activation(work[:, t % 4, :], work[:, t % 4, :], ACT.Exp, bias=nmax[:, t % 4:t % 4 + 1],
                                     scale=-1.0, accum_out=rowsum[:, t % 4:t % 4 + 1]).then_inc(s["exped"], 1)

            def act_copy(act, g, t):
                act.wait_ge(s["mixed"], OFF + g - 1)
                for half in range(2):
                    act.wait_ge(s["turned"], 2 * (OFF + g) + half + 1)
                    nc.scalar.copy(probsT[:, t % 2, half * 4:half * 4 + 4, :].rearrange("p a b -> p (a b)"),
                                   turn_ps[half][:]).then_inc(s["copied"], 1)

            def vec_invert(vec, g, t):
                vec.wait_ge(s["exped"], OFF + g + 1)
                nc.vector.reciprocal(rinv[:, t % 4:t % 4 + 1], rowsum[:, t % 4:t % 4 + 1]).then_inc(inv, 1)

            def vec_norm(vec, g, t, out):
                vec.wait_ge(s["mixed"], OFF + g + 1)
                vec.wait_ge(inv, g + 7)
                nc.vector.tensor_scalar(out, mix_ps[:, (t % NT) * C:(t % NT + 1) * C].unsqueeze(1),
                                        rinv[:, t % 4:t % 4 + 1], None, ALU.mult).then_inc(s["normed"], 1)

            at = Pipeline()
            at.s, at.probsT, at.outs, at.Y2, at.Yl, at.SX = (
                s, probsT, outs, Y2, Yl, SX)
            at.turn_ps, at.mix_ps, at.misc_ps, at.score_ps, at.init_pool, at.init_vec = (
                turn_ps, mix_ps, misc_ps, score_ps, init_pool, init_vec)
            at.pe_scores, at.pe_turn, at.pe_mix, at.vec_weigh, at.pool_zero, at.vec_zero = (
                pe_scores, pe_turn, pe_mix, vec_weigh, pool_zero, vec_zero)
            at.vec_shift, at.act_exp, at.act_copy, at.vec_norm = (
                vec_shift, act_exp, act_copy, vec_norm)
            at.vec_invert = vec_invert
            return at

        acc_scope = keep.enter_context(ExitStack())
        h2T = sb("h2T", [C, B + 1, N], F32, acc_scope)
        PAIRS = B * HEADS

        with ExitStack() as scope:
            at = attention(scope, "hid")
            s, Y2, Yl, SX, outs, misc_ps = at.s, at.Y2, at.Yl, at.SX, at.outs, at.misc_ps
            wh_twice = sb("wh", [P, HEADS, HID], F32, scope)
            wh = wh_twice[0:C]
            wo = sb("wo", [P, HEADS, C], F32, scope)
            bh = sb("bh", [P, HEADS], F32, scope)
            whT = sb("whT", [P, 2, 2, C], F32, scope)
            Mh = sb("Mh", [P, HEADS, 2, C], F32R, scope)
            Ml = sb("Ml", [C, HEADS, 2, C], F32R, scope)
            Mh_now = sb("Mh_now", [P, 2, 2 * C], F32R, scope)
            Ml_now = sb("Ml_now", [C, 2, 2 * C], F32R, scope)
            wh_hi = sb("wh_hi", [P, HEADS, HID], F32R, scope)
            wh_lo = sb("wh_lo", [C, HEADS, HID], F32R, scope)
            wh_hi_now = sb("wh_hi_now", [P, 2, HID], F32R, scope)
            wh_lo_now = sb("wh_lo_now", [C, 2, HID], F32R, scope)
            wo_now = sb("wo_now", [P, 2, C], F32, scope)
            onT = sb("onT", [P, HALF], F32R, scope)
            biased = sb("biased", [P, HALF], F32, scope)
            leaky = sb("leaky", [P, HALF], F32, scope)
            loaded = sem("hid_loaded")
            w_turned, w_copied, m_made, m_split = (sem(f"hid_{n}") for n in ("w_turned", "w_copied", "m_made", "m_split"))
            sx_banked, sx_hi, sx_lo = sem("hid_sx_banked"), sem("hid_sx_hi"), sem("hid_sx_lo")
            misc_made, misc_read = sem("hid_misc_made"), sem("hid_misc_read")
            on_hi, wh_split = sem("hid_on_hi"), sem("hid_wh_split")
            y_hi, leaky_made = sem("hid_y_hi"), sem("hid_leaky")
            staged, cleared = sem("hid_staged"), sem("hid_cleared")

            def pe_small(pe, p, n, k):
                u, t = k // NT, k % NT
                pe.wait_ge(misc_read, OFF + n)
                if t < 2:
                    if t == 0:
                        pe.wait_ge(staged, p + 1)
                    b, cols = bass.ds((p + 1) // HEADS % B, 1), slice(t * HALF, (t + 1) * HALF)
                    o = misc_ps[:].unsqueeze(1)
                    nc.tensor.matmul(o, Mh_now[:, 1 - u, :], SX[:, b, cols], start=True, stop=False)
                    last = nc.tensor.matmul(o, Ml_now[:, 1 - u, :], SX[0:C, b, cols], start=False, stop=True)
                elif t % 3 == 2:
                    half = (t - 2) // 3
                    pe.wait_ge(s["normed"], OFF + NT * (p - 1) + 4 * half + 4)
                    pe.nop(nofuse=True)
                    for q in range(4):
                        last = nc.tensor.transpose(misc_ps[0:C, q * P:(q + 1) * P], outs[:, 1 - u, half * 4 + q, :],
                                                   ident[:])
                elif t % 3 == 0:
                    nc.tensor.matmul(misc_ps[:], wh_hi_now[:, 1 - u, :], onT[:], start=True, stop=False)
                    last = nc.tensor.matmul(misc_ps[:], wh_lo_now[:, 1 - u, :], onT[0:C, :], start=False, stop=True)
                else:
                    pe.wait_ge(leaky_made, 2 * p + (t - 2) // 3 + 1)
                    last = nc.tensor.matmul(misc_ps[0:C, :], wo_now[:, 1 - u, :], leaky[:], start=True, stop=True)
                last.then_inc(misc_made, 1)

            def act_small(act, p, n, k):
                u, t = k // NT, k % NT
                if t < 2:
                    act.wait_ge(misc_made, OFF + n + 1)
                    nc.scalar.copy(Y2[:, 1 - u, t * HALF:(t + 1) * HALF], misc_ps[:]).then_inc(y_hi, 1)
                elif t % 3 == 2:
                    act.wait_ge(misc_made, OFF + n + 1)
                    nc.scalar.copy(onT[0:C, :], misc_ps[0:C, :]).then_inc(on_hi, 1)
                elif t % 3 == 0:
                    act.wait_ge(misc_made, OFF + n + 1)
                    act.nop(nofuse=True)
                    nc.scalar.activation(biased[:], misc_ps[:], ACT.Identity,
                                         bias=bh[:, bass.ds((p + HEADS - 1) % HEADS, 1)]).then_inc(misc_read, 1)

            def vec_small(vec, p, n, k):
                u, t = k // NT, k % NT
                if t < 2:
                    cols = slice(t * HALF, (t + 1) * HALF)
                    vec.wait_ge(y_hi, 2 * p + t + 3)
                    nc.vector.tensor_tensor(Yl[:, 1 - u, cols], misc_ps[0:C, :], Y2[0:C, 1 - u, cols],
                                            ALU.subtract).then_inc(misc_read, 1)
                elif t % 3 == 2:
                    vec.wait_ge(on_hi, 2 * p + (t - 2) // 3 + 1)
                    nc.vector.tensor_tensor(onT[C:P, :], misc_ps[0:C, :], onT[0:C, :], ALU.subtract).then_inc(misc_read, 1)
                elif t % 3 == 0:
                    vec.wait_ge(misc_read, OFF + n + 1)
                    nc.vector.scalar_tensor_tensor(out=leaky[:], in0=biased[:], scalar=0.01, in1=biased[:],
                                                   op0=ALU.mult, op1=ALU.max).then_inc(leaky_made, 1)
                elif t % 3 == 1:
                    half = (t - 2) // 3
                    acc = h2T[:, bass.ds((p + HEADS - 1) // HEADS, 1), half * HALF:(half + 1) * HALF]
                    vec.wait_ge(misc_made, OFF + n + 1)
                    nc.vector.tensor_tensor(acc, acc, misc_ps[0:C, :].unsqueeze(1), ALU.add).then_inc(misc_read, 1)

            def pe_step(pe, p, k, new=True):
                t = k % NT
                g = NT * p + t
                if new:
                    at.pe_scores(pe, g, k, k // NT, bass.ds(p // HEADS, 1))
                if new or t < 3:
                    at.pe_turn(pe, g - 3, (k - 3) % STEPS)
                if new or t < 4:
                    b = p // HEADS % B if t >= 4 else (p + PAIRS - 1) % PAIRS // HEADS
                    at.pe_mix(pe, g - 4, (k - 4) % STEPS, lambda mt: Xrows[:, bass.ds(row(b, mt), 1), :])
                if new or t < NT - 1:
                    pe_small(pe, p + (t + 1) // NT, g + 1, (k + 1) % STEPS)

            def act_step(act, p, k, new=True):
                t = k % NT
                g = NT * p + t
                act_small(act, p, g, k)
                if new or t < 2:
                    at.act_exp(act, g - 2, (k - 2) % STEPS)
                if new or t < 3:
                    at.act_copy(act, g - 3, (k - 3) % STEPS)

            def vec_step(vec, p, k, new=True):
                t = k % NT
                g = NT * p + t
                if new or t < 5:
                    at.vec_norm(vec, g - 5, (k - 5) % STEPS, outs[:, (k - 5) % STEPS // NT, (k - 5) % NT, :].unsqueeze(1))
                if new:
                    at.vec_weigh(vec, g, k)
                vec_small(vec, p, g, k)
                if new or t < 4:
                    at.vec_invert(vec, g - 4, (k - 4) % STEPS)
                if new or t < 1:
                    at.vec_shift(vec, g - 1, (k - 1) % STEPS)
                if new:
                    at.vec_zero(vec, g, k)

            def stage_weights(pool, head_m, head_w, u):
                nc.gpsimd.tensor_copy(Mh_now[:, u, :].unsqueeze(1), Mh[:, head_m, :, :].rearrange("p a r c -> p a (r c)"))
                nc.gpsimd.tensor_copy(Ml_now[:, u, :].unsqueeze(1), Ml[:, head_m, :, :].rearrange("p a r c -> p a (r c)"))
                nc.gpsimd.tensor_copy(wh_hi_now[:, u, :].unsqueeze(1), wh_hi[:, head_w, :])
                nc.gpsimd.tensor_copy(wh_lo_now[:, u, :].unsqueeze(1), wh_lo[:, head_w, :])
                return nc.gpsimd.tensor_copy(wo_now[:, u, :].unsqueeze(1), wo[:, head_w, :])

            block = scope.enter_context(nc.Block())

            @block.sync
            def _(sp):
                for half in range(2):
                    sp.dma_start(wh_twice[half * C:(half + 1) * C], L1_Wh.rearrange("h c d -> c h d")).then_inc(loaded, 16)
                sp.dma_start(wo[:], L1_W_out.rearrange("(h d) c -> d h c", d=HID)).then_inc(loaded, 16)
                sp.dma_start(bh[:], L1_bh.rearrange("h d -> d h"), allow_slow_non_contiguous=True).then_inc(loaded, 16)

            @block.gpsimd
            def _(pool):
                at.init_pool(pool)
                nc.gpsimd.memset(h2T[:], 0.0).then_inc(cleared, 1)
                pool.wait_ge(m_split, HEADS)
                pool.wait_ge(wh_split, 2)
                stage_weights(pool, bass.ds(0, 1), bass.ds(0, 1), 0)
                stage_weights(pool, bass.ds(1, 1), bass.ds(HEADS - 1, 1), 1).then_inc(staged, 1)
                with pool.Fori(0, PAIRS // 2) as i:
                    for k in range(STEPS):
                        p = 2 * i + k // NT
                        at.pool_zero(pool, STEPS * i + k, k)
                        if k % NT == 2:
                            pool.wait_ge(misc_made, OFF + NT * p)
                            stage_weights(pool, bass.ds((p + 2) % HEADS, 1), bass.ds(p % HEADS, 1),
                                          k // NT).then_inc(staged, 1)

            @block.scalar
            def _(act):
                for b in range(B):
                    act.wait_ge(sx_banked, b + 1)
                    nc.scalar.copy(SX[0:C, b, :], at.score_ps[b % 2][0:C, :]).then_inc(sx_hi, 1)
                for half in range(2):
                    act.wait_ge(misc_made, OFF - 2 + half + 1)
                    nc.scalar.copy(Y2[:, 0, half * HALF:(half + 1) * HALF], misc_ps[:]).then_inc(y_hi, 1)
                act.wait_ge(s["filled"], 1)
                with act.Fori(0, PAIRS // 2) as i:
                    for k in range(STEPS):
                        act_step(act, 2 * i + k // NT, k)
                for t in range(NT):
                    act_step(act, PAIRS, t, new=False)

            @block.vector
            def _(vec):
                at.init_vec(vec)
                vec.wait_ge(loaded, 16 * 4)
                nc.vector.tensor_copy(wh_hi[:], wh_twice[:]).then_inc(wh_split, 1)
                vec.wait_ge(wh_split, 1)
                nc.vector.tensor_tensor(wh_lo[:], wh, wh_hi[0:C], ALU.subtract).then_inc(wh_split, 1)
                for h in range(HEADS):
                    vec.wait_ge(w_turned, h + 1)
                    nc.vector.tensor_copy(whT[:, h % 2, :, :], at.turn_ps[0][:, 0:C].unsqueeze(1).to_broadcast([P, 2, C])).then_inc(w_copied, 1)
                    vec.wait_ge(m_made, h + 1)
                    m = at.turn_ps[1][:, 0:C].unsqueeze(1).to_broadcast([P, 2, C])
                    nc.vector.tensor_copy(Mh[:, h, :, :], m).then_inc(w_copied, 1)
                    vec.wait_ge(w_copied, 2 * h + 2)
                    nc.vector.tensor_tensor(Ml[:, h, :, :], m[0:C], Mh[0:C, h, :, :], ALU.subtract).then_inc(m_split, 1)
                for b in range(B):
                    vec.wait_ge(sx_hi, b + 1)
                    nc.vector.tensor_tensor(SX[C:P, b, :], at.score_ps[b % 2][0:C, :], SX[0:C, b, :],
                                            ALU.subtract).then_inc(sx_lo, 1)
                for half in range(2):
                    cols = slice(half * HALF, (half + 1) * HALF)
                    vec.wait_ge(y_hi, half + 1)
                    nc.vector.tensor_tensor(Yl[:, 0, cols], misc_ps[0:C, :], Y2[0:C, 0, cols],
                                            ALU.subtract).then_inc(misc_read, OFF - 1 if half == 0 else 1)
                vec.wait_ge(cleared, 1)
                vec.wait_ge(s["filled"], 1)
                with vec.Fori(0, PAIRS // 2) as i:
                    for k in range(STEPS):
                        vec_step(vec, 2 * i + k // NT, k)
                for t in range(NT):
                    vec_step(vec, PAIRS, t, new=False)

            @block.tensor
            def _(pe):
                pe.wait_ge(loaded, 16 * 4)
                for h in range(HEADS):
                    if h:
                        pe.wait_ge(w_copied, 2 * h - 1)
                    nc.tensor.transpose(at.turn_ps[0][:, 0:C], wh[:, h, :], ident[0:C, 0:C]).then_inc(w_turned, 1)
                    pe.wait_ge(w_copied, 2 * h + 1)
                    if h:
                        pe.wait_ge(m_split, h)
                    nc.tensor.matmul(at.turn_ps[1][:, 0:C], whT[:, h % 2, :, :].rearrange("p r c -> p (r c)"),
                                     whT[:, h % 2, 0, :], start=True, stop=True).then_inc(m_made, 1)
                for b in range(B):
                    if b >= 2:
                        pe.wait_ge(sx_lo, b - 1)
                    for t in range(NT):
                        last = nc.tensor.transpose(at.score_ps[b % 2][0:C, t * P:(t + 1) * P], Xrows[:, row(b, t), :], ident[:])
                    last.then_inc(sx_banked, 1)
                pe.wait_ge(sx_lo, B)
                pe.wait_ge(staged, 1)
                for half in range(2):
                    if half:
                        pe.wait_ge(misc_read, OFF - 1)
                    cols = slice(half * HALF, (half + 1) * HALF)
                    nc.tensor.matmul(misc_ps[:], Mh_now[:, 0, :], SX[:, 0, cols], start=True, stop=False)
                    nc.tensor.matmul(misc_ps[:], Ml_now[:, 0, :], SX[0:C, 0, cols], start=False,
                                     stop=True).then_inc(misc_made, OFF - 1 if half == 0 else 1)
                pe.wait_ge(misc_read, OFF)
                pe.wait_ge(s["filled"], 1)
                pe_small(pe, 0, 0, 0)
                with pe.Fori(0, PAIRS // 2) as i:
                    for k in range(STEPS):
                        pe_step(pe, 2 * i + k // NT, k)
                for t in range(NT):
                    pe_step(pe, PAIRS, t, new=False)

        with ExitStack() as scope:
            at = attention(scope, "fin")
            s, Y2, Yl, SX = at.s, at.Y2, at.Yl, at.SX
            V = sb("V", [P, B, NT, C], F32, scope)
            b_out = sb("b_out", [P, C], F32, scope)
            R = sb("R1", [P, TOK, C], F32, scope)
            norm = residual_norm(1, R[:], V[:].rearrange("p b t c -> p (b t) c"), scope)
            loaded = sem("fin_loaded")
            v_banked, v_copied, sx_hi, sx_lo = sem("fin_v_banked"), sem("fin_v_copied"), sem("fin_sx_hi"), sem("fin_sx_lo")
            y_made = sem("fin_y_made")
            biased, leaked = sem("fin_biased"), sem("fin_leaked")
            TILES = B * NT

            def make_y(pair, u):
                b = bass.ds(pair, 1)
                nc.vector.tensor_copy(Y2[0:C, u, :].unsqueeze(1), SX[0:C, b, :])
                nc.vector.tensor_copy(Y2[C:P, u, :].unsqueeze(1), SX[0:C, b, :])
                return nc.vector.tensor_copy(Yl[:, u, :].unsqueeze(1), SX[C:P, b, :])

            def out_row(p, k):
                t = k % NT
                r = row(p, t - 5) if t >= 5 else row((p + B - 1) % B, t - 5 + NT)
                return R[:, bass.ds(r, 1), :]

            def pe_step(pe, p, k, new=True):
                t = k % NT
                g = NT * p + t
                if new:
                    if t == 0:
                        pe.wait_ge(y_made, p + 1)
                    at.pe_scores(pe, g, k, k // NT, bass.ds(p, 1))
                if new or t < 3:
                    at.pe_turn(pe, g - 3, (k - 3) % STEPS)
                if new or t < 4:
                    b = bass.ds(p if t >= 4 else (p + B - 1) % B, 1)
                    at.pe_mix(pe, g - 4, (k - 4) % STEPS, lambda mt: V[:, b, mt, :])

            def act_step(act, p, k, new=True):
                t = k % NT
                g = NT * p + t
                if new or t < 2:
                    at.act_exp(act, g - 2, (k - 2) % STEPS)
                if new or t < 3:
                    at.act_copy(act, g - 3, (k - 3) % STEPS)

            def vec_step(vec, p, k, new=True):
                t = k % NT
                g = NT * p + t
                if new or t < 5:
                    at.vec_norm(vec, g - 5, (k - 5) % STEPS, out_row(p, k))
                if new:
                    at.vec_weigh(vec, g, k)
                    if t == 1:
                        make_y((p + 1) % B, 1 - k // NT).then_inc(y_made, 1)
                if new or t < 4:
                    at.vec_invert(vec, g - 4, (k - 4) % STEPS)
                if new or t < 1:
                    at.vec_shift(vec, g - 1, (k - 1) % STEPS)
                if new:
                    at.vec_zero(vec, g, k)

            block = scope.enter_context(nc.Block())

            @block.sync
            def _(sp):
                sp.dma_start(b_out[:], L1_b_out.unsqueeze(0).to_broadcast([P, C])).then_inc(loaded, 16)

            @block.gpsimd
            def _(pool):
                at.init_pool(pool)
                with pool.Fori(0, B // 2) as i:
                    for k in range(STEPS):
                        at.pool_zero(pool, STEPS * i + k, k)
                pool.wait_ge(loaded, 16)
                for c in range(J + 1):
                    if c < J:
                        pool.wait_ge(s["normed"], OFF + 2 * NT * (c + 1))
                        rc = R[:, norm.rows(c)]
                        nc.gpsimd.tensor_tensor(rc, rc, b_out[:].unsqueeze(1).to_broadcast([P, 2 * NT, C]),
                                                ALU.add).then_inc(biased, 1)
                    if c >= 1:
                        norm.pool_part(pool, c - 1)

            @block.scalar
            def _(act):
                for b in range(B):
                    nc.scalar.copy(SX[0:C, b, :], h2T[:, b + 1, :]).then_inc(sx_hi, 1)
                for b in range(B):
                    act.wait_ge(v_banked, b + 1)
                    nc.scalar.copy(V[:, b, :, :].rearrange("p t c -> p (t c)"), at.turn_ps[b % 2][:]).then_inc(v_copied, 1)
                act.wait_ge(s["filled"], 1)
                with act.Fori(0, B // 2) as i:
                    for k in range(STEPS):
                        act_step(act, 2 * i + k // NT, k)
                for t in range(NT):
                    act_step(act, B, t, new=False)
                norm.act_part(act)

            @block.vector
            def _(vec):
                at.init_vec(vec)
                for b in range(B):
                    vec.wait_ge(sx_hi, b + 1)
                    nc.vector.tensor_tensor(SX[C:P, b, :], h2T[:, b + 1, :], SX[0:C, b, :], ALU.subtract).then_inc(sx_lo, 1)
                vec.wait_ge(sx_lo, 1)
                make_y(0, 0).then_inc(y_made, 1)
                vec.wait_ge(s["filled"], 1)
                with vec.Fori(0, B // 2) as i:
                    for k in range(STEPS):
                        vec_step(vec, 2 * i + k // NT, k)
                for t in range(NT):
                    vec_step(vec, B, t, new=False)
                def leak(c):
                    vec.wait_ge(biased, c + 1)
                    rc = R[:, norm.rows(c)]
                    nc.vector.scalar_tensor_tensor(out=rc, in0=rc, scalar=0.01, in1=rc, op0=ALU.mult,
                                                   op1=ALU.max).then_inc(leaked, 1)
                    vec.wait_ge(leaked, c + 1)

                norm.vec_part(vec, leak)

            @block.tensor
            def _(pe):
                for b in range(B):
                    if b >= 2:
                        pe.wait_ge(v_copied, b - 1)
                    for t in range(NT):
                        last = nc.tensor.transpose(at.turn_ps[b % 2][:, t * C:(t + 1) * C],
                                                   h2T[:, b + 1, t * P:(t + 1) * P], ident[0:C, 0:C])
                    last.then_inc(v_banked, 1)
                pe.wait_ge(v_copied, B)
                pe.wait_ge(sx_lo, B)
                pe.wait_ge(s["filled"], 1)
                with pe.Fori(0, B // 2) as i:
                    for k in range(STEPS):
                        pe_step(pe, 2 * i + k // NT, k)
                for t in range(NT):
                    pe_step(pe, B, t, new=False)
        acc_scope.close()

        NEG = -1.0e9
        Xj = X[:].rearrange("p j t h c -> p j t (h c)")
        l2_scope = keep.enter_context(ExitStack())
        ind = sb("ind", [P, J, NT, 2, C], F32, l2_scope)
        agg = sb("agg", [P, J, E], F32, l2_scope)
        node_edge = sb("node_edge", [P, 2, J, N], F32, l2_scope)
        gate = node_edge[:, 0]
        coefT = node_edge[:, 1]
        with ExitStack() as first_use:
            AT = sb("AT2", [P, NT, N], F32, first_use)
        hT_parts = sb("hT_parts", [P, 2, J, N], F32R, l2_scope)
        AxT = coefT
        wi2 = sb("wi2", [P, P], F32, l2_scope)
        rdeg = sb("rdeg", [P, NT], F32, l2_scope)
        fcw = sb("fcw", [P, P], F32, l2_scope)
        fcb = sb("fcb", [P, 1], F32, l2_scope)
        av = sb("av", [P, 1], F32, l2_scope)
        late_scope = ExitStack()
        hT = sb("hT", [P, J, N], F32, late_scope)
        hN = sb("hN", [P, J, NT, P], F32, late_scope)

        def couple_blocks(m):
            return m[0:C, 0:C], m[C:P, C:P]

        with ExitStack() as scope:
            xT = gate
            w2 = sb("w2", [P, P], F32, scope)
            deg = sb("deg", [P, NT], F32, scope)
            banks = [ps(f"l2_bank{k}", [P, HALF], scope) for k in range(2)]
            wide = [ps(f"l2_wide{k}", [P, N], scope) for k in range(3)]
            zeroed, loaded = sem("l2_zeroed"), sem("l2_loaded")
            at_banked, at_copied = sem("l2_at_banked"), sem("l2_at_copied")
            xt_banked, xt_copied = sem("l2_xt_banked"), sem("l2_xt_copied")
            h_banked, hT_copied, hN_copied = sem("l2_h_banked"), sem("l2_hT_copied"), sem("l2_hN_copied")
            deg_made = sem("l2_deg_made")

            block = scope.enter_context(nc.Block())

            @block.sync
            def _(sp):
                sp.wait_ge(zeroed, 2)
                for m, w in ((w2, L2_W), (wi2, L2_W_ind)):
                    for part in couple_blocks(m):
                        sp.dma_start(part, w).then_inc(loaded, 16)
                for half in range(2):
                    sp.dma_start(fcw[half * C:(half + 1) * C, :], L2_fcW).then_inc(loaded, 16)
                sp.dma_start(fcb[:], L2_fcb.unsqueeze(1)).then_inc(loaded, 16)
                sp.dma_start(av[:], L2_av.unsqueeze(1)).then_inc(loaded, 16)
                sp.wait_ge(loaded, 16 * 8)

            @block.gpsimd
            def _(pool):
                nc.gpsimd.memset(w2[:], 0.0).then_inc(zeroed, 1)
                nc.gpsimd.memset(wi2[:], 0.0).then_inc(zeroed, 1)

            @block.scalar
            def _(act):
                for j in range(J):
                    act.wait_ge(h_banked, 2 * j + 2)
                    nc.scalar.copy(hN[:, j, :, :].rearrange("p t f -> p (t f)"), wide[(2 * j + 1) % 3][:]).then_inc(hN_copied, 1)
                copy_adj(act, nc.scalar.copy, AT, banks, at_banked, at_copied)

            @block.vector
            def _(vec):
                for j in range(J):
                    vec.wait_ge(xt_banked, j + 1)
                    nc.vector.tensor_copy(xT[:, j, :], wide[j % 3][:]).then_inc(xt_copied, 1)
                for j in range(J):
                    vec.wait_ge(h_banked, 2 * j + 1)
                    nc.vector.tensor_copy(hT[:, j, :], wide[2 * j % 3][:]).then_inc(hT_copied, 1)
                nc.vector.tensor_reduce(deg[:], A[:], AX.X, ALU.add).then_inc(deg_made, 1)
                vec.wait_ge(deg_made, 1)
                nc.vector.tensor_scalar(deg[:], deg[:], 1.0, None, ALU.max).then_inc(deg_made, 1)
                vec.wait_ge(deg_made, 2)
                nc.vector.reciprocal(rdeg[:], deg[:]).then_inc(deg_made, 1)

            @block.tensor
            def _(pe):
                for j in range(J):
                    if j >= 3:
                        pe.wait_ge(xt_copied, j - 2)
                    for t in range(NT):
                        last = nc.tensor.transpose(wide[j % 3][:, t * P:(t + 1) * P], Xj[:, j, t, :], ident[:])
                    last.then_inc(xt_banked, 1)
                pe.wait_ge(xt_copied, J)
                pe.wait_ge(loaded, 16 * 8)
                for n in range(2 * J):
                    j, o = n // 2, wide[n % 3]
                    if n >= 3:
                        pe.wait_ge(hN_copied if (n - 3) % 2 else hT_copied, (n - 3) // 2 + 1)
                    if n % 2 == 0:
                        for half in range(2):
                            cols = slice(half * HALF, (half + 1) * HALF)
                            last = nc.tensor.matmul(o[:, cols], w2[:], xT[:, j, cols], start=True, stop=True)
                    else:
                        for t in range(NT):
                            cols = slice(t * P, (t + 1) * P)
                            last = nc.tensor.matmul(o[:, cols], xT[:, j, cols], w2[:], start=True, stop=True)
                    last.then_inc(h_banked, 1)
                transpose_adj(pe, AT, banks, at_banked, at_copied)

        with ExitStack() as scope:
            incid = sb("incid", [P, NT, 2, E], F32, scope)
            member = sb("member", [P, NT, E], F32, scope)
            outside = sb("outside", [P, NT, E], F32, scope)
            memberT = sb("memberT", [P, N], F32, scope)
            outsideT = sb("outsideT", [P, N], F32, scope)
            a_rows = sb("a_rows", [P, 3], F32, scope)
            a_node2 = sb("a_node2", [P, P], F32, scope)
            a_gn2 = sb("a_gn2", [P, P], F32, scope)
            a_ge = sb("a_ge", [P, C], F32, scope)
            sc = sb("sc", [P, N], F32, scope)
            lk = sb("lk", [P, 2, N], F32, scope)
            alphaT = sb("alphaT", [P, NT, P], F32, scope)
            cells = hN[:].rearrange("p j t (h e) -> p j t h e", h=2)
            small = sb("small", [P, 24], F32, scope)
            elu_a = sb("elu_a", [P, J, E], F32, scope)
            heT = sb("heT", [C, J * P], F32, scope)
            th = sb("th", [P, J * P], F32, scope)
            se = sb("se", [P, B, E], F32, scope)
            cmax = sb("cmax", [P, NT * B], F32, scope)
            crcp = sb("crcp", [P, NT * B], F32, scope)
            banks = [ps(f"l2b_bank{k}", [P, HALF], scope) for k in range(2)]
            wide = [ps(f"l2b_wide{k}", [P, N], scope) for k in range(3)]
            zeroed, loaded = sem("l2b_zeroed"), sem("l2b_loaded")
            (s_made, s_copied, s_turned, s_turn_copied, s_agg, s_exped, s_gn, s_gexp, v_steps, s_h, s_he, s_he_c, s_fc,
             s_tanh, s_se, s_elu, s_ct, s_ct_copied, s_cexp, s_ht) = (
                sem(f"l2b_{n}") for n in ("scored", "score_copied", "turned", "turn_copied", "agg_made", "exped",
                                          "gn_made", "gate_exped", "vector_steps", "incid_turned", "he_turned",
                                          "he_copied", "fc_made", "tanhed", "se_made", "elu_exped", "coef_turned",
                                          "coef_copied", "coef_exped", "logits_ready"))
            s_leaked, s_masked, s_lowered, s_inverted, s_divided = (
                sem(f"l2b_{n}") for n in ("leaked", "masked", "lowered", "inverted", "divided"))
            ax_made, ax_copied, ind_made, ind_taken, h_rounded, h_parted = (
                sem(f"l2b_{n}") for n in ("ax_made", "ax_copied", "ind_made", "ind_taken", "h_rounded", "h_parted"))
            units = [(j, slice(half * HALF, (half + 1) * HALF)) for j in range(J) for half in range(2)]
            block = scope.enter_context(nc.Block())

            @block.sync
            def _(sp):
                Hn = L2_H.rearrange("(t p) e -> p t e", p=P)
                for half in range(2):
                    sp.dma_start(incid[:, :, half, :], Hn).then_inc(loaded, 16)
                for k, v in enumerate((L2_a_node, L2_a_gn)):
                    for half in range(2):
                        sp.dma_start(a_rows[half * C:(half + 1) * C, k:k + 1], v.unsqueeze(1)).then_inc(loaded, 16)
                sp.dma_start(a_ge[:], L2_a_ge.unsqueeze(0).to_broadcast([P, C])).then_inc(loaded, 16)
                sp.wait_ge(loaded, 16 * 7)

            @block.gpsimd
            def _(pool):
                nc.gpsimd.memset(a_node2[:], 0.0).then_inc(zeroed, 1)
                nc.gpsimd.memset(a_gn2[:], 0.0).then_inc(zeroed, 1)
                shape = [P, NT, 2, E]
                pool.wait_ge(v_steps, 600)
                for j in range(J):
                    nc.gpsimd.tensor_tensor(cells[:, j], se[:, 2 * j:2 * j + 2, :].unsqueeze(1).to_broadcast(shape),
                                            member[:].unsqueeze(2).to_broadcast(shape), ALU.mult).then_inc(s_masked, 1)
                for j in range(J):
                    rows = slice(2 * NT * j, 2 * NT * (j + 1))
                    cj = cells[:, j].rearrange("p t h e -> p (t h) e")
                    pool.wait_ge(s_inverted, j + 1)
                    nc.gpsimd.tensor_tensor(cj, cj, crcp[:, rows].unsqueeze(2).to_broadcast([P, 2 * NT, E]),
                                            ALU.mult).then_inc(s_divided, 1)

            @block.scalar
            def _(act):
                def copy_score(j):
                    act.wait_ge(s_made, j + 1)
                    if j:
                        act.wait_ge(s_leaked, j)
                    nc.scalar.copy(sc[:], wide[0][:]).then_inc(s_copied, 1)

                def copy_ax(n):
                    j, cols = units[n]
                    act.wait_ge(ax_made, n + 1)
                    nc.scalar.copy(AxT[:, j, cols], wide[2][:, cols]).then_inc(ax_copied, 1)

                copy_ax(0)
                copy_score(0)
                for j in range(J):
                    act.wait_ge(s_ht, j + 1)
                    nc.scalar.activation(lk[:, j % 2, :], lk[:, j % 2, :], ACT.Exp, bias=small[:, j:j + 1], scale=-1.0,
                                         accum_out=small[:, 4 + j:5 + j]).then_inc(s_exped, 1)
                    copy_ax(j + 1)
                    if j + 1 < J:
                        copy_score(j + 1)
                    act.wait_ge(s_turned, j + 1)
                    if j:
                        act.wait_ge(s_agg, j)
                    nc.scalar.copy(alphaT[:].rearrange("p t k -> p (t k)"), wide[1][:]).then_inc(s_turn_copied, 1)
                copy_ax(J + 1)
                act.wait_ge(v_steps, 400)
                nc.scalar.activation(elu_a[:], agg[:], ACT.Exp).then_inc(s_elu, 1)
                copy_ax(J + 2)

                def gates(j):
                    act.wait_ge(s_gn, j + 1)
                    nc.scalar.activation(gate[:, j, :], wide[j % 2][:], ACT.Sigmoid,
                                         bias=small[:, 12 + j:13 + j]).then_inc(s_gexp, 1)

                gates(0)
                act.wait_ge(s_fc, 1)
                nc.scalar.activation(th[:], banks[1][:], ACT.Tanh, bias=fcb[:]).then_inc(s_tanh, 1)
                for j in range(1, J):
                    gates(j)
                for j in range(J):
                    act.wait_ge(s_lowered, j + 1)
                    nc.scalar.activation(cells[:, j], cells[:, j], ACT.Exp).then_inc(s_cexp, 1)
                    if j == 0:
                        copy_ax(J + 3)
                for j in range(J):
                    nc.scalar.copy(hT_parts[:, 0, j, :], hT[:, j, :]).then_inc(h_rounded, 1)
                for j in range(J):
                    act.wait_ge(s_ct, j + 1)
                    nc.scalar.copy(coefT[:, j, :], wide[j % 2][:]).then_inc(s_ct_copied, 1)

            @block.vector
            def _(vec):
                count = [0]

                def step(instruction, to=None):
                    n = 1 if to is None else to - count[0]
                    instruction.then_inc(v_steps, n)
                    count[0] += n
                    vec.wait_ge(v_steps, count[0])

                vec.wait_ge(loaded, 16 * 7)
                vec.wait_ge(zeroed, 2)
                for m, k in ((a_node2, 0), (a_gn2, 1)):
                    for half in range(2):
                        rows = slice(half * C, (half + 1) * C)
                        last = nc.vector.tensor_copy(m[rows, rows], a_rows[rows, k:k + 1].to_broadcast([C, C]))
                step(last, 3)
                step(nc.vector.tensor_scalar(member[:], incid[:, :, 0, :], 0.0, None, ALU.is_gt))
                step(nc.vector.tensor_scalar(outside[:], member[:], -NEG, NEG, ALU.mult, ALU.add))
                vec.wait_ge(s_h, 1)
                step(nc.vector.tensor_scalar(memberT[:], wide[0][:], 0.0, None, ALU.is_gt))
                step(nc.vector.tensor_scalar(outsideT[:], memberT[:], -NEG, NEG, ALU.mult, ALU.add), 10)
                def logits(j):
                    lj = lk[:, j % 2, :]
                    vec.wait_ge(s_copied, j + 1)
                    if j >= 2:
                        vec.wait_ge(s_turned, j - 1)
                    nc.vector.scalar_tensor_tensor(out=lj, in0=sc[:], scalar=0.2, in1=sc[:], op0=ALU.mult,
                                                   op1=ALU.max).then_inc(s_leaked, 1)
                    vec.wait_ge(s_leaked, j + 1)
                    step(nc.vector.tensor_tensor(lj, lj, memberT[:], ALU.mult))
                    nc.vector.tensor_tensor_reduce(lj, lj, outsideT[:], -1.0, 3.0e38, ALU.add, ALU.min,
                                                   small[:, j:j + 1]).then_inc(s_ht, 1)

                logits(0)
                for j in range(J):
                    if j + 1 < J:
                        logits(j + 1)
                    vec.wait_ge(s_exped, j + 1)
                    step(nc.vector.reciprocal(small[:, 8 + j:9 + j], small[:, 4 + j:5 + j]))
                    vec.wait_ge(s_agg, j + 1)
                    for half in range(2):
                        rows = slice(half * C, (half + 1) * C)
                        last = nc.vector.tensor_scalar(agg[rows, j, :], banks[j % 2][rows, rows], small[rows, 8 + j:9 + j],
                                                       None, ALU.mult)
                    step(last)
                    step(nc.vector.tensor_tensor_reduce(elu_a[:, j, :], agg[:, j, :], a_ge[:], 1.0, 0.0, ALU.mult,
                                                        ALU.add, small[:, 12 + j:13 + j]), 100 * (j + 1))
                vec.wait_ge(s_elu, 1)
                step(nc.vector.tensor_scalar(elu_a[:], elu_a[:], 1.0, -1.0, ALU.min, ALU.add))
                step(nc.vector.tensor_tensor(elu_a[:], elu_a[:], agg[:], ALU.max), 500)
                vec.wait_ge(s_he, 1)
                nc.vector.tensor_copy(heT[:], banks[0][0:C, :]).then_inc(s_he_c, 1)
                vec.wait_ge(s_se, 1)
                step(nc.vector.tensor_copy(se[:].rearrange("p b e -> p (b e)"), banks[0][:]), 600)
                def lower(j):
                    cj = cells[:, j].rearrange("p t h e -> p (t h) e")
                    rows = slice(2 * NT * j, 2 * NT * (j + 1))
                    vec.wait_ge(s_masked, j + 1)
                    step(nc.vector.tensor_tensor(cells[:, j], cells[:, j], outside[:].unsqueeze(2).to_broadcast([P, NT, 2, E]),
                                                 ALU.add))
                    step(nc.vector.tensor_reduce(cmax[:, rows], cj, AX.X, ALU.max))
                    nc.vector.tensor_tensor(cj, cj, cmax[:, rows].unsqueeze(2).to_broadcast([P, 2 * NT, E]),
                                            ALU.subtract).then_inc(s_lowered, 1)

                lower(0)
                for j in range(J):
                    if j + 1 < J:
                        lower(j + 1)
                    cj = cells[:, j].rearrange("p t h e -> p (t h) e")
                    rows = slice(2 * NT * j, 2 * NT * (j + 1))
                    vec.wait_ge(s_cexp, j + 1)
                    step(nc.vector.tensor_reduce(crcp[:, rows], cj, AX.X, ALU.add))
                    nc.vector.reciprocal(crcp[:, rows], crcp[:, rows]).then_inc(s_inverted, 1)
                for n, (j, cols) in enumerate(units):
                    tiles = slice(cols.start // P, cols.stop // P)
                    vec.wait_ge(ind_made, n + 1)
                    nc.vector.tensor_tensor(ind[:, j, tiles].rearrange("p t h f -> p t (h f)"),
                                            wide[2][:, cols].rearrange("p (t k) -> p t k", k=P),
                                            rdeg[:, tiles].unsqueeze(2).to_broadcast([P, NT // 2, P]),
                                            ALU.mult).then_inc(ind_taken, 1)
                for j in range(J):
                    vec.wait_ge(h_rounded, j + 1)
                    nc.vector.tensor_tensor(hT_parts[:, 1, j, :], hT[:, j, :], hT_parts[:, 0, j, :],
                                            ALU.subtract).then_inc(h_parted, 1)

            @block.tensor
            def _(pe):
                def ax(n):
                    j, cols = units[n]
                    if n >= 2:
                        pe.wait_ge(ax_copied, n - 1)
                    for mt in range(NT):
                        last = nc.tensor.matmul(wide[2][:, cols], Xj[:, j, mt, :], AT[:, mt, cols],
                                                start=(mt == 0), stop=(mt == NT - 1))
                    last.then_inc(ax_made, 1)

                ax(0)
                pe.wait_ge(loaded, 16 * 7)
                for t in range(NT):
                    last = nc.tensor.transpose(wide[0][:, t * P:(t + 1) * P], incid[:, t, :, :].rearrange("p h e -> p (h e)"),
                                               ident[:])
                last.then_inc(s_h, 1)
                pe.wait_ge(v_steps, 10)
                def score(j):
                    if j:
                        pe.wait_ge(s_copied, j)
                    for half in range(2):
                        cols = slice(half * HALF, (half + 1) * HALF)
                        last = nc.tensor.matmul(wide[0][:, cols], a_node2[:], hT[:, j, cols], start=True, stop=True)
                    last.then_inc(s_made, 1)

                def gate_sum(j):
                    if j >= 2:
                        pe.wait_ge(s_gexp, j - 1)
                    for half in range(2):
                        cols = slice(half * HALF, (half + 1) * HALF)
                        last = nc.tensor.matmul(wide[j % 2][:, cols], a_gn2[:], hT[:, j, cols], start=True, stop=True)
                    last.then_inc(s_gn, 1)

                score(0)
                ax(1)
                for j in range(J):
                    if j + 1 < J:
                        score(j + 1)
                    pe.wait_ge(s_exped, j + 1)
                    if j:
                        pe.wait_ge(s_turn_copied, j)
                    for t in range(NT):
                        last = nc.tensor.transpose(wide[1][:, t * P:(t + 1) * P], lk[:, j % 2, t * P:(t + 1) * P], ident[:])
                    last.then_inc(s_turned, 1)
                    ax(j + 2)
                    pe.wait_ge(s_turn_copied, j + 1)
                    if j >= 2:
                        pe.wait_ge(v_steps, 100 * (j - 1))
                    for t in range(NT):
                        last = nc.tensor.matmul(banks[j % 2][:, 0:P], alphaT[:, t, :], hN[:, j, t, :], start=(t == 0),
                                                stop=(t == NT - 1))
                    last.then_inc(s_agg, 1)
                ax(J + 2)
                pe.wait_ge(s_copied, J)
                pe.wait_ge(v_steps, 500)
                for j in range(J):
                    last = nc.tensor.transpose(banks[0][0:C, j * P:(j + 1) * P], elu_a[:, j, :], ident[:])
                last.then_inc(s_he, 1)
                gate_sum(0)
                pe.wait_ge(s_he_c, 1)
                nc.tensor.matmul(banks[1][:], fcw[0:C, :], heT[:], start=True, stop=True).then_inc(s_fc, 1)
                gate_sum(1)
                pe.wait_ge(s_tanh, 1)
                nc.tensor.matmul(banks[0][:], av[:].to_broadcast([P, P]), th[:], start=True, stop=True).then_inc(s_se, 1)
                gate_sum(2)
                gate_sum(3)
                ax(J + 3)
                pe.wait_ge(ax_copied, 2 * J)
                for n, (j, cols) in enumerate(units):
                    if n >= 2:
                        pe.wait_ge(ind_taken, n - 1)
                    for t in range(cols.start // P, cols.stop // P):
                        tile = slice(t * P, (t + 1) * P)
                        last = nc.tensor.matmul(wide[2][:, tile], AxT[:, j, tile], wi2[:], start=True, stop=True)
                    last.then_inc(ind_made, 1)
                pe.wait_ge(s_gexp, J)
                for j in range(J):
                    pe.wait_ge(s_divided, j + 1)
                    if j >= 2:
                        pe.wait_ge(s_ct_copied, j - 1)
                    for t in range(NT):
                        last = nc.tensor.transpose(wide[j % 2][:, t * P:(t + 1) * P],
                                                   cells[:, j, t].rearrange("p h e -> p (h e)"), ident[:])
                    last.then_inc(s_ct, 1)
        late_scope.close()

        GF = 8
        GROUPS = J * C // GF
        PER = C // GF
        BODY = 2 * GF
        LAST_LAG = 5
        gT = sb("gT_acc", [P, J, N], F32, l2_scope)
        with ExitStack() as scope:
            agg1 = sb("agg1", [P, J, E], F32, scope)
            ident_r = sb("ident_r", [P, 2, C], F32R, scope)
            window = sb("window", [P, 2 * P], F32, scope)
            pick = sb("pick", [P, 2, GF, 2, E], F32R, scope)
            place = sb("place", [P, 2, P + GF], F32, scope)
            a_now = sb("a_now", [P, 2, GF], F32, scope)
            a1_now = sb("a1_now", [P, 2, GF], F32, scope)
            u_buf = sb("u_buf", [P, 2, N], F32, scope)
            ex = sb("ex", [P, 2, N], F32, scope)
            lin = sb("lin", [P, 2, N], F32, scope)
            el = sb("el", [P, 4, N], F32, scope)
            spread = [ps(f"spread{k}", [P, N], scope) for k in range(2)]
            summed = [ps(f"summed{k}", [P, N], scope) for k in range(2)]
            gT_cleared = sem("l2c_gT_cleared")
            cleared, made, ready, staged, picked = (sem(f"l2c_{n}") for n in ("cleared", "made", "ready", "staged", "picked"))
            s_spread, s_u, s_ex, s_lin, s_el, s_weighted, s_summed, s_added = (
                sem(f"l2c_{n}") for n in ("spread", "u", "ex", "lin", "elu", "weighted", "summed", "added"))
            block = scope.enter_context(nc.Block())

            def at_lag(i, k, lag):
                group = BODY // GF * i + (k - lag) // GF
                return BODY * i + k - lag, (k - lag) % BODY, group, group // PER

            def stage_group(pool, group, par):
                nc.gpsimd.tensor_copy(place[:, par, :], window[:, bass.ds(P - GF - group % PER * GF, P + GF)])
                cols = bass.ds(group * GF, GF)
                nc.gpsimd.tensor_copy(a_now[:, par, :], agg[:].rearrange("p j f -> p (j f)")[:, cols])
                nc.gpsimd.tensor_copy(a1_now[:, par, :], agg1[:].rearrange("p j f -> p (j f)")[:, cols]).then_inc(staged, 1)

            def pick_group(vec, group, par):
                cols = ident_r[:, :, bass.ds(group % PER * GF, GF)].rearrange("p h f -> p f h")
                nc.vector.tensor_copy(pick[:, par], cols.unsqueeze(3).to_broadcast([P, GF, 2, E])).then_inc(picked, 1)

            def add_group(vec, group, par):
                acc = gT[:, bass.ds(group // PER, 1), :]
                nc.vector.tensor_tensor(acc, acc, summed[par][:].unsqueeze(1), ALU.add).then_inc(s_added, 1)

            def pe_step(pe, i, k, peeled=False, spreads=True):
                if spreads:
                    q, kk, group, couple = at_lag(i, k, 0)
                    par, f = kk // GF, kk % GF
                    if f == 0:
                        pe.wait_ge(picked, group + 1)
                    if not peeled or q >= 2:
                        pe.wait_ge(s_u, q - 1)
                    stay = pick[:, par, f].rearrange("p h e -> p (h e)")
                    for half in range(2):
                        cols = slice(half * HALF, (half + 1) * HALF)
                        o = spread[k % 2][:, cols].unsqueeze(1)
                        nc.tensor.matmul(o, stay, hT_parts[:, 0, bass.ds(couple, 1), cols], start=True, stop=False)
                        last = nc.tensor.matmul(o, stay, hT_parts[:, 1, bass.ds(couple, 1), cols], start=False, stop=True)
                    last.then_inc(s_spread, 1)
                q, kk, group, couple = at_lag(i, k, 5)
                if not peeled or q >= 0:
                    par, f = kk // GF, kk % GF
                    pe.wait_ge(s_weighted, q + 1)
                    if f == 0:
                        pe.wait_ge(staged, group + 1)
                        if not peeled or group >= 2:
                            pe.wait_ge(s_added, group - 1)
                    for half in range(2):
                        cols = slice(half * HALF, (half + 1) * HALF)
                        last = nc.tensor.matmul(summed[par][:, cols], place[:, par, GF - 1 - f:GF - 1 - f + P],
                                                el[:, kk % 4, cols], start=(f == 0), stop=(f == GF - 1))
                    last.then_inc(s_summed, 1)

            def vec_step(vec, i, k, peeled=False, until=LAST_LAG):
                q, kk, group, couple = at_lag(i, k, 1)
                if (not peeled or q >= 0) and until > 0:
                    par, f = kk // GF, kk % GF
                    if f == 0:
                        vec.wait_ge(staged, group + 1)
                    vec.wait_ge(s_spread, q + 1)
                    if not peeled or q >= 2:
                        vec.wait_ge(s_lin, q - 1)
                    nc.vector.scalar_tensor_tensor(out=u_buf[:, kk % 2, :].unsqueeze(1), in0=spread[kk % 2][:].unsqueeze(1),
                                                   scalar=a_now[:, par, f:f + 1], in1=gate[:, bass.ds(couple, 1), :],
                                                   op0=ALU.subtract, op1=ALU.mult).then_inc(s_u, 1)
                q, kk, group, couple = at_lag(i, k, 3)
                if not peeled or q >= 0:
                    vec.wait_ge(s_lin, q + 1)
                    if not peeled or q >= 4:
                        vec.wait_ge(s_summed, q - 3)
                    nc.vector.scalar_tensor_tensor(out=el[:, kk % 4, :], in0=ex[:, kk % 2, :], scalar=1.0,
                                                   in1=lin[:, kk % 2, :], op0=ALU.min, op1=ALU.max).then_inc(s_el, 1)
                if until < LAST_LAG:
                    return
                q, kk, group, couple = at_lag(i, k, 0)
                if kk % GF == 3:
                    vec.wait_ge(s_spread, GF * group + 1)
                    pick_group(vec, (group + 1) % GROUPS, 1 - kk // GF)
                if kk % GF == 7 and (not peeled or group >= 1):
                    vec.wait_ge(s_summed, GF * group)
                    if peeled:
                        vec.wait_ge(gT_cleared, 1)
                    add_group(vec, group - 1, 1 - kk // GF)

            def act_step(act, i, k, peeled=False):
                q, kk, group, couple = at_lag(i, k, 2)
                if not peeled or q >= 0:
                    bias = slice(kk % GF, kk % GF + 1)
                    act.wait_ge(s_u, q + 1)
                    if not peeled or q >= 2:
                        act.wait_ge(s_el, q - 1)
                    nc.scalar.activation(ex[:, kk % 2, :], u_buf[:, kk % 2, :], ACT.Exp,
                                         bias=a_now[:, kk // GF, bias]).then_inc(s_ex, 1)
                    nc.scalar.activation(lin[:, kk % 2, :], u_buf[:, kk % 2, :], ACT.Identity,
                                         bias=a1_now[:, kk // GF, bias]).then_inc(s_lin, 1)

            def pool_step(pool, i, k, peeled=False, stages=True):
                q, kk, group, couple = at_lag(i, k, 4)
                if not peeled or q >= 0:
                    pool.wait_ge(s_el, q + 1)
                    pool.nop(nofuse=True)
                    nc.gpsimd.tensor_tensor(el[:, kk % 4, :].unsqueeze(1), el[:, kk % 4, :].unsqueeze(1),
                                            coefT[:, bass.ds(couple, 1), :], ALU.mult).then_inc(s_weighted, 1)
                q, kk, group, couple = at_lag(i, k, 0)
                if stages and kk % GF == 6:
                    if not peeled or group >= 1:
                        pool.wait_ge(s_summed, GF * group)
                    stage_group(pool, (group + 1) % GROUPS, 1 - kk // GF)

            def bodies(engine, step):
                for k in range(BODY):
                    step(engine, 0, k, peeled=True)
                with engine.Fori(1, GROUPS * GF // BODY) as i:
                    for k in range(BODY):
                        step(engine, i, k)

            END = GROUPS * GF // BODY

            @block.gpsimd
            def _(pool):
                nc.gpsimd.memset(window[:], 0.0).then_inc(cleared, 1)
                pool.wait_ge(cleared, 1)
                nc.gpsimd.memset(window[0:C, P - 1:P], 1.0)
                nc.gpsimd.memset(window[C:P, P + C - 1:P + C], 1.0).then_inc(made, 1)
                pool.wait_ge(ready, 2)
                pool.wait_ge(made, 1)
                stage_group(pool, 0, 0)
                nc.gpsimd.memset(gT[:], 0.0).then_inc(gT_cleared, 1)
                bodies(pool, pool_step)
                for k in range(4):
                    pool_step(pool, END, k, stages=False)

            @block.scalar
            def _(act):
                act.wait_ge(staged, 1)
                bodies(act, act_step)
                for k in range(2):
                    act_step(act, END, k)

            @block.vector
            def _(vec):
                nc.vector.tensor_scalar(agg1[:], agg[:], 1.0, None, ALU.add).then_inc(ready, 1)
                nc.vector.tensor_copy(ident_r[:].rearrange("p h f -> p (h f)"), ident[:]).then_inc(ready, 1)
                vec.wait_ge(ready, 2)
                pick_group(vec, 0, 0)
                bodies(vec, vec_step)
                for k in range(3):
                    vec_step(vec, END, k, until=1 - k)
                vec.wait_ge(s_summed, GROUPS * GF)
                add_group(vec, GROUPS - 1, 1)

            @block.tensor
            def _(pe):
                bodies(pe, pe_step)
                for k in range(5):
                    pe_step(pe, END, k, spreads=False)

        AT3 = node_edge[:].rearrange("p a j n -> p (a j) n")
        at3_banked, at3_copied = sem("at3_banked"), sem("at3_copied")
        with ExitStack() as scope:
            indT = sb("indT", [P, J, N], F32, scope)
            gN = sb("gN", [P, J, NT, 2, C], F32, scope)
            th = [sb(f"th{k}", [P, HALF], F32, scope) for k in range(2)]
            score = sb("score", [P, 2, TOK], F32, scope)
            av_window = sb("av_window", [P, 8 * B], F32, scope)
            score_rows = sb("score_rows", [4 * B, HALF], F32, scope)
            smax = sb("smax", [P, TOK], F32, scope)
            R = sb("R2", [P, TOK, C], F32, scope)
            gN_rows = gN[:].rearrange("p j t h c -> p (j t h) c")
            norm = residual_norm(2, R[:], gN_rows, scope)
            AxT = indT
            w_nl = sb("w_nl", [P, 2], F32, scope)
            b_nl = sb("b_nl", [C, 1], F32, scope)
            w_out = sb("w_out", [C, 2, C], F32, scope)
            w_outT = sb("w_outT", [P, C], F32, scope)
            mix = sb("mix", [P, P], F32, scope)
            b_out = sb("b_out3", [P, C], F32, scope)
            v = sb("v", [P, 1], F32, scope)
            const = sb("const", [P, C], F32, scope)
            norm3 = residual_norm(3, R[:], gN_rows, scope)
            stored = sem("stored")
            loaded, cleared, prep, prep_t = sem("l3_loaded"), sem("l3_cleared"), sem("l3_prep"), sem("l3_prep_t")
            ax_banked, ax_copied = sem("l3_ax_banked"), sem("l3_ax_copied")
            out_banked, out_taken = sem("l3_out_banked"), sem("l3_out_taken")
            wide = [ps(f"l2d_wide{k}", [P, N], scope) for k in range(2)]
            out_ps = ps("l2d_fc", [P, N], scope)
            fc = [out_ps[:, k * HALF:(k + 1) * HALF] for k in range(2)]
            score_ps = ps("l2d_score", [4 * B, HALF], scope)
            score_turned = ps("l2d_score_turned", [P, 4, 4 * B], scope)
            prep_ps = score_turned[:].rearrange("p a b -> p (a b)")[:, 0:C]
            shifted, turned, copied, fc_made, tanhed, scored, exped, steps = (
                sem(f"l2d_{n}") for n in ("shifted", "turned", "copied", "fc_made", "tanhed", "scored", "exped", "steps"))
            windowed, rows_taken, rows_turned = sem("l2d_windowed"), sem("l2d_rows_taken"), sem("l2d_rows_turned")
            g_weighed = sem("l2d_g_weighed")
            block = scope.enter_context(nc.Block())
            slabs = [(kind, j, half, h) for kind in range(2) for j in range(J) for half in range(2) for h in range(2)]
            SLABS = len(slabs)

            @block.sync
            def _(sp):
                for half in range(2):
                    sp.dma_start(w_nl[half * C:(half + 1) * C, :], L3_w_nl).then_inc(loaded, 16)
                    sp.dma_start(w_out[:, half, :], L3_w_out).then_inc(loaded, 16)
                sp.dma_start(b_nl[:], L3_b_nl.unsqueeze(1)).then_inc(loaded, 16)
                sp.dma_start(b_out[:], L3_b_out.unsqueeze(0).to_broadcast([P, C])).then_inc(loaded, 16)
                sp.wait_ge(loaded, 16 * 6)
                for b in range(B):
                    sp.wait_ge(norm3.done, norm3.BASE + b // 2 + 1)
                    sp.dma_start(out[b].rearrange("(t p) c -> p t c", p=P), X[:, b // 2, :, b % 2, :]).then_inc(stored, 16)
                sp.wait_ge(stored, 16 * B)

            @block.gpsimd
            def _(pool):
                nc.gpsimd.memset(av_window[:], 0.0).then_inc(windowed, 1)
                nc.gpsimd.memset(mix[:], 0.0).then_inc(cleared, 1)
                gf = gN[:].rearrange("p j t h c -> p (j t h) c")
                pool.wait_ge(steps, 8)
                for c in range(J + 1):
                    if c < J:
                        r = norm.rows(c)
                        w = score[:, 1, r].unsqueeze(2).to_broadcast([P, 2 * NT, C])
                        nc.gpsimd.tensor_tensor(gf[:, r], gf[:, r], w, ALU.mult).then_inc(g_weighed, 1)
                    if c >= 1:
                        norm.pool_part(pool, c - 1)
                for c in range(J):
                    norm3.pool_part(pool, c)

            @block.scalar
            def _(act):
                copy_adj(act, nc.scalar.copy, AT3, fc, at3_banked, at3_copied)
                for n in range(len(slabs)):
                    act.wait_ge(fc_made, n + 1)
                    if n >= 2:
                        act.wait_ge(scored, n - 1)
                    nc.scalar.activation(th[n % 2][:], fc[n % 2], ACT.Tanh, bias=fcb[:]).then_inc(tanhed, 1)
                act.wait_ge(steps, 4)
                nc.scalar.activation(score[:], score[:], ACT.Exp).then_inc(exped, 1)
                norm.act_part(act)
                for j in range(J + 2):
                    if j < J:
                        act.wait_ge(ax_banked, j + 1)
                        nc.scalar.copy(AxT[:, j, :], wide[j % 2][:]).then_inc(ax_copied, 1)
                    if j:
                        norm3.act_step(act, j - 1)

            @block.vector
            def _(vec):
                nc.vector.tensor_scalar(gT[:], gT[:], -1.0, None, ALU.add).then_inc(shifted, 1)
                vec.wait_ge(windowed, 1)
                nc.vector.tensor_copy(av_window[:, SLABS - 1:SLABS], av[:]).then_inc(windowed, 1)
                for n in range(2 * J):
                    j = n // 2
                    vec.wait_ge(turned, n + 1)
                    if n % 2 == 0:
                        nc.vector.tensor_copy(indT[:, j, :], wide[0][:]).then_inc(copied, 1)
                    else:
                        nc.vector.tensor_copy(gN[:, j].rearrange("p t h f -> p (t h f)"), wide[1][:]).then_inc(copied, 1)
                vec.wait_ge(loaded, 16 * 6)
                vec.wait_ge(cleared, 1)
                nc.vector.tensor_scalar(v[:], w_nl[:, 0:1], w_nl[:, 1:2], 1.0 / 2.0 ** 0.5, ALU.add,
                                        ALU.mult).then_inc(prep, 1)
                vec.wait_ge(prep_t, 1)
                nc.vector.tensor_copy(w_outT[:], prep_ps).then_inc(prep, 1)
                vec.wait_ge(prep, 2)
                for half in range(2):
                    rows = slice(half * C, (half + 1) * C)
                    last = nc.vector.tensor_scalar(mix[rows, rows], w_outT[rows, :], v[rows, :], None, ALU.mult)
                last.then_inc(prep, 1)
                vec.wait_ge(prep_t, 2)
                nc.vector.tensor_tensor(const[:], prep_ps, b_out[:], ALU.add).then_inc(prep, 1)
                vec.wait_ge(prep, 4)
                vec.wait_ge(scored, len(slabs))
                nc.vector.tensor_copy(score_rows[:], score_ps[:]).then_inc(rows_taken, 1)
                vec.wait_ge(rows_turned, 1)
                count = [0]

                def step(instruction):
                    instruction.then_inc(steps, 1)
                    count[0] += 1
                    vec.wait_ge(steps, count[0])

                for q in range(4):
                    for kind in range(2):
                        last = nc.vector.tensor_copy(
                            score[:, kind].rearrange("p (a q h) -> p a q h", q=4, h=2)[:, :, q, :],
                            score_turned[:, q, kind * SLABS // 2:(kind + 1) * SLABS // 2].rearrange("p (a h) -> p a h", h=2))
                step(last)
                step(nc.vector.tensor_tensor(smax[:], score[:, 0], score[:, 1], ALU.max))
                step(nc.vector.tensor_tensor(score[:, 0], score[:, 0], smax[:], ALU.subtract))
                step(nc.vector.tensor_tensor(score[:, 1], score[:, 1], smax[:], ALU.subtract))
                vec.wait_ge(exped, 1)
                step(nc.vector.tensor_tensor(smax[:], score[:, 0], score[:, 1], ALU.add))
                step(nc.vector.reciprocal(smax[:], smax[:]))
                step(nc.vector.tensor_tensor(score[:, 0], score[:, 0], smax[:], ALU.mult))
                step(nc.vector.tensor_tensor(score[:, 1], score[:, 1], smax[:], ALU.mult))
                indf, gf = (m[:].rearrange("p j t h c -> p (j t h) c") for m in (ind, gN))

                def weigh(c):
                    r = norm.rows(c)
                    w = score[:, 0, r].unsqueeze(2).to_broadcast([P, 2 * NT, C])
                    step(nc.vector.tensor_tensor(R[:, r], indf[:, r], w, ALU.mult))
                    vec.wait_ge(g_weighed, c + 1)
                    step(nc.vector.tensor_tensor(R[:, r], R[:, r], gf[:, r], ALU.add))

                norm.vec_part(vec, weigh)

                def take(j):
                    vec.wait_ge(out_banked, j + 1)
                    nc.vector.tensor_tensor(R[:, norm3.rows(j), :], out_ps[:].rearrange("p (r c) -> p r c", c=C),
                                            const[:].unsqueeze(1).to_broadcast([P, 2 * NT, C]), ALU.add).then_inc(out_taken, 1)
                    vec.wait_ge(out_taken, j + 1)

                norm3.vec_part(vec, take)

            @block.tensor
            def _(pe):
                indj = ind[:].rearrange("p j t h f -> p j t (h f)")
                for j in range(J):
                    if j:
                        pe.wait_ge(copied, 2 * j)
                    for t in range(NT):
                        last = nc.tensor.transpose(wide[0][:, t * P:(t + 1) * P], indj[:, j, t, :], ident[:])
                    last.then_inc(turned, 1)
                    if j == 0:
                        pe.wait_ge(shifted, 1)
                    for t in range(NT):
                        last = nc.tensor.transpose(wide[1][:, t * P:(t + 1) * P], gT[:, j, t * P:(t + 1) * P], ident[:])
                    last.then_inc(turned, 1)
                    transpose_adj(pe, AT3, fc, at3_banked, at3_copied, range(4 * j, 4 * j + 4))
                pe.wait_ge(copied, 2 * J)
                pe.wait_ge(at3_copied, 2 * NT)

                pe.wait_ge(loaded, 16 * 6)
                nc.tensor.transpose(prep_ps, w_out[:].rearrange("o h f -> o (h f)"), ident[0:C, 0:C]).then_inc(prep_t, 1)
                pe.wait_ge(prep, 2)
                nc.tensor.matmul(prep_ps, b_nl[:].to_broadcast([C, P]), w_outT[0:C, :], start=True,
                                 stop=True).then_inc(prep_t, 1)
                pe.wait_ge(prep, 4)

                def scores_of(n):
                    pe.wait_ge(tanhed, n + 1)
                    nc.tensor.matmul(score_ps[:], av_window[:, SLABS - 1 - n:2 * SLABS - 1 - n], th[n % 2][:],
                                     start=(n == 0), stop=(n == SLABS - 1)).then_inc(scored, 1)

                pe.wait_ge(windowed, 2)
                for n, (kind, j, half, h) in enumerate(slabs):
                    if n >= 2:
                        pe.wait_ge(tanhed, n - 1)
                    rows, cols = slice(h * C, (h + 1) * C), slice(half * HALF, (half + 1) * HALF)
                    nc.tensor.matmul(fc[n % 2], fcw[rows, :], (gT if kind else indT)[rows, j, cols], start=True,
                                     stop=True).then_inc(fc_made, 1)
                    if n:
                        scores_of(n - 1)
                scores_of(SLABS - 1)
                pe.wait_ge(rows_taken, 1)
                for q in range(4):
                    last = nc.tensor.transpose(score_turned[:, q, :], score_rows[:, q * P:(q + 1) * P],
                                               ident[0:SLABS, 0:SLABS])
                last.then_inc(rows_turned, 1)

                def out_of(j):
                    pe.wait_ge(ax_copied, j + 1)
                    if j:
                        pe.wait_ge(out_taken, j)
                    for t in range(NT):
                        cols = slice(t * P, (t + 1) * P)
                        last = nc.tensor.matmul(out_ps[:, cols], AxT[:, j, cols], mix[:], start=True, stop=True)
                    last.then_inc(out_banked, 1)

                for j in range(J):
                    if j >= 2:
                        pe.wait_ge(ax_copied, j - 1)
                    pe.wait_ge(norm.done, norm.BASE + j + 1)
                    for half in range(2):
                        cols = slice(half * HALF, (half + 1) * HALF)
                        for mt in range(NT):
                            last = nc.tensor.matmul(wide[j % 2][:, cols], Xj[:, j, mt, :], AT3[:, mt, cols],
                                                    start=(mt == 0), stop=(mt == NT - 1))
                    last.then_inc(ax_banked, 1)
                    if j:
                        out_of(j - 1)
                out_of(J - 1)

_INS = ["x", "adj", "L0_gnn_embedding", "L0_gnn_weight", "L0_gnn_bias", "L1_gnn_Wh", "L1_gnn_bh", "L1_gnn_W_out",
        "L1_gnn_b_out", "L2_gnn_H", "L2_gnn_W", "L2_gnn_W_ind", "L2_gnn_a_node", "L2_gnn_a_gn", "L2_gnn_a_ge",
        "L2_gnn_fcW", "L2_gnn_fcb", "L2_gnn_av", "L3_gnn_w_nl", "L3_gnn_b_nl", "L3_gnn_w_out", "L3_gnn_b_out"]


def kernel(**inputs):
    import numpy as _np
    import concourse.bacc as _bacc
    from concourse.bass_utils import run_bass_kernel_spmd as _run

    nc = _bacc.Bacc("TRN2", target_bir_lowering=False, num_devices=1)
    arrays, args = {}, []
    for name in _INS:
        a = _np.ascontiguousarray(inputs[name])
        arrays[f"in_{name}_dram"] = a
        args.append(nc.dram_tensor(f"in_{name}_dram", a.shape, mybir.dt.from_np(a.dtype), kind="ExternalInput").ap())
    args.append(nc.dram_tensor("out_dram", inputs["x"].shape, F32, kind="ExternalOutput").ap())
    adjacency_stack_kernel(nc, *args)
    return _run(nc, [arrays], core_ids=[0]).results[0]["out_dram"]
```
